# Optimizing a Trainium2 kernel written in Bass

```python
import numpy as np
import jax
import jax.numpy as jnp

def _softmax(x, axis=-1):
    return jax.nn.softmax(x, axis=axis)

def _gelu(x):
    return jax.nn.gelu(x, approximate=True)

def _silu(x):
    return jax.nn.silu(x)

def _sigmoid(x):
    return jax.nn.sigmoid(x)

def _layernorm(x, axis=-1, eps=1e-05):
    m = jnp.mean(x, axis=axis, keepdims=True)
    v = jnp.var(x, axis=axis, keepdims=True)
    return (x - m) / jnp.sqrt(v + eps)

def _scatter_add(tgt, idx, src, axis=0):
    return tgt.at[idx].add(src)

def _segment_sum(src, seg, n):
    return jax.ops.segment_sum(src, seg, n)
kernel_name = 'mk_flamingo_gated_d1_seqx_r8_ee8ec2'

def setup_inputs(seed: int=0):
    np.random.seed(seed)
    _w = jnp.asarray

    def _rec_inputs():
        import jax
        import jax.numpy as jnp
        _rk = jax.random.key(seed)
        x = -0.0002928 + 1 * jax.random.normal(jax.random.fold_in(_rk, 1), (32, 128, 128), jnp.float32)
        _lenS = 128 - jax.random.randint(jax.random.fold_in(_rk, 7), (32,), 0, max(1, 128 // 4) + 1, jnp.int32)
        _lenS2 = 128 - jax.random.randint(jax.random.fold_in(_rk, 8), (32,), 0, max(1, 128 // 4) + 1, jnp.int32)
        _ctx_1024P = jax.random.normal(jax.random.fold_in(_rk, 11), (32, 16, 128), jnp.float32)
        _ctx_1024c = jax.random.dirichlet(jax.random.fold_in(_rk, 511), 0.3 * jnp.ones((16,), jnp.float32), (32, 128))
        _ctx_1024t = jnp.einsum('bsk,bkd->bsd', _ctx_1024c, _ctx_1024P)
        _ctx_1024t = _ctx_1024t * jax.lax.rsqrt(jnp.mean(jnp.square(_ctx_1024t)) + 1e-12) * 0.953939
        ctx_1024 = 1.43633e-05 + 1.0001 * (_ctx_1024t + 0.3 * jax.random.normal(jax.random.fold_in(_rk, 611), (32, 128, 128), jnp.float32))
        _g = jax.random.normal(jax.random.fold_in(_rk, 9001), (2, 1), jnp.float32)
        _g = jnp.sign(_g) * jnp.maximum(jnp.abs(_g), 1.0) + (_g == 0) * 1.0
        g_xattn = _g[0]
        g_ffn = _g[1]
        return (x, ctx_1024, g_xattn, g_ffn)
    x, ctx_1024, g_xattn, g_ffn = _rec_inputs()

    def _L0_xattn_setup():
        import jax, jax.numpy as jnp
        import numpy as np
        D, H = (128, 16)
        DH = D // H

        def _split_heads(z):
            b, t, _ = z.shape
            return z.reshape(b, t, H, DH).transpose(0, 2, 1, 3)
        key = jax.random.key(seed)
        ks = jax.random.split(key, 11)
        b, t, ta = (2, 256, 1500)
        s = 1.0 / np.sqrt(D)
        return {'x': jax.random.normal(ks[0], (b, t, D), dtype=jnp.float32), 'xa': jax.random.normal(ks[1], (b, ta, D), dtype=jnp.float32), 'Wqkv': jax.random.normal(ks[2], (D, 3 * D), dtype=jnp.float32) * s, 'bqkv': jax.random.normal(ks[3], (3 * D,), dtype=jnp.float32) * 0.01, 'Wqkv_aux': jax.random.normal(ks[4], (D, 3 * D), dtype=jnp.float32) * s, 'bqkv_aux': jax.random.normal(ks[5], (3 * D,), dtype=jnp.float32) * 0.01, 'Wo': jax.random.normal(ks[6], (D, D), dtype=jnp.float32) * s, 'bo': jax.random.normal(ks[7], (D,), dtype=jnp.float32) * 0.01, 'g': jnp.zeros((H,), dtype=jnp.float32)}
    _L0_xattn_all = _L0_xattn_setup()
    _L0_xattn_in = {k: v for k, v in _L0_xattn_all.items() if k in ('Wqkv', 'bqkv', 'Wqkv_aux', 'bqkv_aux', 'Wo', 'bo', 'g')}
    del _L0_xattn_all

    def _L0_ffn_setup():
        import jax, jax.numpy as jnp
        import numpy as np
        B, S, H = (2, 256, 128)
        E, F, K = (64, 64, 8)
        G, TG = (8, 4)
        SCALE = 2.5
        F_SH = 64

        def _gate(x, gate_w, gate_bias):
            scores = jax.nn.sigmoid(x @ gate_w.T)
            sc = scores + gate_bias[None, :]
            T = x.shape[0]
            group_scores = jax.lax.top_k(sc.reshape(T, G, E // G), 2)[0].sum(-1)
            _, gidx = jax.lax.top_k(group_scores, TG)
            gmask = jnp.zeros((T, G), sc.dtype).at[jnp.arange(T)[:, None], gidx].set(1.0)
            smask = jnp.repeat(gmask, E // G, axis=1)
            masked = jnp.where(smask > 0, sc, -jnp.inf)
            _, tidx = jax.lax.top_k(masked, K)
            tw = jnp.take_along_axis(scores, tidx, axis=1)
            tw = tw / (tw.sum(-1, keepdims=True) + 1e-20)
            return (tidx, tw * SCALE)
        key = jax.random.key(seed)
        ks = jax.random.split(key, 9)

        def w(k, shape, fan_in):
            return jax.random.normal(k, shape, jnp.float32) / np.float32(np.sqrt(fan_in))
        return {'hidden_states': jax.random.normal(ks[0], (B, S, H), jnp.float32), 'gate_w': w(ks[1], (E, H), H), 'gate_bias': jax.random.normal(ks[2], (E,), jnp.float32) * 0.01, 'We_gate': w(ks[3], (E, H, F), H), 'We_up': w(ks[4], (E, H, F), H), 'We_down': w(ks[5], (E, F, H), F), 'Ws_gate': w(ks[6], (H, F_SH), H), 'Ws_up': w(ks[7], (H, F_SH), H), 'Ws_down': w(ks[8], (F_SH, H), F_SH)}
    _L0_ffn_all = _L0_ffn_setup()
    _L0_ffn_in = {k: v for k, v in _L0_ffn_all.items() if k in ('gate_w', 'gate_bias', 'We_gate', 'We_up', 'We_down', 'Ws_gate', 'Ws_up', 'Ws_down')}
    del _L0_ffn_all
    return {'x': x, 'ctx_1024': ctx_1024, 'g_xattn': g_xattn, 'g_ffn': g_ffn, 'L0_xattn_Wqkv': _L0_xattn_in['Wqkv'], 'L0_xattn_bqkv': _L0_xattn_in['bqkv'], 'L0_xattn_Wqkv_aux': _L0_xattn_in['Wqkv_aux'], 'L0_xattn_bqkv_aux': _L0_xattn_in['bqkv_aux'], 'L0_xattn_Wo': _L0_xattn_in['Wo'], 'L0_xattn_bo': _L0_xattn_in['bo'], 'L0_xattn_g': _L0_xattn_in['g'], 'L0_ffn_gate_w': _L0_ffn_in['gate_w'], 'L0_ffn_gate_bias': _L0_ffn_in['gate_bias'], 'L0_ffn_We_gate': _L0_ffn_in['We_gate'], 'L0_ffn_We_up': _L0_ffn_in['We_up'], 'L0_ffn_We_down': _L0_ffn_in['We_down'], 'L0_ffn_Ws_gate': _L0_ffn_in['Ws_gate'], 'L0_ffn_Ws_up': _L0_ffn_in['Ws_up'], 'L0_ffn_Ws_down': _L0_ffn_in['Ws_down']}

def reference(x, ctx_1024, g_xattn, g_ffn, L0_xattn_Wqkv, L0_xattn_bqkv, L0_xattn_Wqkv_aux, L0_xattn_bqkv_aux, L0_xattn_Wo, L0_xattn_bo, L0_xattn_g, L0_ffn_gate_w, L0_ffn_gate_bias, L0_ffn_We_gate, L0_ffn_We_up, L0_ffn_We_down, L0_ffn_Ws_gate, L0_ffn_Ws_up, L0_ffn_Ws_down):
    import jax
    import jax.numpy as jnp

    def _L0_xattn_ref(x, xa, Wqkv, bqkv, Wqkv_aux, bqkv_aux, Wo, bo, g):
        import jax, jax.numpy as jnp
        import numpy as np
        D, H = (128, 16)
        DH = D // H

        def _split_heads(z):
            b, t, _ = z.shape
            return z.reshape(b, t, H, DH).transpose(0, 2, 1, 3)
        qkv = x @ Wqkv + bqkv
        qkv_a = xa @ Wqkv_aux + bqkv_aux
        q, k, v = (_split_heads(c) for c in jnp.split(qkv, 3, axis=-1))
        qa, ka, va = (_split_heads(c) for c in jnp.split(qkv_a, 3, axis=-1))
        scale = 1.0 / jnp.sqrt(jnp.float32(DH))
        dots = jnp.einsum('bhqd,bhkd->bhqk', q, k) * scale
        dots_aux = jnp.einsum('bhqd,bhkd->bhqk', q, ka) * scale
        p = jax.nn.softmax(dots, axis=-1)
        pa = jax.nn.softmax(dots_aux, axis=-1)
        h_main = jnp.einsum('bhqk,bhkd->bhqd', p, v)
        h_aux = jnp.einsum('bhqk,bhkd->bhqd', pa, va)
        gate = jax.nn.sigmoid(g).reshape(1, H, 1, 1)
        out = h_main * (1.0 - gate) + h_aux * gate
        b, _, t, _ = out.shape
        out = out.transpose(0, 2, 1, 3).reshape(b, t, H * DH)
        return out @ Wo + bo

    def _L0_ffn_ref(hidden_states, gate_w, gate_bias, We_gate, We_up, We_down, Ws_gate, Ws_up, Ws_down):
        import jax, jax.numpy as jnp
        import numpy as np
        B, S, H = (2, 256, 128)
        E, F, K = (64, 64, 8)
        G, TG = (8, 4)
        SCALE = 2.5
        F_SH = 64

        def _gate(x, gate_w, gate_bias):
            scores = jax.nn.sigmoid(x @ gate_w.T)
            sc = scores + gate_bias[None, :]
            T = x.shape[0]
            group_scores = jax.lax.top_k(sc.reshape(T, G, E // G), 2)[0].sum(-1)
            _, gidx = jax.lax.top_k(group_scores, TG)
            gmask = jnp.zeros((T, G), sc.dtype).at[jnp.arange(T)[:, None], gidx].set(1.0)
            smask = jnp.repeat(gmask, E // G, axis=1)
            masked = jnp.where(smask > 0, sc, -jnp.inf)
            _, tidx = jax.lax.top_k(masked, K)
            tw = jnp.take_along_axis(scores, tidx, axis=1)
            tw = tw / (tw.sum(-1, keepdims=True) + 1e-20)
            return (tidx, tw * SCALE)
        b, s, h = hidden_states.shape
        x = hidden_states.reshape(-1, h).astype(jnp.float32)
        tidx, tw = _gate(x, gate_w, gate_bias)
        T = x.shape[0]
        w_dense = jnp.zeros((T, E), tw.dtype).at[jnp.arange(T)[:, None], tidx].add(tw)

        def body(acc, ws):
            wg, wu, wdn, cw = ws
            hmid = jax.nn.silu(x @ wg) * (x @ wu)
            return (acc + cw[:, None] * (hmid @ wdn), None)
        y, _ = jax.lax.scan(body, jnp.zeros_like(x), (We_gate, We_up, We_down, w_dense.T))
        y = y.reshape(b, s, h)
        shared = jax.nn.silu(hidden_states @ Ws_gate) * (hidden_states @ Ws_up) @ Ws_down
        return y + shared
    x = x + jnp.tanh(g_xattn[0]) * _L0_xattn_ref(_layernorm(x, axis=-1), ctx_1024, L0_xattn_Wqkv, L0_xattn_bqkv, L0_xattn_Wqkv_aux, L0_xattn_bqkv_aux, L0_xattn_Wo, L0_xattn_bo, L0_xattn_g)
    x = x + jnp.tanh(g_ffn[0]) * _L0_ffn_ref(_layernorm(x, axis=-1), L0_ffn_gate_w, L0_ffn_gate_bias, L0_ffn_We_gate, L0_ffn_We_up, L0_ffn_We_down, L0_ffn_Ws_gate, L0_ffn_Ws_up, L0_ffn_Ws_down)
    return x

_drawn_inputs = setup_inputs


def setup_inputs(seed=0):
    import zlib

    import numpy as np

    out = dict(_drawn_inputs(seed))
    spreads = {'L0_xattn_g': (0.0, 0.1)}
    factors = {}
    for name, (base, spread) in spreads.items():
        noise = np.random.default_rng([zlib.crc32(name.encode()), seed]).standard_normal(out[name].shape)
        drawn = base * np.exp(spread * noise) if base else spread * noise
        out[name] = jnp.asarray(drawn.astype(out[name].dtype))
    for name, factor in factors.items():
        out[name] = (out[name] * factor).astype(out[name].dtype)
    return out
```

```python
from contextlib import ExitStack

import concourse.bass as bass
from concourse import mybir

F32 = mybir.dt.float32
F32R = mybir.dt.float32r
BF16 = mybir.dt.bfloat16
FP16 = mybir.dt.float16
ALU = mybir.AluOpType
ACT = mybir.ActivationFunctionType
AXX = mybir.AxisListType.X

P = 128
H, DH = 16, 8
PART = 3
Q_SLOTS = (0, 0, 0, 1, 1, 2)
K_SLOTS = (0, 1, 2, 0, 1, 0)
ROWS = len(Q_SLOTS) * DH
SHIFT = 96
ROWS_S, ROWS_ST = SHIFT, SHIFT + 4
VC = PART * DH + 1
EPS = 1e-5
HPU = 4
UNITS = 2 * H // HPU
E, F = 64, 64
NG, TG, TK = 8, 4, 8
ROUTE_SCALE = 2.5
LOW, LOWER = -3.0e38, -3.4e38


class Map:

    def __init__(self, nc, base, end):
        self.nc, self.at, self.end = nc, base, end

    def __call__(self, name, shape, dt):
        size = {F32: 4, F32R: 4, BF16: 2, FP16: 2}[dt]
        for n in shape[1:]:
            size *= n
        t = self.nc.alloc_sbuf_tensor_at(name, shape, dt, offset=self.at)
        self.at += (size + 31) // 32 * 32
        assert self.at <= self.end, (name, self.at, self.end)
        return t


def wait(eng, sem, value):
    if isinstance(value, int) and value <= 0:
        return
    eng.wait_ge(sem, value)


def wait_tick(nc, sem, value, tick):
    wait(nc.vector, sem, value)
    if not isinstance(value, int):
        nc.vector.tensor_copy(tick[0:1, 1:2], tick[0:1, 0:1])


def build(nc, x, ctx, g_xattn, g_ffn, Wqkv, bqkv, Wqkv_aux, bqkv_aux, Wo, bo, g_head,
          gate_w, gate_bias, We_gate, We_up, We_down, Ws_gate, Ws_up, Ws_down, out):
    NB = x.shape[0]
    CH = 2
    TC = CH * P
    base = (nc.sbuf_base + 63) // 64 * 64
    end = nc.sbuf_usable_end

    x2d = nc.dram_tensor("x2_scratch", (NB, P, P), F32, kind="Internal").ap()
    parts_d = nc.dram_tensor("parts_scratch", (NB // CH, 3 * PART, P, TC), BF16, kind="Internal").ap()

    with ExitStack() as ctx_:
        psum = [ctx_.enter_context(nc.psum_tensor(f"bank{i}", [P, 512], F32)) for i in range(8)]
        names = {}

        def sem(name):
            names[name] = ctx_.enter_context(nc.semaphore(name))
            return names[name]

        keep = Map(nc, base, end)
        ident = keep("ident", [P, P], F32)
        tick = keep("tick", [P, 2], F32)
        ident_bf = keep("ident_bf", [P, P], BF16)
        tg_x = keep("tg_x", [P, 1], F32)
        tg_f = keep("tg_f", [P, 1], F32)
        NEX = E + 2
        NP = NEX // 2
        raw_base = (end - (2 * NEX * F + NP * P) * 4) // 32 * 32
        raw = Map(nc, raw_base, end)
        wg_raw = raw("wg_raw", [P, NEX, F], F32)
        wu_raw = raw("wu_raw", [P, NEX, F], F32)
        wd_raw = raw("wd_raw", [P, NP, P], F32)
        w_in = [sem(f"w_in{i}") for i in range(3)]
        w_zero = sem("w_zero")

        v = dict(locals())
        with ExitStack() as stage:
            attention(nc, stage, sem, Map(nc, keep.at, raw_base), psum, v)
        with ExitStack() as stage:
            experts(nc, stage, sem, Map(nc, keep.at, raw_base), Map(nc, raw_base, end), psum, v)


def attention(nc, ctx_, sem, m, psum, v):
    x, ctx, x2d, parts_d = v["x"], v["ctx"], v["x2d"], v["parts_d"]
    tick = v["tick"]
    ident, ident_bf, tg_x, tg_f = v["ident"], v["ident_bf"], v["tg_x"], v["tg_f"]
    wg_raw, wu_raw, wd_raw, w_in, w_zero = v["wg_raw"], v["wu_raw"], v["wd_raw"], v["w_in"], v["w_zero"]
    NB, CH, TC = v["NB"], v["CH"], v["TC"]
    NC = NB // CH
    BODY = 2 * CH
    LOOPS = NB // BODY

    stack = [[m(f"stack_{o}{i}", [P, H, TC], BF16) for o in ("q", "k", "ka")] for i in range(2)]
    kones = m("kones", [P, 2], BF16)
    xin = [m(f"xin{i}", [P, CH, P], F32) for i in range(2)]
    cin = [m(f"cin{i}", [P, CH, P], F32) for i in range(2)]
    xres = [m(f"xres{i}", [P, CH, P], F32) for i in range(2)]
    x2 = [m(f"x2_{i}", [P, CH, P], F32) for i in range(2)]
    stats = m("stats", [P, CH, 6], F32)
    mv = m("mv", [P, CH, 2], F32)
    var = m("var", [P, CH], F32)
    rstd = m("rstd", [P, CH], F32)
    mhalf = m("mhalf", [P, CH], F32)
    xn = m("xn", [P, CH, P], F32)
    xcT = [m(f"xcT{i}", [P, 2, TC], F32) for i in range(2)]
    parts = [m(f"parts{i}", [P, 3, PART, TC], BF16) for i in range(2)]
    rest = m("rest", [P, 3, TC], F32)
    vrest = m("vrest", [P, 2 * CH, P], F32)
    V = [m(f"V{i}", [P, 2 * CH, H, VC], BF16) for i in range(2)]
    RP = 4
    p_hi = [m(f"p_hi{i}", [P, HPU * P], FP16) for i in range(RP)]
    p_all = [m(f"p_all{i}", [P, HPU * P], F32) for i in range(RP)]
    p_lo = [m(f"p_lo{i}", [P, HPU * P], FP16) for i in range(RP)]
    mx = m("mx", [P, 2, H], F32)
    nmax = m("nmax", [P, 4, 2, H], BF16)
    nmaxT = m("nmaxT", [4 * H, P], BF16)
    osum = m("osum", [P, 2, H, DH], F32)
    rden = m("rden", [P, 2, H], F32)
    rgate = m("rgate", [P, 2, H], F32)
    onorm = m("onorm", [P, 2, H, DH], F32)
    att = m("att", [P, P], F32)
    attT = m("attT", [P, P], F32)
    wqkv = m("wqkv", [P, 3, P], F32)
    wqkva = m("wqkva", [P, 3, P], F32)
    wo = m("wo", [P, P], F32)
    bcol = m("bcol", [P, 5], F32)
    bo_row = m("bo_row", [P, P], F32)
    gh = m("gh", [P, H], F32)
    ghc = m("ghc", [P, 1], F32)
    gcoef = m("gcoef", [P, 2, H], F32)
    gcol = m("gcol", [P, 2], F32)
    bvcol = m("bvcol", [P, 1], F32)
    tmpc = m("tmpc", [P, 4 + H], F32)
    scale = float(DH) ** -0.5

    s_bank, st_bank, o_bank, misc = psum[0:2], psum[2:4], psum[4:6], psum[6:8]

    c_in = sem("consts_loaded")
    ident_ok = sem("ident_ready")
    ident_step = sem("ident_step")
    kones_ok = sem("kones_ready")
    const_ok, tanh_ok = sem("consts_ready"), sem("tanh_ready")
    cstep_a, cstep_v = sem("const_step_act"), sem("const_step_dve")
    bo_ok = sem("bo_row_scaled")
    stack_zero = sem("stacks_zeroed")
    x_in = [sem(f"x_in{i}") for i in range(2)]
    xr_in = [sem(f"xres_in{i}") for i in range(2)]
    stats_ok, mv_ok, var_ok, rstd_ok, xn_ok = (sem(n) for n in ("ln_stats", "ln_mv", "ln_var", "ln_rstd", "xn_ready"))
    t_mm, t_ev = sem("transposes_done"), sem("xcT_ready")
    qk_mm, ka_mm, v_mm = sem("qk_projected"), sem("ka_projected"), sem("v_projected")
    qk_hi, ka_hi, v_hi = sem("qk_hi"), sem("ka_hi"), sem("v_hi")
    qk_rest, ka_rest, v_rest = sem("qk_rest"), sem("ka_rest"), sem("v_rest")
    mid_ok, lo_ok, v_mid, v_ok = sem("mid_ready"), sem("lo_ready"), sem("v_mid"), sem("v_ready")
    scr = [sem(f"parts_stored{i}") for i in range(2)]
    stk = [sem(f"stack_loaded{i}") for i in range(2)]
    s_mm, mx_ok = sem("scores_for_max"), sem("max_taken")
    nm_hi, nm_ok, nm_mm, nm_ev = sem("nmax_hi"), sem("nmax_ready"), sem("nmax_transposed"), sem("nmaxT_ready")
    shift = sem("shift_rows_loaded")
    st_mm, ph_ok, pa_ok, pl_ok = sem("shifted_scores"), sem("p_hi_ready"), sem("p_ready"), sem("p_lo_ready")
    pv_ok = sem("pv_done")
    o_sum, o_red = sem("o_summed"), sem("o_reduced")
    rg_ok, on_ok, at_ok = sem("rgate_ready"), sem("onorm_ready"), sem("att_ready")
    at_mm, at_ev, wo_mm = sem("att_transposed"), sem("attT_ready"), sem("wo_done")
    xb_ok, x2_ok = sem("xres_biased"), sem("x2_ready")
    x2_st = [sem(f"x2_stored{i}") for i in range(2)]

    x_v = x.rearrange("(n k) t d -> n t k d", k=CH)
    c_v = ctx.rearrange("(n k) t d -> n t k d", k=CH)
    x2_v = x2d.rearrange("(n k) t d -> n t k d", k=CH)
    parts_v = parts_d.rearrange("n a (h d) t -> n a d h t", d=DH)
    CONSTS = 13

    block = ctx_.enter_context(nc.Block())

    def const_loads(eng):
        one = lambda a: a.rearrange("(a n) -> a n", a=1)
        col = lambda a: a.rearrange("(n a) -> n a", a=1)
        eng.dma_start(wqkv[:], v["Wqkv"].rearrange("d (o n) -> d o n", o=3)).then_inc(c_in, 16)
        eng.dma_start(wqkva[:], v["Wqkv_aux"].rearrange("d (o n) -> d o n", o=3)).then_inc(c_in, 16)
        eng.dma_start(wo[:], v["Wo"]).then_inc(c_in, 16)
        for i, b in enumerate((v["bqkv"][0:P], v["bqkv"][P:2 * P], v["bqkv"][2 * P:3 * P],
                               v["bqkv_aux"][P:2 * P], v["bqkv_aux"][2 * P:3 * P])):
            eng.dma_start(bcol[:, i:i + 1], col(b)).then_inc(c_in, 16)
        eng.dma_start(bo_row[:], one(v["bo"]).to_broadcast([P, P])).then_inc(c_in, 16)
        eng.dma_start(gh[:], one(v["g_head"]).to_broadcast([P, H])).then_inc(c_in, 16)
        eng.dma_start(ghc[:].rearrange("p a -> p a"),
                      v["g_head"].rearrange("(h a b) -> h a b", a=1, b=1).to_broadcast([H, DH, 1])).then_inc(c_in, 16)
        eng.dma_start(tg_x[:], one(v["g_xattn"]).to_broadcast([P, 1])).then_inc(c_in, 16)
        eng.dma_start(tg_f[:], one(v["g_ffn"]).to_broadcast([P, 1])).then_inc(c_in, 16)

    @block.sync
    def _(sp):
        def load_x(n, i):
            wait(sp, t_ev, n - 1)
            sp.dma_start(xin[i][:], x_v[n]).then_inc(x_in[i], 16)
            sp.dma_start(cin[i][:], c_v[n]).then_inc(x_in[i], 16)

        def load_res(n, i):
            wait(sp, x2_ok, CH * (n - 1))
            sp.dma_start(xres[i][:], x_v[n]).then_inc(xr_in[i], 16)

        def store_parts(n, n2, i):
            wait(sp, lo_ok, n + 1)
            sp.dma_start(parts_d[n].rearrange("a p t -> p a t"),
                         parts[i][:].rearrange("p o a t -> p (o a) t")).then_inc(scr[i], 16)

        def load_stack(n, n2, i, operands):
            wait(sp, st_mm, UNITS * CH * (n - 1))
            wait(sp, scr[i], 16 * (n2 + 1))
            for o in operands:
                for slot, a in enumerate(Q_SLOTS if o == 0 else K_SLOTS):
                    sp.dma_start(stack[i][o][slot * DH:(slot + 1) * DH, :, :],
                                 parts_v[n][o * PART + a]).then_inc(stk[i], 16)

        def shift_rows(b, k):
            wait(sp, nm_ev, b + 1)
            sp.dma_start(stack[k // CH][0][SHIFT:SHIFT + 4, :, (k % CH) * P:(k % CH + 1) * P],
                         nmaxT[:]).then_inc(shift, 16)

        def store_x2(n, i):
            wait(sp, x2_ok, CH * (n + 1))
            sp.dma_start(x2_v[n], x2[i][:]).then_inc(x2_st[i], 16)

        load_x(0, 0)
        const_loads(sp)
        load_x(1, 1)
        load_res(0, 0)
        load_res(1, 1)
        store_parts(0, 0, 0)
        sp.wait_ge(stack_zero, 1)
        load_stack(0, 0, 0, (0, 1, 2))
        store_parts(1, 0, 1)
        shift_rows(0, 0)

        def body(g, last):
            for j in range(2):
                n, i = 2 * g + j, j
                more, more2 = not (last and j == 1), not last
                if more:
                    load_stack(n + 1, g + (j + 1) // 2, (j + 1) % 2, (0, 1))
                if more2:
                    load_x(n + 2, i)
                shift_rows(2 * n + 1, 2 * i + 1)
                if more:
                    load_stack(n + 1, g + (j + 1) // 2, (j + 1) % 2, (2,))
                if more2:
                    store_parts(n + 2, g + 1, i)
                if not (isinstance(n, int) and n == 0):
                    store_x2(n - 1, (j + 1) % 2)
                    if more:
                        load_res(n + 1, (j + 1) % 2)
                if more:
                    shift_rows(2 * n + 2, (2 * i + 2) % BODY)

        body(0, False)
        with sp.Fori(1, LOOPS - 1) as g:
            body(g, False)
        body(LOOPS - 1, True)
        store_x2(NC - 1, 1)
        for i in range(2):
            sp.wait_ge(x2_st[i], 16 * (NC // 2))

    @block.gpsimd
    def _(pool):
        pool.memset(ident[:], 0.0).then_inc(ident_step, 1)
        pool.wait_ge(ident_step, 1)
        pool.affine_select(out=ident[:], in_=ident[:], compare_op=ALU.not_equal, fill=1.0, base=0,
                           pattern=[[-1, P]], channel_multiplier=1).then_inc(ident_step, 1)
        pool.wait_ge(ident_step, 2)
        pool.tensor_copy(ident_bf[:], ident[:]).then_inc(ident_ok, 1)
        pool.memset(kones[:], 1.0).then_inc(kones_ok, 1)
        pool.memset(mhalf[:], -0.5).then_inc(kones_ok, 1)
        pool.wait_ge(kones_ok, 2)
        pool.affine_select(out=kones[:, 0:1], in_=kones[:, 0:1], compare_op=ALU.is_ge, fill=0.0,
                           base=SHIFT + 1, pattern=[[0, 1]], channel_multiplier=-1).then_inc(kones_ok, 1)
        pool.affine_select(out=kones[:, 1:2], in_=kones[:, 1:2], compare_op=ALU.is_ge, fill=0.0,
                           base=-SHIFT - 2, pattern=[[0, 1]], channel_multiplier=1).then_inc(kones_ok, 1)
        for i in range(2):
            pool.memset(V[i][:], 1.0).then_inc(kones_ok, 1)
        pool.memset(wg_raw[:, E + 1, :], 0.0).then_inc(w_zero, 1)
        pool.memset(wu_raw[:, E + 1, :], 0.0).then_inc(w_zero, 1)
        pool.wait_ge(kones_ok, 6)
        pool.wait_ge(w_zero, 2)
        pool.memset(wd_raw[F:P, (E + 1) // 2, :], 0.0).then_inc(w_zero, 1)
        pool.wait_ge(w_zero, 3)
        for e0 in range(0, E, 16):
            for w, d in ((wg_raw, v["We_gate"]), (wu_raw, v["We_up"])):
                pool.dma_start(w[:, e0:e0 + 16, :], d[e0:e0 + 16].rearrange("e d f -> d e f")).then_inc(w_in[0], 16)
        pool.dma_start(wg_raw[:, E, :], v["Ws_gate"]).then_inc(w_in[1], 16)
        pool.dma_start(wu_raw[:, E, :], v["Ws_up"]).then_inc(w_in[1], 16)
        wd_v = v["We_down"].rearrange("(p two) f d -> two f p d", two=2)
        for half in range(2):
            pool.dma_start(wd_raw[half * F:(half + 1) * F, 0:E // 2, :], wd_v[half]).then_inc(w_in[2], 16)
        pool.dma_start(wd_raw[0:F, E // 2, :], v["Ws_down"]).then_inc(w_in[2], 16)

        pool.wait_ge(tanh_ok, 2)
        pool.tensor_scalar(bo_row[:], bo_row[:], tg_x[:, 0:1], 1.0, ALU.mult, ALU.mult).then_inc(bo_ok, 1)
        pool.wait_ge(bo_ok, 1)

        def root(n):
            wait(pool, var_ok, n + 1)
            pool.tensor_tensor(rstd[:], var[:], mhalf[:], ALU.pow).then_inc(rstd_ok, 1)

        def bias_res(n, n2, i):
            wait(pool, xr_in[i], 16 * (n2 + 1))
            pool.tensor_tensor(xres[i][:], xres[i][:], bo_row[:].unsqueeze(1).to_broadcast([P, CH, P]),
                               ALU.add).then_inc(xb_ok, 1)

        def low_part(b, u):
            wait(pool, pa_ok, UNITS * b + u + 1)
            wait(pool, pv_ok, UNITS * b + u + 1 - RP)
            pool.tensor_tensor(p_lo[u % RP][:], p_all[u % RP][:], p_hi[u % RP][:], ALU.subtract).then_inc(pl_ok, 1)

        def normalise(b):
            wait(pool, o_red, 2 * b + 2)
            pool.tensor_tensor(rgate[:], rden[:], gcoef[:], ALU.mult).then_inc(rg_ok, 1)
            wait(pool, rg_ok, b + 1)
            pool.tensor_tensor(onorm[:], osum[:], rgate[:].unsqueeze(3).to_broadcast([P, 2, H, DH]),
                               ALU.mult).then_inc(on_ok, 1)
            wait(pool, on_ok, b + 1)
            wait(pool, at_mm, b)
            pool.tensor_tensor(att[:].rearrange("p (h d) -> p h d", h=H), onorm[:, 0], onorm[:, 1],
                               ALU.add).then_inc(at_ok, 1)

        root(0)
        root(1)
        bias_res(0, 0, 0)

        def body(g, last):
            for k in range(BODY):
                b, n, i = BODY * g + k, 2 * g + k // CH, k // CH
                first = isinstance(b, int) and b == 0
                for u in range(UNITS):
                    low_part(b, u)
                    if u == 1 and not first:
                        normalise(b - 1)
                    if u == 0 and k % CH == 0 and not last:
                        root(n + 2)
                    if u == 5 and k % CH == 1 and not (last and k == BODY - 1):
                        bias_res(n + 1, g + (i + 1) // 2, (i + 1) % 2)

        body(0, False)
        with pool.Fori(1, LOOPS - 1) as g:
            body(g, False)
        body(LOOPS - 1, True)
        normalise(NB - 1)

    @block.scalar
    def _(act):
        act.wait_ge(c_in, 16 * CONSTS)
        act.activation(tmpc[:, 0:H], gh[:], ACT.Exp, scale=-1.0).then_inc(cstep_a, 1)
        act.activation(tmpc[:, H:H + 1], ghc[:], ACT.Exp, scale=-1.0).then_inc(cstep_a, 1)
        act.activation(tg_x[:], tg_x[:], ACT.Tanh).then_inc(tanh_ok, 1)
        act.activation(tg_f[:], tg_f[:], ACT.Tanh).then_inc(tanh_ok, 1)

        def evac_t(n, i):
            wait(act, t_mm, n + 1)
            act.activation(xcT[i][:].rearrange("p a t -> p (a t)"), misc[0][:], ACT.Copy).then_inc(t_ev, 1)

        def hi_qk(n, n2, i):
            wait(act, qk_mm, n + 1)
            wait(act, scr[i], 16 * n2)
            for o in range(2):
                ins = act.activation(parts[i][:, o, 0, :], misc[1][:, o * TC:(o + 1) * TC], ACT.Identity,
                                     bias=bcol[:, o:o + 1])
            ins.then_inc(qk_hi, 1)

        def hi_ka(n, i):
            wait(act, ka_mm, n + 1)
            act.activation(parts[i][:, 2, 0, :], misc[1][:, 0:TC], ACT.Identity, bias=bcol[:, 3:4]).then_inc(ka_hi, 1)

        def mid(n, i):
            wait(act, ka_rest, n + 1)
            act.activation(parts[i][:, :, 1, :], rest[:], ACT.Copy).then_inc(mid_ok, 1)

        def hi_v(n, i):
            wait(act, v_mm, n + 1)
            act.activation(V[i][:, :, :, 0:DH], misc[0][:].rearrange("p (a h d) -> p a h d", h=H, d=DH),
                           ACT.Copy).then_inc(v_hi, 1)

        def mid_v(n, i):
            wait(act, v_rest, n + 1)
            act.activation(V[i][:, :, :, DH:2 * DH], vrest[:].rearrange("p a (h d) -> p a h d", d=DH),
                           ACT.Copy).then_inc(v_mid, 1)

        def exps(b, u):
            wait(act, st_mm, UNITS * b + u + 1)
            wait(act, pv_ok, UNITS * b + u + 1 - RP)
            act.activation(p_hi[u % RP][:], st_bank[u % 2][:], ACT.Exp, scale=scale).then_inc(ph_ok, 1)
            act.activation(p_all[u % RP][:], st_bank[u % 2][:], ACT.Exp, scale=scale).then_inc(pa_ok, 1)

        def evac_att(b, bank):
            wait(act, at_mm, b + 1)
            wait(act, wo_mm, b)
            act.activation(attT[:], misc[bank][:, 0:P], ACT.Identity, bias=bvcol[:, 0:1]).then_inc(at_ev, 1)

        act.wait_ge(kones_ok, 6)
        for n in range(2):
            evac_t(n, n)
            hi_qk(n, 0, n)
            hi_ka(n, n)
            mid(n, n)
            if n == 0:
                hi_v(0, 0)
                mid_v(0, 0)
        act.wait_ge(const_ok, 1)

        def body(g, last):
            for k in range(BODY):
                b, n, i, odd = BODY * g + k, 2 * g + k // CH, k // CH, k % CH
                first = isinstance(b, int) and b == 0
                more = not (last and i == 1)
                for u in range(UNITS):
                    exps(b, u)
                    if u == 2 and not odd and not last:
                        evac_t(n + 2, i)
                    if u == 4 and not odd and not last:
                        hi_qk(n + 2, g + 1, i)
                    if u == 1 and odd and not last:
                        hi_ka(n + 2, i)
                    if u == 2 and odd and not last:
                        mid(n + 2, i)
                    if u == 3 and odd and more:
                        hi_v(n + 1, (i + 1) % 2)
                    if u == 4 and odd and more:
                        mid_v(n + 1, (i + 1) % 2)
                    if u == 5 and not first:
                        evac_att(b - 1, odd)

        body(0, False)
        with act.Fori(1, LOOPS - 1) as g:
            body(g, False)
        body(LOOPS - 1, True)
        evac_att(NB - 1, 0)

    @block.vector
    def _(dve):
        for o in range(3):
            for i in range(2):
                nc.vector.memset(stack[i][o][:], 0.0)
        dve.wait_ge(kones_ok, 4)
        nc.vector.memset(nmax[:], 0.0)
        nc.vector.memset(tick[:], 0.0)
        ins = nc.vector.memset(mx[:], 0.0)
        ins.then_inc(cstep_v, 1)
        dve.wait_ge(cstep_v, 1)
        for i in range(2):
            for o in (1, 2):
                ins = nc.vector.tensor_copy(stack[i][o][SHIFT:SHIFT + 4, :, :].rearrange("p h t -> p (h t)"),
                                            kones[SHIFT:SHIFT + 4, o - 1:o].to_broadcast([4, H * TC]))
        ins.then_inc(stack_zero, 1)

        dve.wait_ge(cstep_a, 2)
        nc.vector.tensor_scalar(tmpc[:, 0:H + 1], tmpc[:, 0:H + 1], 1.0, None, ALU.add).then_inc(cstep_v, 1)
        dve.wait_ge(cstep_v, 2)
        nc.vector.reciprocal(gcoef[:, 1, :], tmpc[:, 0:H]).then_inc(cstep_v, 1)
        nc.vector.reciprocal(gcol[:, 0:1], tmpc[:, H:H + 1]).then_inc(cstep_v, 1)
        dve.wait_ge(cstep_v, 4)
        nc.vector.tensor_scalar(gcoef[:, 0, :], gcoef[:, 1, :], -1.0, 1.0, ALU.mult, ALU.add).then_inc(cstep_v, 1)
        nc.vector.tensor_scalar(gcol[:, 1:2], gcol[:, 0:1], -1.0, 1.0, ALU.mult, ALU.add).then_inc(cstep_v, 1)
        dve.wait_ge(cstep_v, 6)
        nc.vector.tensor_scalar(bvcol[:], bcol[:, 4:5], gcol[:, 0:1], None, ALU.mult).then_inc(cstep_v, 1)
        dve.wait_ge(cstep_v, 7)
        nc.vector.scalar_tensor_tensor(out=bvcol[:], in0=bcol[:, 2:3], scalar=gcol[:, 1:2], in1=bvcol[:],
                                       op0=ALU.mult, op1=ALU.add).then_inc(const_ok, 1)

        def norm_stats(n, n2, i):
            wait(dve, x_in[i], 32 * (n2 + 1))
            for c in range(CH):
                ins = nc.vector.bn_stats(stats[:, c, :], xin[i][:, c, :])
            ins.then_inc(stats_ok, 1)
            wait_tick(nc, stats_ok, n + 1, tick)
            for c in range(CH):
                ins = nc.vector.bn_aggr(mv[:, c, :], stats[:, c, :])
            ins.then_inc(mv_ok, 1)
            wait(dve, mv_ok, n + 1)
            nc.vector.tensor_scalar(var[:], mv[:, :, 1], EPS, None, ALU.add).then_inc(var_ok, 1)

        def norm(n, i):
            wait(dve, rstd_ok, n + 1)
            wait(dve, t_mm, n)
            for c in range(CH):
                ins = nc.vector.tensor_scalar(xn[:, c, :], xin[i][:, c, :], mv[:, c, 0:1], rstd[:, c:c + 1],
                                              ALU.subtract, ALU.mult)
            ins.then_inc(xn_ok, 1)

        def rest_qk(n, i):
            wait(dve, qk_hi, n + 1)
            wait(dve, lo_ok, n)
            wait(dve, mid_ok, n)
            for o in range(2):
                ins = nc.vector.scalar_tensor_tensor(
                    out=rest[:, o, :], in0=misc[1][:, o * TC:(o + 1) * TC], scalar=bcol[:, o:o + 1],
                    in1=parts[i][:, o, 0, :], op0=ALU.add, op1=ALU.subtract)
            ins.then_inc(qk_rest, 1)

        def rest_ka(n, i):
            wait(dve, ka_hi, n + 1)
            nc.vector.scalar_tensor_tensor(
                out=rest[:, 2, :], in0=misc[1][:, 0:TC], scalar=bcol[:, 3:4],
                in1=parts[i][:, 2, 0, :], op0=ALU.add, op1=ALU.subtract).then_inc(ka_rest, 1)

        def low(n, i):
            wait(dve, mid_ok, n + 1)
            wait(dve, ka_rest, n + 1)
            nc.vector.tensor_tensor(parts[i][:, :, 2, :], rest[:], parts[i][:, :, 1, :],
                                    ALU.subtract).then_inc(lo_ok, 1)

        def rest_v(n, i):
            wait(dve, v_hi, n + 1)
            nc.vector.tensor_tensor(vrest[:].rearrange("p a (h d) -> p (a h) d", d=DH),
                                    misc[0][:].rearrange("p (a h d) -> p (a h) d", h=H, d=DH),
                                    V[i][:, :, :, 0:DH].rearrange("p a h d -> p (a h) d"),
                                    ALU.subtract).then_inc(v_rest, 1)

        def low_v(n, i):
            wait(dve, v_mid, n + 1)
            wait(dve, v_rest, n + 1)
            nc.vector.tensor_tensor(V[i][:, :, :, 2 * DH:3 * DH].rearrange("p a h d -> p (a h) d"),
                                    vrest[:].rearrange("p a (h d) -> p (a h) d", d=DH),
                                    V[i][:, :, :, DH:2 * DH].rearrange("p a h d -> p (a h) d"),
                                    ALU.subtract).then_inc(v_ok, 1)

        def maxima(b, u):
            wait(dve, s_mm, UNITS * b + u + 1)
            if u == 0:
                wait(dve, nm_ok, b)
            nc.vector.tensor_reduce(mx[:, u // (UNITS // 2), (u % (UNITS // 2)) * HPU:(u % (UNITS // 2) + 1) * HPU],
                                    s_bank[u % 2][:].rearrange("p (h k) -> p h k", h=HPU), AXX,
                                    ALU.max).then_inc(mx_ok, 1)

        def minus_max(b):
            wait(dve, mx_ok, UNITS * (b + 1))
            wait(dve, nm_mm, b)
            nc.vector.tensor_scalar(nmax[:, 0:2, 0, :], mx[:], -1.0, None, ALU.mult).then_inc(nm_hi, 1)
            wait(dve, nm_hi, b + 1)
            nc.vector.scalar_tensor_tensor(out=nmax[:, 0:2, 1, :], in0=mx[:], scalar=-1.0, in1=nmax[:, 0:2, 0, :],
                                           op0=ALU.mult, op1=ALU.subtract).then_inc(nm_ok, 1)

        def evac_nmax(b, bank):
            wait(dve, nm_mm, b + 1)
            wait(dve, shift, 16 * b)
            nc.vector.tensor_copy(nmaxT[:], misc[bank][0:4 * H, 0:P // 2].bitcast(BF16)).then_inc(nm_ev, 1)

        def sums(b, a):
            wait(dve, pv_ok, UNITS * b + (UNITS // 2) * (a + 1))
            wait(dve, on_ok, b)
            wait(dve, rg_ok, b)
            o = o_bank[a][:, 0:H * VC].rearrange("p (h c) -> p h c", h=H)
            nc.vector.tensor_reduce(osum[:, a], o[:, :, 0:PART * DH].rearrange("p h (s d) -> p h d s", s=PART),
                                    AXX, ALU.add)
            nc.vector.reciprocal(rden[:, a, :], o[:, :, VC - 1]).then_inc(o_red, 1)

        def residual(b, n, i, odd, bank):
            wait(dve, wo_mm, b + 1)
            wait(dve, xb_ok, n + 1)
            if not odd:
                wait(dve, x2_st[i], 16 * ((n - i) // 2 if isinstance(n, int) else 0) if isinstance(n, int)
                     else n * 8 - 8 * i)
            nc.vector.scalar_tensor_tensor(out=x2[i][:, odd, :], in0=misc[bank][:, 0:P], scalar=tg_x[:, 0:1],
                                           in1=xres[i][:, odd, :], op0=ALU.mult, op1=ALU.add).then_inc(x2_ok, 1)

        dve.wait_ge(tanh_ok, 2)
        dve.wait_ge(const_ok, 1)
        for n in range(2):
            norm_stats(n, 0, n)
            norm(n, n)
            rest_qk(n, n)
            rest_ka(n, n)
            low(n, n)
            if n == 0:
                rest_v(0, 0)
                low_v(0, 0)
        for u in range(UNITS):
            maxima(0, u)
        minus_max(0)
        evac_nmax(0, 1)

        def body(g, last):
            for k in range(BODY):
                b, n, i, odd = BODY * g + k, 2 * g + k // CH, k // CH, k % CH
                first = isinstance(b, int) and b == 0
                more = not (last and i == 1)
                ahead = not (last and k == BODY - 1)
                nu = 0
                for u in range(UNITS):
                    for _ in range(S_PLAN[u]):
                        if ahead:
                            maxima(b + 1, nu)
                        nu += 1
                    if u == 0 and not odd and not last:
                        norm_stats(n + 2, g + 1, i)
                    if u == 1 and not odd and not last:
                        norm(n + 2, i)
                    if u == 2 and not first:
                        sums(b - 1, 1)
                    if u == 4 and not odd and not last:
                        rest_qk(n + 2, i)
                    if u == 1 and odd and not last:
                        rest_ka(n + 2, i)
                    if u == 3 and odd and not last:
                        low(n + 2, i)
                    if u == 4 and odd and more:
                        rest_v(n + 1, (i + 1) % 2)
                    if u == 5 and odd and more:
                        low_v(n + 1, (i + 1) % 2)
                    if u == 5 and ahead:
                        minus_max(b + 1)
                    if u == 6:
                        sums(b, 0)
                    if u == 6 and not first:
                        nb, ni = (n, i) if odd else (n - 1, 1 - i)
                        residual(b - 1, nb, ni, 1 - odd, 1 - odd)
                    if u == 7 and ahead:
                        evac_nmax(b + 1, odd)

        body(0, False)
        with dve.Fori(1, LOOPS - 1) as g:
            body(g, False)
        body(LOOPS - 1, True)
        sums(NB - 1, 1)
        residual(NB - 1, NC - 1, 1, 1, 1)

    @block.tensor
    def _(pe):
        def transposes(n, n2, i):
            wait(pe, xn_ok, n + 1)
            wait(pe, x_in[i], 32 * (n2 + 1))
            for c in range(CH):
                nc.tensor.transpose(misc[0][:, c * P:(c + 1) * P], xn[:, c, :], ident[:])
            for c in range(CH):
                ins = nc.tensor.transpose(misc[0][:, TC + c * P:TC + (c + 1) * P], cin[i][:, c, :], ident[:])
            ins.then_inc(t_mm, 1)

        def project_qk(n, i):
            wait(pe, t_ev, n + 1)
            for o in range(2):
                ins = nc.tensor.matmul(misc[1][:, o * TC:(o + 1) * TC], wqkv[:, o, :], xcT[i][:, 0, :],
                                       start=True, stop=True)
            ins.then_inc(qk_mm, 1)

        def project_ka(n, i):
            nc.tensor.matmul(misc[1][:, 0:TC], wqkva[:, 1, :], xcT[i][:, 1, :],
                             start=True, stop=True).then_inc(ka_mm, 1)

        def project_v(n, i):
            for a, w in enumerate((wqkv, wqkva)):
                for c in range(CH):
                    o = (a * CH + c) * P
                    ins = nc.tensor.matmul(misc[0][:, o:o + P], xcT[i][:, a, c * P:(c + 1) * P], w[:, 2, :],
                                           start=True, stop=True)
            ins.then_inc(v_mm, 1)

        def scores(b, k, u, n2):
            i, c = k // CH, k % CH
            if u == 0:
                wait(pe, stk[i], 16 * 3 * len(Q_SLOTS) * (n2 + 1))
            wait(pe, mx_ok, UNITS * b + u - 1)
            q, kk = stack[i][0], stack[i][1 + u // (UNITS // 2)]
            for j in range(HPU):
                h = (u % (UNITS // 2)) * HPU + j
                ins = nc.tensor.matmul(s_bank[u % 2][:, j * P:(j + 1) * P], q[0:ROWS_S, h, c * P:(c + 1) * P],
                                       kk[0:ROWS_S, h, c * P:(c + 1) * P], start=True, stop=True)
            ins.then_inc(s_mm, 1)

        def shifted(b, k, u):
            i, c = k // CH, k % CH
            if u == 0:
                wait(pe, shift, 16 * (b + 1))
            wait(pe, pa_ok, UNITS * b + u - 1)
            q, kk = stack[i][0], stack[i][1 + u // (UNITS // 2)]
            for j in range(HPU):
                h = (u % (UNITS // 2)) * HPU + j
                ins = nc.tensor.matmul(st_bank[u % 2][:, j * P:(j + 1) * P], kk[0:ROWS_ST, h, c * P:(c + 1) * P],
                                       q[0:ROWS_ST, h, c * P:(c + 1) * P], start=True, stop=True)
            ins.then_inc(st_mm, 1)

        def weighted(b, k, u):
            i, c = k // CH, k % CH
            a = u // (UNITS // 2)
            wait(pe, pl_ok, UNITS * b + u + 1)
            if u == 0:
                wait(pe, v_ok, b // CH + 1 if isinstance(b, int) else v_ready_of(b))
                wait(pe, o_red, 2 * b - 1)
            if u == UNITS // 2:
                wait(pe, o_red, 2 * b)
            for j in range(HPU):
                h = (u % (UNITS // 2)) * HPU + j
                o = o_bank[a][:, h * VC:(h + 1) * VC]
                nc.tensor.matmul(o, p_hi[u % RP][:, j * P:(j + 1) * P], V[i][:, a * CH + c, h, :],
                                 start=True, stop=False)
                ins = nc.tensor.matmul(o, p_lo[u % RP][:, j * P:(j + 1) * P], V[i][:, a * CH + c, h, :],
                                       start=False, stop=True)
            ins.then_inc(pv_ok, 1)

        chunk_now = [None]

        def v_ready_of(b):
            return chunk_now[0] + 1

        def turn_att(b, bank):
            wait(pe, at_ok, b + 1)
            nc.tensor.transpose(misc[bank][:, 0:P], att[:], ident[:]).then_inc(at_mm, 1)

        def out_proj(b, bank):
            wait(pe, at_ev, b + 1)
            nc.tensor.matmul(misc[bank][:, 0:P], attT[:], wo[:], start=True, stop=True).then_inc(wo_mm, 1)

        def turn_max(b, bank):
            wait(pe, nm_ok, b + 1)
            nc.tensor.transpose(misc[bank][:, 0:P // 2].bitcast(BF16),
                                nmax[:].rearrange("p a s h -> p (a s h)"), ident_bf[:]).then_inc(nm_mm, 1)

        pe.wait_ge(ident_ok, 1)
        pe.wait_ge(c_in, 16 * CONSTS)
        for n in range(2):
            if n == 1:
                pe.wait_ge(v_rest, 1)
            transposes(n, 0, n)
            if n == 1:
                pe.wait_ge(ka_rest, 1)
            project_qk(n, n)
            pe.wait_ge(qk_rest, n + 1)
            project_ka(n, n)
            if n == 0:
                project_v(0, 0)
        pe.wait_ge(stack_zero, 1)
        for u in range(UNITS):
            scores(0, 0, u, 0)
        pe.wait_ge(ka_rest, 2)
        turn_max(0, 1)

        def body(g, last):
            for k in range(BODY):
                b, n, i, odd = BODY * g + k, 2 * g + k // CH, k // CH, k % CH
                first = isinstance(b, int) and b == 0
                more = not (last and i == 1)
                ahead = not (last and k == BODY - 1)
                nu = 0
                for u in range(UNITS):
                    shifted(b, k, u)
                    if u >= 2:
                        chunk_now[0] = n
                        weighted(b, k, u - 2)
                    elif not first:
                        chunk_now[0] = n if odd else n - 1
                        weighted(b - 1, (k - 1) % BODY, u + UNITS - 2)
                    for _ in range(S_PLAN[u]):
                        if ahead:
                            scores(b + 1, (k + 1) % BODY, nu, g + (k + 1) // BODY)
                        nu += 1
                    if not odd:
                        if u == 2 and not last:
                            wait(pe, x2_ok, b - 1)
                            transposes(n + 2, g + 1, i)
                        if u == 4 and not last:
                            wait(pe, nm_ev, b + 1)
                            project_qk(n + 2, i)
                        if u == 4 and not first:
                            if not last:
                                wait(pe, t_ev, n + 3)
                            wait(pe, x2_ok, b - 1)
                            turn_att(b - 1, 0)
                        if u == 6 and not first:
                            if not last:
                                wait(pe, qk_rest, n + 3)
                            wait(pe, nm_ev, b + 1)
                            out_proj(b - 1, 1)
                        if u == 7 and ahead:
                            wait(pe, at_ev, b)
                            if first:
                                wait(pe, t_ev, n + 3)
                            turn_max(b + 1, 0)
                    else:
                        if u == 1 and not last:
                            wait(pe, x2_ok, b - 1)
                            if isinstance(b, int) and b == 1:
                                wait(pe, qk_rest, n + 3)
                            project_ka(n + 2, i)
                        if u == 3 and more:
                            wait(pe, nm_ev, b + 1)
                            project_v(n + 1, (i + 1) % 2)
                        if u == 4:
                            if not last:
                                wait(pe, ka_rest, n + 3)
                            wait(pe, x2_ok, b - 1)
                            turn_att(b - 1, 1)
                        if u == 6:
                            if more:
                                wait(pe, v_rest, n + 2)
                            wait(pe, nm_ev, b + 1)
                            out_proj(b - 1, 0)
                        if u == 7 and ahead:
                            wait(pe, at_ev, b)
                            turn_max(b + 1, 1)

        body(0, False)
        with pe.Fori(1, LOOPS - 1) as g:
            body(g, False)
        body(LOOPS - 1, True)
        for u in range(2):
            chunk_now[0] = NC - 1
            weighted(NB - 1, BODY - 1, u + UNITS - 2)
        pe.wait_ge(x2_ok, NB - 1)
        turn_att(NB - 1, 0)
        out_proj(NB - 1, 1)


S_PLAN = (2, 1, 1, 2, 1, 1, 0, 0)


def experts(nc, ctx_, sem, m, r, psum, v):
    tick = v["tick"]
    x2d, out, ident, tg_f = v["x2d"], v["out"], v["ident"], v["tg_f"]
    wg_raw, wu_raw, wd_raw, w_in, w_zero = v["wg_raw"], v["wu_raw"], v["wd_raw"], v["w_in"], v["w_zero"]
    NEX, NP, NB = v["NEX"], v["NP"], v["NB"]
    K = 4
    T = K * P
    NCH = NB // K
    LOOPS = NCH // 2
    LAG = 4
    GP = 3
    GROUPS = NP // GP
    EPG = E // NG
    RS, RH = 3, 6

    wg = [m(f"wg_{s}", [P, NEX, F], F32R) for s in ("hi", "lo")]
    wu = [m(f"wu_{s}", [P, NEX, F], F32R) for s in ("hi", "lo")]
    wd = [m(f"wd_{s}", [P, NP, P], F32R) for s in ("hi", "lo")]
    x2c = [m(f"x2c{i}", [P, K, P], F32) for i in range(2)]
    xhi = [m(f"xhi{i}", [P, T], F32R) for i in range(2)]
    xlo = [m(f"xlo{i}", [P, T], F32R) for i in range(2)]
    hhi = [m(f"hhi{i}", [P, T], F32R) for i in range(RH)]
    hlo = [m(f"hlo{i}", [P, T], F32R) for i in range(RH)]
    xn = m("xn2", [P, K, P], F32)
    xT = m("xT2", [P, T], F32)
    wT = m("wT", [NEX, T], F32)
    stats = m("stats2", [P, K, 6], F32)
    mv = m("mv2", [P, K, 2], F32)
    var = m("var2", [P, K], F32)
    rstd = m("rstd2", [P, K], F32)
    mhalf = m("mhalf2", [P, K], F32)
    gw_in = m("gw_in", [E, P], F32)
    gwT = m("gwT", [P, E], F32)
    gbias = m("gbias", [P, E], F32)
    tri = m("tri", [P, NG, NG], F32)
    s_buf = [r(f"silu{i}", [P, T], F32) for i in range(RS)]
    a_buf = [r(f"act{i}", [P, T], F32) for i in range(RS)]
    h_buf = [r(f"hid{i}", [P, T], F32) for i in range(RS)]
    cwb = [r(f"cwb{i}", [P, GP, T], F32) for i in range(2)]
    ysb = r("ysb", [P, T], F32)
    osb = [r(f"osb{i}", [P, K, P], F32) for i in range(2)]
    sig = m("sig", [P, K, E], F32)
    sc = m("sc", [P, K, E], F32)
    top_a, low_a = m("top_a", [P, K * NG, 4], F32), m("low_a", [P, K * NG, 4], F32)
    top_b, low_b, mid_b = (m(f"{n}_b", [P, K * NG, 2], F32) for n in ("top", "low", "mid"))
    top_c, low_c, mid_c = (m(f"{n}_c", [P, K * NG, 1], F32) for n in ("top", "low", "mid"))
    gs = m("gs", [P, K, NG], F32)
    gt = r("gt", [P, K, NG, NG], F32)
    eq = r("eq", [P, K, NG, NG], F32)
    rank = m("rank", [P, K, NG], F32)
    gm = m("gm", [P, K, NG], F32)
    pen = m("pen", [P, K, NG], F32)
    masked = r("masked", [P, K, E], F32)
    best = m("best", [P, K, TK], F32)
    rep = r("rep", [P, K, E], F32)
    wsel = r("wsel", [P, K, E], F32)
    wsum = m("wsum", [P, K], F32)
    wnorm = r("wnorm", [P, K, E], F32)

    g_bank, u_bank, y_bank, misc = psum[0:2], psum[2:5], psum[5:7], psum[7]
    wts_d = nc.dram_tensor("wts_scratch", (NCH, NEX, T), F32, kind="Internal").ap()
    wts_v = wts_d.rearrange("c (p two) t -> c two p t", two=2)
    x2_v = x2d.rearrange("(c k) t d -> c t k d", k=K)
    out_v = out.rearrange("(c k) t d -> c t k d", k=K)

    g_in = sem("gate_loaded")
    c_ok = sem("expert_consts")
    gw_mm, gw_ev = sem("gate_w_transposed"), sem("gate_wT_ready")
    cv_hi, cv_lo = sem("weights_hi"), sem("weights_lo")
    x2_in = [sem(f"x2_loaded{i}") for i in range(2)]
    st_ok, mv_ok, var_ok, rstd_ok, xn_ok = (sem(f"{n}_2") for n in ("ln_stats", "ln_mv", "ln_var", "ln_rstd", "xn"))
    xt_mm, xhi_ok, xT_ok, xlo_ok = sem("x2_transposed"), sem("xhi_ready"), sem("xT_ready"), sem("xlo_ready")
    lg_mm, sig_ok, rt, w_ok = sem("logits"), sem("sigmoids"), sem("route_step"), sem("route_weights")
    rd_ok = sem("route_denominators")
    wt_mm, wt_ev, wt_st = sem("weights_transposed"), sem("wT_ready"), sem("wT_stored")
    cw_in = [sem(f"cwb_loaded{i}") for i in range(2)]
    g_mm, u_mm, s_ok, a_ok, h_ok = (sem(n) for n in ("gate_mm", "up_mm", "silu_ready", "act_ready", "hid_ready"))
    hh_ok, hl_ok, dn_mm = sem("hid_hi"), sem("hid_lo"), sem("down_mm")
    y_ev, yt_mm, out_ok = sem("y_copied"), sem("y_transposed"), sem("out_ready")
    o_st = [sem(f"out_stored{i}") for i in range(2)]

    F_COPY, F_TURN, F_OUT, F_GROUP = LAG + 1, LAG + 2, LAG + 3, 4
    P_STAT, P_ROOT, P_NORM, P_TURN, P_OPER, P_LOGIT, P_SIG, P_ROUTE, P_WT, P_WEV = 10, 10, 11, 12, 13, 14, 15, 16, 26, 27
    CONV = 3
    R_STEPS = 26

    block = ctx_.enter_context(nc.Block())

    def conv_slices():
        for s in range(CONV):
            e0, e1 = s * NEX // CONV, (s + 1) * NEX // CONV
            q0, q1 = s * NP // CONV, (s + 1) * NP // CONV
            yield wg_raw[:, e0:e1, :], [w[:, e0:e1, :] for w in wg]
            yield wu_raw[:, e0:e1, :], [w[:, e0:e1, :] for w in wu]
            yield wd_raw[:, q0:q1, :], [w[:, q0:q1, :] for w in wd]

    @block.sync
    def _(sp):
        def load_x2(c, c2, i):
            wait(sp, out_ok, c - 1)
            sp.dma_start(x2c[i][:], x2_v[c]).then_inc(x2_in[i], 16)

        def store_w(c):
            wait(sp, wt_ev, c + 1)
            sp.dma_start(wts_d[c], wT[:]).then_inc(wt_st, 16)
            wait(sp, wt_st, 16 * c + 16)

        def load_cwb(c, gr, slot):
            wait(sp, h_ok, NP * c + GP * (gr - 1))
            for half in range(2):
                sp.dma_start(cwb[slot][half * F:(half + 1) * F, :, :],
                             wts_v[c][half][GP * gr:GP * (gr + 1)].unsqueeze(0).to_broadcast([F, GP, T])
                             ).then_inc(cw_in[slot], 16)

        def store_out(c, i):
            wait(sp, out_ok, c + 1)
            sp.dma_start(out_v[c], osb[i][:]).then_inc(o_st[i], 16)

        sp.dma_start(gw_in[:], v["gate_w"]).then_inc(g_in, 16)
        sp.dma_start(gbias[:], v["gate_bias"].rearrange("(a n) -> a n", a=1).to_broadcast([P, E])).then_inc(g_in, 16)
        load_x2(0, 0, 0)
        store_w(0)
        sp.wait_ge(cv_lo, 3 * CONV)
        load_cwb(0, 0, 0)
        load_cwb(0, 1, 1)

        def body(g, last):
            for j in range(2):
                c = 2 * g + j
                first = isinstance(c, int) and c == 0
                more = not (last and j == 1)
                for gr in range(2, GROUPS):
                    load_cwb(c, gr, (GROUPS * j + gr) % 2)
                    if gr == F_GROUP:
                        if not first:
                            store_out(c - 1, 1 - j)
                        if more:
                            load_x2(c + 1, g + (j + 1) // 2, 1 - j)
                if more:
                    store_w(c + 1)
                    for gr in range(2):
                        load_cwb(c + 1, gr, (GROUPS * (j + 1) + gr) % 2)

        body(0, False)
        with sp.Fori(1, LOOPS - 1) as g:
            body(g, False)
        body(LOOPS - 1, True)
        store_out(NCH - 1, 1)
        for i in range(2):
            sp.wait_ge(o_st[i], 16 * (NCH // 2))

    @block.gpsimd
    def _(pool):
        pool.memset(mhalf[:], -0.5).then_inc(c_ok, 1)
        pool.wait_ge(c_ok, 1)
        pool.memset(wT[E:NEX, :], 1.0).then_inc(c_ok, 1)
        pool.wait_ge(c_ok, 2)
        pool.memset(tri[:], 1.0).then_inc(c_ok, 1)
        pool.wait_ge(c_ok, 3)
        pool.affine_select(out=tri[:], in_=tri[:], compare_op=ALU.is_gt, fill=0.0, base=0,
                           pattern=[[1, NG], [-1, NG]], channel_multiplier=0).then_inc(c_ok, 1)

        def root(c):
            wait(pool, var_ok, c + 1)
            pool.tensor_tensor(rstd[:], var[:], mhalf[:], ALU.pow).then_inc(rstd_ok, 1)

        def hidden(n, q, j, g):
            slot = (GROUPS * j + q // GP) % 2
            wait(pool, a_ok, n + 1)
            if q % GP == 0:
                wait(pool, cw_in[slot], 32 * (GROUPS * g + (GROUPS * j + q // GP) // 2 + 1))
            wait(pool, hl_ok, n + 1 - RS)
            k = (NP * j + q) % RS
            pool.tensor_tensor(h_buf[k][:], a_buf[k][:], cwb[slot][:, q % GP, :], ALU.mult).then_inc(h_ok, 1)

        root(0)
        pool.wait_ge(cv_lo, 3 * CONV)

        def body(g, last):
            for j in range(2):
                c = 2 * g + j
                for q in range(NP):
                    hidden(NP * c + q, q, j, g)
                    if q == P_ROOT and not (last and j == 1):
                        root(c + 1)

        body(0, False)
        with pool.Fori(1, LOOPS - 1) as g:
            body(g, False)
        body(LOOPS - 1, True)

    @block.scalar
    def _(act):
        def operands(c, i):
            wait(act, xt_mm, c + 1)
            wait(act, u_mm, NP * (c - 1))
            act.activation(xhi[i][:], misc[:], ACT.Copy).then_inc(xhi_ok, 1)
            wait(act, lg_mm, c)
            act.activation(xT[:], misc[:], ACT.Copy).then_inc(xT_ok, 1)

        def sigmoids(c):
            wait(act, lg_mm, c + 1)
            wait(act, w_ok, c)
            act.activation(sig[:].rearrange("p k e -> p (k e)"), misc[:, 0:K * E], ACT.Sigmoid).then_inc(sig_ok, 1)

        def evac_w(c):
            wait(act, wt_mm, c + 1)
            wait(act, wt_st, 16 * c)
            act.activation(wT[0:E, :], misc[0:E, :], ACT.Copy).then_inc(wt_ev, 1)

        def silu(n, k):
            wait(act, g_mm, n + 1)
            wait(act, a_ok, n + 1 - RS)
            act.activation(s_buf[k % RS][:], g_bank[k % 2][:], ACT.Silu).then_inc(s_ok, 1)

        def hid_hi(n, k):
            wait(act, h_ok, n + 1)
            wait(act, dn_mm, n + 1 - RH)
            act.activation(hhi[k % RH][:], h_buf[k % RS][:], ACT.Copy).then_inc(hh_ok, 1)

        def copy_y(c, i):
            wait(act, dn_mm, NP * (c + 1))
            wait(act, yt_mm, c)
            act.activation(ysb[:], y_bank[i][:], ACT.Copy).then_inc(y_ev, 1)

        act.wait_ge(gw_mm, 1)
        act.activation(gwT[:], misc[:, 0:E], ACT.Copy).then_inc(gw_ev, 1)
        act.wait_ge(w_zero, 3)
        for i, n in enumerate((2 * E // 16, 2, 3)):
            act.wait_ge(w_in[i], 16 * n)
        for s, (src, dst) in enumerate(conv_slices()):
            act.activation(dst[0], src, ACT.Copy).then_inc(cv_hi, 1)
            if s == 2:
                operands(0, 0)
            if s == 4:
                sigmoids(0)
        evac_w(0)
        act.wait_ge(cv_lo, 3 * CONV)

        def body(g, last):
            for j in range(2):
                c = 2 * g + j
                first = isinstance(c, int) and c == 0
                more = not (last and j == 1)
                for q in range(NP):
                    n, k = NP * c + q, NP * j + q
                    silu(n, k)
                    if not (first and q < 2):
                        hid_hi(n - 2, k - 2)
                    if q == F_COPY and not first:
                        copy_y(c - 1, 1 - j)
                    if more:
                        if q == P_OPER:
                            operands(c + 1, 1 - j)
                        if q == P_SIG:
                            sigmoids(c + 1)
                        if q == P_WEV:
                            evac_w(c + 1)

        body(0, False)
        with act.Fori(1, LOOPS - 1) as g:
            body(g, False)
        body(LOOPS - 1, True)
        for q in range(2):
            hid_hi(NP * NCH - 2 + q, 2 * NP - 2 + q)
        copy_y(NCH - 1, 1)

    @block.vector
    def _(dve):
        def norm_stats(c, c2, i):
            wait(dve, x2_in[i], 16 * (c2 + 1))
            for k in range(K):
                ins = nc.vector.bn_stats(stats[:, k, :], x2c[i][:, k, :])
            ins.then_inc(st_ok, 1)
            wait_tick(nc, st_ok, c + 1, tick)
            for k in range(K):
                ins = nc.vector.bn_aggr(mv[:, k, :], stats[:, k, :])
            ins.then_inc(mv_ok, 1)
            wait(dve, mv_ok, c + 1)
            nc.vector.tensor_scalar(var[:], mv[:, :, 1], EPS, None, ALU.add).then_inc(var_ok, 1)

        def norm(c, i):
            wait(dve, rstd_ok, c + 1)
            wait(dve, xt_mm, c)
            for k in range(K):
                ins = nc.vector.tensor_scalar(xn[:, k, :], x2c[i][:, k, :], mv[:, k, 0:1], rstd[:, k:k + 1],
                                              ALU.subtract, ALU.mult)
            ins.then_inc(xn_ok, 1)

        def oper_lo(c, i):
            wait(dve, xT_ok, c + 1)
            wait(dve, xhi_ok, c + 1)
            wait(dve, u_mm, NP * (c - 1))
            nc.vector.tensor_tensor(xlo[i][:], misc[:], xhi[i][:].bitcast(F32), ALU.subtract).then_inc(xlo_ok, 1)

        def route_groups(c, part):
            done = lambda k: wait(dve, rt, R_STEPS * c + k)
            tt = nc.vector.tensor_tensor
            if part == 0:
                wait(dve, sig_ok, c + 1)
                tt(sc[:], sig[:], gbias[:].unsqueeze(1).to_broadcast([P, K, E]), ALU.add).then_inc(rt, 1)
                s8 = sc[:].rearrange("p k (g e) -> p (k g) e", g=NG)
                done(1)
                tt(top_a[:], s8[:, :, 0:4], s8[:, :, 4:8], ALU.max).then_inc(rt, 1)
                tt(low_a[:], s8[:, :, 0:4], s8[:, :, 4:8], ALU.min).then_inc(rt, 1)
                done(3)
                tt(mid_b[:], top_a[:, :, 0:2], top_a[:, :, 2:4], ALU.min).then_inc(rt, 1)
                tt(top_b[:], top_a[:, :, 0:2], top_a[:, :, 2:4], ALU.max).then_inc(rt, 1)
                tt(low_b[:], low_a[:, :, 0:2], low_a[:, :, 2:4], ALU.max).then_inc(rt, 1)
                done(6)
                tt(low_b[:], low_b[:], mid_b[:], ALU.max).then_inc(rt, 1)
            if part == 1:
                tt(mid_c[:], top_b[:, :, 0:1], top_b[:, :, 1:2], ALU.min).then_inc(rt, 1)
                tt(top_c[:], top_b[:, :, 0:1], top_b[:, :, 1:2], ALU.max).then_inc(rt, 1)
                done(9)
                tt(low_c[:], low_b[:, :, 0:1], low_b[:, :, 1:2], ALU.max).then_inc(rt, 1)
                done(10)
                tt(low_c[:], low_c[:], mid_c[:], ALU.max).then_inc(rt, 1)
                done(11)
                tt(gs[:].rearrange("p k g -> p (k g)"), top_c[:, :, 0], low_c[:, :, 0], ALU.add).then_inc(rt, 1)
            if part == 2:
                done(12)
                other = gs[:].unsqueeze(2).to_broadcast([P, K, NG, NG])
                own = gs[:].unsqueeze(3).to_broadcast([P, K, NG, NG])
                tt(eq[:], other, own, ALU.is_equal).then_inc(rt, 1)
                tt(gt[:], other, own, ALU.is_gt).then_inc(rt, 1)
                done(14)
                tt(eq[:], eq[:], tri[:].unsqueeze(1).to_broadcast([P, K, NG, NG]), ALU.mult).then_inc(rt, 1)
            if part == 3:
                done(15)
                tt(gt[:], gt[:], eq[:], ALU.add).then_inc(rt, 1)
                done(16)
                nc.vector.tensor_reduce(rank[:], gt[:], AXX, ALU.add).then_inc(rt, 1)
                done(17)
                nc.vector.tensor_scalar(gm[:], rank[:], float(TG), None, ALU.is_lt).then_inc(rt, 1)
            if part == 4:
                done(18)
                nc.vector.tensor_scalar(pen[:], gm[:], -LOW, LOW, ALU.mult, ALU.add).then_inc(rt, 1)
                s8 = sc[:].rearrange("p k (g e) -> p (k g) e", g=NG)
                m8 = masked[:].rearrange("p k (g e) -> p (k g) e", g=NG)
                by_group = lambda t: t[:].rearrange("p k g -> p (k g)").unsqueeze(2).to_broadcast([P, K * NG, EPG])
                tt(m8, s8, by_group(gm), ALU.mult).then_inc(rt, 1)
                done(20)
                tt(m8, m8, by_group(pen), ALU.add).then_inc(rt, 1)

        def route_experts(c, part):
            done = lambda k: wait(dve, rt, R_STEPS * c + k)
            tt = nc.vector.tensor_tensor
            if part == 0:
                wait_tick(nc, rt, R_STEPS * c + 21, tick)
                for k in range(K):
                    ins = nc.vector.max(best[:, k, :], masked[:, k, :])
                ins.then_inc(rt, 1)
                wait_tick(nc, rt, R_STEPS * c + 22, tick)
                for k in range(K):
                    ins = nc.vector.match_replace(out=rep[:, k, :], in_to_replace=best[:, k, :],
                                                  in_values=masked[:, k, :], imm_value=LOWER)
                ins.then_inc(rt, 1)
            if part == 1:
                done(23)
                tt(wsel[:], rep[:], masked[:], ALU.not_equal).then_inc(rt, 1)
                done(24)
                tt(wsel[:], wsel[:], sig[:], ALU.mult).then_inc(rt, 1)
                done(25)
                nc.vector.tensor_reduce(wsum[:], wsel[:], AXX, ALU.add).then_inc(rt, 1)
            if part == 2:
                done(26)
                nc.vector.tensor_scalar(wsum[:], wsum[:], 1e-20, 1.0 / ROUTE_SCALE, ALU.add, ALU.mult).then_inc(rd_ok, 1)
                wait(dve, rd_ok, 2 * c + 1)
                nc.vector.reciprocal(wsum[:], wsum[:]).then_inc(rd_ok, 1)
                wait(dve, rd_ok, 2 * c + 2)
                wait(dve, wt_mm, c)
                tt(wnorm[:], wsel[:], wsum[:].unsqueeze(2).to_broadcast([P, K, E]), ALU.mult).then_inc(w_ok, 1)

        def act_up(n, k):
            wait(dve, s_ok, n + 1)
            wait(dve, u_mm, n + 1)
            wait(dve, h_ok, n + 1 - RS)
            nc.vector.tensor_tensor(a_buf[k % RS][:], s_buf[k % RS][:], u_bank[k % 3][:], ALU.mult).then_inc(a_ok, 1)

        def hid_lo(n, k):
            wait(dve, hh_ok, n + 1)
            nc.vector.tensor_tensor(hlo[k % RH][:], h_buf[k % RS][:], hhi[k % RH][:].bitcast(F32),
                                    ALU.subtract).then_inc(hl_ok, 1)

        def finish(c, c2, i):
            wait(dve, yt_mm, c + 1)
            wait(dve, o_st[i], 16 * c2)
            nc.vector.scalar_tensor_tensor(out=osb[i][:].rearrange("p k d -> p (k d)"), in0=misc[:],
                                           scalar=tg_f[:, 0:1], in1=x2c[i][:].rearrange("p k d -> p (k d)"),
                                           op0=ALU.mult, op1=ALU.add).then_inc(out_ok, 1)

        dve.wait_ge(c_ok, 4)
        dve.wait_ge(g_in, 32)
        norm_stats(0, 0, 0)
        norm(0, 0)
        for s, (src, dst) in enumerate(conv_slices()):
            wait(dve, cv_hi, s + 1)
            nc.vector.tensor_tensor(dst[1], src, dst[0].bitcast(F32), ALU.subtract).then_inc(cv_lo, 1)
            if s == 2:
                oper_lo(0, 0)
        for part in range(5):
            route_groups(0, part)
        for part in range(3):
            route_experts(0, part)

        def body(g, last):
            for j in range(2):
                c = 2 * g + j
                first = isinstance(c, int) and c == 0
                more = not (last and j == 1)
                for q in range(NP):
                    n, k = NP * c + q, NP * j + q
                    act_up(n, k)
                    if not (first and q < 2):
                        hid_lo(n - 2, k - 2)
                    if q == F_OUT and not first:
                        finish(c - 1, g - 1 + j, 1 - j)
                    if more:
                        if q == P_STAT:
                            norm_stats(c + 1, g + (j + 1) // 2, 1 - j)
                        if q == P_NORM:
                            norm(c + 1, 1 - j)
                        if q == P_OPER:
                            oper_lo(c + 1, 1 - j)
                        if P_ROUTE <= q < P_ROUTE + 5:
                            route_groups(c + 1, q - P_ROUTE)
                        if P_ROUTE + 5 <= q < P_ROUTE + 8:
                            route_experts(c + 1, q - P_ROUTE - 5)

        body(0, False)
        with dve.Fori(1, LOOPS - 1) as g:
            body(g, False)
        body(LOOPS - 1, True)
        for q in range(2):
            hid_lo(NP * NCH - 2 + q, 2 * NP - 2 + q)
        finish(NCH - 1, LOOPS - 1, 1)

    @block.tensor
    def _(pe):
        def turn_x(c):
            wait(pe, xn_ok, c + 1)
            for k in range(K):
                ins = nc.tensor.transpose(misc[:, k * P:(k + 1) * P], xn[:, k, :], ident[:])
            ins.then_inc(xt_mm, 1)

        def logits(c):
            wait(pe, xT_ok, c + 1)
            wait(pe, xlo_ok, c + 1)
            for k in range(K):
                ins = nc.tensor.matmul(misc[:, k * E:(k + 1) * E], xT[:, k * P:(k + 1) * P], gwT[:],
                                       start=True, stop=True)
            ins.then_inc(lg_mm, 1)

        def before_turn_w(c):
            wait(pe, sig_ok, c + 1)
            wait(pe, w_ok, c + 1)

        def turn_w(c):
            for k in range(K):
                ins = nc.tensor.transpose(misc[0:E, k * P:(k + 1) * P], wnorm[:, k, :], ident[:])
            ins.then_inc(wt_mm, 1)

        def turn_y(c):
            wait(pe, y_ev, c + 1)
            for k in range(K):
                ins = nc.tensor.transpose(misc[:, k * P:(k + 1) * P], ysb[:, k * P:(k + 1) * P], ident[:])
            ins.then_inc(yt_mm, 1)

        def three(bank, w, mh, ml, first, last):
            nc.tensor.matmul(bank, w[0], mh, start=first, stop=False)
            nc.tensor.matmul(bank, w[1], mh, start=False, stop=False)
            return nc.tensor.matmul(bank, w[0], ml, start=False, stop=last)

        def gate_up(n, k, q, i):
            pick = lambda w: [t[:, 2 * q:2 * q + 2, :].rearrange("p e f -> p (e f)") for t in w]
            wait(pe, s_ok, n - 1)
            three(g_bank[k % 2][:], pick(wg), xhi[i][:], xlo[i][:], True, True).then_inc(g_mm, 1)
            wait(pe, a_ok, n - 2)
            three(u_bank[k % 3][:], pick(wu), xhi[i][:], xlo[i][:], True, True).then_inc(u_mm, 1)

        def down(n, k, q, i):
            wait(pe, hl_ok, n + 1)
            three(y_bank[i][:], [w[:, q, :] for w in wd], hhi[k % RH][:], hlo[k % RH][:],
                  q == 0, q == NP - 1).then_inc(dn_mm, 1)

        pe.wait_ge(g_in, 32)
        nc.tensor.transpose(misc[:, 0:E], gw_in[:], ident[0:E, 0:E]).then_inc(gw_mm, 1)
        pe.wait_ge(gw_ev, 1)
        turn_x(0)
        logits(0)
        before_turn_w(0)
        turn_w(0)
        pe.wait_ge(cv_lo, 3 * CONV)

        def body(g, last):
            for j in range(2):
                c = 2 * g + j
                first = isinstance(c, int) and c == 0
                more = not (last and j == 1)
                for q in range(NP):
                    n, k = NP * c + q, NP * j + q
                    if q == P_WT and more:
                        before_turn_w(c + 1)
                    gate_up(n, k, q, j)
                    if q >= LAG:
                        if q == LAG:
                            wait(pe, y_ev, c - 1)
                        down(n - LAG, k - LAG, q - LAG, j)
                    elif not first:
                        down(n - LAG, k - LAG, q - LAG + NP, 1 - j)
                    if q == F_TURN and not first:
                        turn_y(c - 1)
                    if more:
                        if q == P_TURN:
                            wait(pe, out_ok, c)
                            turn_x(c + 1)
                        if q == P_LOGIT:
                            logits(c + 1)
                        if q == P_WT:
                            turn_w(c + 1)

        body(0, False)
        with pe.Fori(1, LOOPS - 1) as g:
            body(g, False)
        body(LOOPS - 1, True)
        for q in range(LAG):
            down(NP * NCH - LAG + q, 2 * NP - LAG + q, NP - LAG + q, 1)
        turn_y(NCH - 1)


_INS = ['x', 'ctx_1024', 'g_xattn', 'g_ffn', 'L0_xattn_Wqkv', 'L0_xattn_bqkv', 'L0_xattn_Wqkv_aux',
        'L0_xattn_bqkv_aux', 'L0_xattn_Wo', 'L0_xattn_bo', 'L0_xattn_g', 'L0_ffn_gate_w', 'L0_ffn_gate_bias',
        'L0_ffn_We_gate', 'L0_ffn_We_up', 'L0_ffn_We_down', 'L0_ffn_Ws_gate', 'L0_ffn_Ws_up', 'L0_ffn_Ws_down']
_OUTS = [((32, 128, 128), 'float32')]


def kernel(**inputs):
    import numpy as _np
    import concourse.bacc as _bacc
    from concourse import mybir as _mybir
    from concourse.bass_utils import run_bass_kernel_spmd as _run

    nc = _bacc.Bacc("TRN2", target_bir_lowering=False, num_devices=1)
    arrays, args = {}, []
    for name in _INS:
        a = _np.ascontiguousarray(inputs[name])
        arrays[f"in_{name}_dram"] = a
        args.append(nc.dram_tensor(f"in_{name}_dram", a.shape, _mybir.dt.from_np(a.dtype), kind="ExternalInput").ap())
    for i, (shape, dtype) in enumerate(_OUTS):
        dt = _mybir.dt.from_np(_np.dtype(dtype))
        args.append(nc.dram_tensor(f"out_{i}_dram", shape, dt, kind="ExternalOutput").ap())
    build(nc, *args)
    r = _run(nc, [arrays], core_ids=[0])
    got = tuple(r.results[0][f"out_{i}_dram"] for i in range(len(_OUTS)))
    return got[0]
```

```python
from contextlib import ExitStack

import concourse.bass as bass
from concourse import mybir

F32 = mybir.dt.float32
F32R = mybir.dt.float32r
BF16 = mybir.dt.bfloat16
FP16 = mybir.dt.float16
ALU = mybir.AluOpType
ACT = mybir.ActivationFunctionType
AXX = mybir.AxisListType.X

P = 128
H, DH = 16, 8
PART = 3
Q_SLOTS = (0, 0, 0, 1, 1, 2)
K_SLOTS = (0, 1, 2, 0, 1, 0)
ROWS = len(Q_SLOTS) * DH
SHIFT = 96
ROWS_S, ROWS_ST = SHIFT, SHIFT + 4
VC = PART * DH + 1
EPS = 1e-5
HPU = 4
UNITS = 2 * H // HPU
E, F = 64, 64
NG, TG, TK = 8, 4, 8
ROUTE_SCALE = 2.5
LOW, LOWER = -3.0e38, -3.4e38


class Map:

    def __init__(self, nc, base, end):
        self.nc, self.at, self.end = nc, base, end

    def __call__(self, name, shape, dt):
        size = {F32: 4, F32R: 4, BF16: 2, FP16: 2}[dt]
        for n in shape[1:]:
            size *= n
        t = self.nc.alloc_sbuf_tensor_at(name, shape, dt, offset=self.at)
        self.at += (size + 31) // 32 * 32
        assert self.at <= self.end, (name, self.at, self.end)
        return t


def wait(eng, sem, value):
    if isinstance(value, int) and value <= 0:
        return
    eng.wait_ge(sem, value)


def wait_tick(nc, sem, value, tick):
    wait(nc.vector, sem, value)
    if not isinstance(value, int):
        nc.vector.tensor_copy(tick[0:1, 1:2], tick[0:1, 0:1])


def build(nc, x, ctx, g_xattn, g_ffn, Wqkv, bqkv, Wqkv_aux, bqkv_aux, Wo, bo, g_head,
          gate_w, gate_bias, We_gate, We_up, We_down, Ws_gate, Ws_up, Ws_down, out):
    NB = x.shape[0]
    CH = 2
    TC = CH * P
    base = (nc.sbuf_base + 63) // 64 * 64
    end = nc.sbuf_usable_end

    x2d = nc.dram_tensor("x2_scratch", (NB, P, P), F32, kind="Internal").ap()
    parts_d = nc.dram_tensor("parts_scratch", (NB // CH, 3 * PART, P, TC), BF16, kind="Internal").ap()

    with ExitStack() as ctx_:
        psum = [ctx_.enter_context(nc.psum_tensor(f"bank{i}", [P, 512], F32)) for i in range(8)]
        names = {}

        def sem(name):
            names[name] = ctx_.enter_context(nc.semaphore(name))
            return names[name]

        keep = Map(nc, base, end)
        ident = keep("ident", [P, P], F32)
        tick = keep("tick", [P, 2], F32)
        ident_bf = keep("ident_bf", [P, P], BF16)
        tg_x = keep("tg_x", [P, 1], F32)
        tg_f = keep("tg_f", [P, 1], F32)
        NEX = E + 2
        NP = NEX // 2
        raw_base = (end - (2 * NEX * F + NP * P) * 4) // 32 * 32
        raw = Map(nc, raw_base, end)
        wg_raw = raw("wg_raw", [P, NEX, F], F32)
        wu_raw = raw("wu_raw", [P, NEX, F], F32)
        wd_raw = raw("wd_raw", [P, NP, P], F32)
        w_in = [sem(f"w_in{i}") for i in range(3)]
        w_zero = sem("w_zero")

        v = dict(locals())
        with ExitStack() as stage:
            attention(nc, stage, sem, Map(nc, keep.at, raw_base), psum, v)
        with ExitStack() as stage:
            experts(nc, stage, sem, Map(nc, keep.at, raw_base), Map(nc, raw_base, end), psum, v)


def attention(nc, ctx_, sem, m, psum, v):
    x, ctx, x2d, parts_d = v["x"], v["ctx"], v["x2d"], v["parts_d"]
    tick = v["tick"]
    ident, ident_bf, tg_x, tg_f = v["ident"], v["ident_bf"], v["tg_x"], v["tg_f"]
    wg_raw, wu_raw, wd_raw, w_in, w_zero = v["wg_raw"], v["wu_raw"], v["wd_raw"], v["w_in"], v["w_zero"]
    NB, CH, TC = v["NB"], v["CH"], v["TC"]
    NC = NB // CH
    BODY = 2 * CH
    LOOPS = NB // BODY

    stack = [[m(f"stack_{o}{i}", [P, H, TC], BF16) for o in ("q", "k", "ka")] for i in range(2)]
    kones = m("kones", [P, 2], BF16)
    xin = [m(f"xin{i}", [P, CH, P], F32) for i in range(2)]
    cin = [m(f"cin{i}", [P, CH, P], F32) for i in range(2)]
    xres = [m(f"xres{i}", [P, CH, P], F32) for i in range(2)]
    x2 = [m(f"x2_{i}", [P, CH, P], F32) for i in range(2)]
    stats = m("stats", [P, CH, 6], F32)
    mv = m("mv", [P, CH, 2], F32)
    var = m("var", [P, CH], F32)
    rstd = m("rstd", [P, CH], F32)
    mhalf = m("mhalf", [P, CH], F32)
    xn = m("xn", [P, CH, P], F32)
    xcT = [m(f"xcT{i}", [P, 2, TC], F32) for i in range(2)]
    parts = [m(f"parts{i}", [P, 3, PART, TC], BF16) for i in range(2)]
    rest = m("rest", [P, 3, TC], F32)
    vrest = m("vrest", [P, 2 * CH, P], F32)
    V = [m(f"V{i}", [P, 2 * CH, H, VC], BF16) for i in range(2)]
    RP = 8
    LOW_U = 5
    LAG = 4
    p_hi = [m(f"p_hi{i}", [P, HPU * P], FP16) for i in range(RP)]
    p_all = [m(f"p_all{i}", [P, HPU * P], F32) for i in range(RP)]
    p_lo = [m(f"p_lo{i}", [P, HPU * P], FP16) for i in range(RP)]
    mx = [m(f"mx{i}", [P, 2, H], F32) for i in range(2)]
    nmax = m("nmax", [P, 4, 2, H], BF16)
    nmaxT = m("nmaxT", [4 * H, P], BF16)
    osum = m("osum", [P, 2, H, DH], F32)
    rden = m("rden", [P, 2, H], F32)
    rgate = m("rgate", [P, 2, H], F32)
    onorm = m("onorm", [P, 2, H, DH], F32)
    att = m("att", [P, P], F32)
    attT = m("attT", [P, P], F32)
    wqkv = m("wqkv", [P, 3, P], F32)
    wqkva = m("wqkva", [P, 3, P], F32)
    wqk = m("wqk", [P, 3, P], F32)
    wo = m("wo", [P, P], F32)
    bcol = m("bcol", [P, 5], F32)
    bo_row = m("bo_row", [1, P], F32)
    ones = m("ones", [P, P], F32)
    gh = m("gh", [P, H], F32)
    ghc = m("ghc", [P, 1], F32)
    gcoef = m("gcoef", [P, 2, H], F32)
    gcol = m("gcol", [P, 2], F32)
    bvcol = m("bvcol", [P, 1], F32)
    tmpc = m("tmpc", [P, 4 + H], F32)
    scale = float(DH) ** -0.5

    s_bank, st_bank, o_bank, misc = psum[0:2], psum[2:4], psum[4:6], psum[6:8]

    c_in = sem("consts_loaded")
    ident_ok = sem("ident_ready")
    ident_step = sem("ident_step")
    kones_ok = sem("kones_ready")
    const_ok, tanh_ok = sem("consts_ready"), sem("tanh_ready")
    cstep_a, cstep_v = sem("const_step_act"), sem("const_step_dve")
    wqk_ok = sem("wqk_reordered")
    stack_zero = sem("stacks_zeroed")
    x_in = [sem(f"x_in{i}") for i in range(2)]
    xr_in = [sem(f"xres_in{i}") for i in range(2)]
    stats_ok, mv_ok, var_ok, rstd_ok, xn_ok = (sem(n) for n in ("ln_stats", "ln_mv", "ln_var", "ln_rstd", "xn_ready"))
    t_mm, t_ev = sem("transposes_done"), sem("xcT_ready")
    qk_mm, ka_mm, v_mm = sem("qk_projected"), sem("ka_projected"), sem("v_projected")
    qk_hi, ka_hi, v_hi = sem("qk_hi"), sem("ka_hi"), sem("v_hi")
    qk_rest, ka_rest, v_rest = sem("qk_rest"), sem("ka_rest"), sem("v_rest")
    mid_ok, lo_ok, v_mid, v_ok = sem("mid_ready"), sem("lo_ready"), sem("v_mid"), sem("v_ready")
    scr = [sem(f"parts_stored{i}") for i in range(2)]
    stk = [sem(f"stack_loaded{i}") for i in range(2)]
    s_mm, mx_ok = sem("scores_for_max"), sem("max_taken")
    nm_hi, nm_ok, nm_mm, nm_ev = sem("nmax_hi"), sem("nmax_ready"), sem("nmax_transposed"), sem("nmaxT_ready")
    shift = sem("shift_rows_loaded")
    st_mm, ph_ok, pa_ok, pl_ok = sem("shifted_scores"), sem("p_hi_ready"), sem("p_ready"), sem("p_lo_ready")
    pv_ok, pd_ok = sem("pv_done"), sem("p_lo_by_dve")
    o_sum, o_red = sem("o_summed"), sem("o_reduced")
    rg_ok, on_ok, at_ok = sem("rgate_ready"), sem("onorm_ready"), sem("att_ready")
    at_mm, at_ev, wo_mm = sem("att_transposed"), sem("attT_ready"), sem("wo_done")
    x2_ok = sem("x2_ready")
    x2_st = [sem(f"x2_stored{i}") for i in range(2)]

    x_v = x.rearrange("(n k) t d -> n t k d", k=CH)
    c_v = ctx.rearrange("(n k) t d -> n t k d", k=CH)
    x2_v = x2d.rearrange("(n k) t d -> n t k d", k=CH)
    parts_v = parts_d.rearrange("n a (d h) t -> n a d (h t)", d=DH)
    CONSTS = 13
    q_runs = ((0, (0, 0, 0)), (3, (1, 1)), (5, (2,)))
    k_runs = ((0, (0, 1, 2)), (3, (0, 1)), (5, (0,)))

    block = ctx_.enter_context(nc.Block())

    def const_loads(eng):
        one = lambda a: a.rearrange("(a n) -> a n", a=1)
        col = lambda a: a.rearrange("(n a) -> n a", a=1)
        turned = lambda a: a.rearrange("(h d a) -> d h a", d=DH, a=1)
        eng.dma_start(wqkv[:], v["Wqkv"].rearrange("d (o n) -> d o n", o=3)).then_inc(c_in, 16)
        eng.dma_start(wqkva[:], v["Wqkv_aux"].rearrange("d (o n) -> d o n", o=3)).then_inc(c_in, 16)
        eng.dma_start(wo[:], v["Wo"]).then_inc(c_in, 16)
        for i, b in enumerate((turned(v["bqkv"][0:P]), turned(v["bqkv"][P:2 * P]), col(v["bqkv"][2 * P:3 * P]),
                               turned(v["bqkv_aux"][P:2 * P]), col(v["bqkv_aux"][2 * P:3 * P]))):
            eng.dma_start(bcol[:, i:i + 1], b, allow_slow_non_contiguous=True).then_inc(c_in, 16)
        eng.dma_start(bo_row[:], one(v["bo"])).then_inc(c_in, 16)
        eng.dma_start(gh[:], one(v["g_head"]).to_broadcast([P, H])).then_inc(c_in, 16)
        eng.dma_start(ghc[:].rearrange("p a -> p a"),
                      v["g_head"].rearrange("(h a b) -> h a b", a=1, b=1).to_broadcast([H, DH, 1])).then_inc(c_in, 16)
        eng.dma_start(tg_x[:], one(v["g_xattn"]).to_broadcast([P, 1])).then_inc(c_in, 16)
        eng.dma_start(tg_f[:], one(v["g_ffn"]).to_broadcast([P, 1])).then_inc(c_in, 16)

    @block.sync
    def _(sp):
        def load_x(n, i):
            wait(sp, t_ev, n - 1)
            sp.dma_start(xin[i][:], x_v[n]).then_inc(x_in[i], 16)
            sp.dma_start(cin[i][:], c_v[n]).then_inc(x_in[i], 16)

        def load_res(n, i):
            wait(sp, x2_ok, CH * (n - 1))
            sp.dma_start(xres[i][:], x_v[n]).then_inc(xr_in[i], 16)

        def store_parts(n, n2, i):
            wait(sp, lo_ok, n + 1)
            sp.dma_start(parts_d[n].rearrange("a p t -> p a t"),
                         parts[i][:].rearrange("p o a t -> p (o a) t")).then_inc(scr[i], 16)

        def load_stack(n, n2, i):
            wait(sp, st_mm, UNITS * CH * (n - 1))
            wait(sp, scr[i], 16 * (n2 + 1))
            for o in range(3):
                for slot, run in (k_runs if o else q_runs):
                    src = parts_v[n][o * PART + run[0]]
                    if o == 0:
                        src = src.unsqueeze(0).to_broadcast([len(run), DH, H * TC])
                    else:
                        src = parts_v[n][o * PART + run[0]:o * PART + run[0] + len(run)]
                    sp.dma_start(stack[i][o][slot * DH:(slot + len(run)) * DH, :, :].rearrange("p h t -> p (h t)"),
                                 src).then_inc(stk[i], 16)

        def shift_rows(b, k):
            wait(sp, nm_ev, b + 1)
            sp.dma_start(stack[k // CH][0][SHIFT:SHIFT + 4, :, (k % CH) * P:(k % CH + 1) * P],
                         nmaxT[:]).then_inc(shift, 16)

        def store_x2(n, i):
            wait(sp, x2_ok, CH * (n + 1))
            sp.dma_start(x2_v[n], x2[i][:]).then_inc(x2_st[i], 16)

        load_x(0, 0)
        const_loads(sp)
        load_x(1, 1)
        load_res(0, 0)
        load_res(1, 1)
        store_parts(0, 0, 0)
        sp.wait_ge(stack_zero, 1)
        load_stack(0, 0, 0)
        store_parts(1, 0, 1)
        shift_rows(0, 0)

        def body(g, last):
            for j in range(2):
                n, i = 2 * g + j, j
                first = isinstance(n, int) and n == 0
                more, more2 = not (last and j == 1), not last
                if more2:
                    load_x(n + 2, i)
                if more:
                    load_stack(n + 1, g + (j + 1) // 2, 1 - j)
                shift_rows(2 * n + 1, 2 * i + 1)
                if not first:
                    store_x2(n - 1, 1 - j)
                    if more:
                        load_res(n + 1, 1 - j)
                if more2:
                    store_parts(n + 2, g + 1, i)
                if more:
                    shift_rows(2 * n + 2, (2 * i + 2) % BODY)

        body(0, False)
        with sp.Fori(1, LOOPS - 1) as g:
            body(g, False)
        body(LOOPS - 1, True)
        store_x2(NC - 1, 1)
        for i in range(2):
            sp.wait_ge(x2_st[i], 16 * (NC // 2))

    @block.gpsimd
    def _(pool):
        pool.memset(ident[:], 0.0).then_inc(ident_step, 1)
        pool.wait_ge(ident_step, 1)
        pool.affine_select(out=ident[:], in_=ident[:], compare_op=ALU.not_equal, fill=1.0, base=0,
                           pattern=[[-1, P]], channel_multiplier=1).then_inc(ident_step, 1)
        pool.wait_ge(ident_step, 2)
        pool.tensor_copy(ident_bf[:], ident[:]).then_inc(ident_ok, 1)
        pool.memset(kones[:], 1.0).then_inc(kones_ok, 1)
        pool.memset(mhalf[:], -0.5).then_inc(kones_ok, 1)
        pool.wait_ge(kones_ok, 2)
        pool.affine_select(out=kones[:, 0:1], in_=kones[:, 0:1], compare_op=ALU.is_ge, fill=0.0,
                           base=SHIFT + 1, pattern=[[0, 1]], channel_multiplier=-1).then_inc(kones_ok, 1)
        pool.affine_select(out=kones[:, 1:2], in_=kones[:, 1:2], compare_op=ALU.is_ge, fill=0.0,
                           base=-SHIFT - 2, pattern=[[0, 1]], channel_multiplier=1).then_inc(kones_ok, 1)
        for t in (V[0], V[1], ones):
            pool.memset(t[:], 1.0).then_inc(kones_ok, 1)
        pool.memset(wg_raw[:, E + 1, :], 0.0).then_inc(w_zero, 1)
        pool.memset(wu_raw[:, E + 1, :], 0.0).then_inc(w_zero, 1)
        pool.wait_ge(kones_ok, 7)
        pool.wait_ge(w_zero, 2)
        pool.memset(wd_raw[F:P, (E + 1) // 2, :], 0.0).then_inc(w_zero, 1)
        pool.wait_ge(w_zero, 3)
        for e0 in range(0, E, 16):
            for w, d in ((wg_raw, v["We_gate"]), (wu_raw, v["We_up"])):
                pool.dma_start(w[:, e0:e0 + 16, :], d[e0:e0 + 16].rearrange("e d f -> d e f")).then_inc(w_in[0], 16)
        pool.dma_start(wg_raw[:, E, :], v["Ws_gate"]).then_inc(w_in[1], 16)
        pool.dma_start(wu_raw[:, E, :], v["Ws_up"]).then_inc(w_in[1], 16)
        wd_v = v["We_down"].rearrange("(p two) f d -> two f p d", two=2)
        for half in range(2):
            pool.dma_start(wd_raw[half * F:(half + 1) * F, 0:E // 2, :], wd_v[half]).then_inc(w_in[2], 16)
        pool.dma_start(wd_raw[0:F, E // 2, :], v["Ws_down"]).then_inc(w_in[2], 16)

        def root(n):
            wait(pool, var_ok, n + 1)
            pool.tensor_tensor(rstd[:], var[:], mhalf[:], ALU.pow).then_inc(rstd_ok, 1)

        def low_part(b, u):
            wait(pool, pa_ok, UNITS * b + u + 1)
            wait(pool, pv_ok, UNITS * b + u + 1 - RP)
            pool.tensor_tensor(p_lo[u % RP][:], p_all[u % RP][:], p_hi[u % RP][:], ALU.subtract).then_inc(pl_ok, 1)

        def normalise(b):
            wait(pool, rg_ok, b + 1)
            pool.tensor_tensor(onorm[:], osum[:], rgate[:].unsqueeze(3).to_broadcast([P, 2, H, DH]),
                               ALU.mult).then_inc(on_ok, 1)
            wait(pool, on_ok, b + 1)
            wait(pool, at_mm, b)
            pool.tensor_tensor(att[:].rearrange("p (h d) -> p h d", h=H), onorm[:, 0], onorm[:, 1],
                               ALU.add).then_inc(at_ok, 1)

        root(0)
        root(1)

        def body(g, last):
            for k in range(BODY):
                b, n, i = BODY * g + k, 2 * g + k // CH, k // CH
                first = isinstance(b, int) and b == 0
                odd = k % CH
                for u in range(UNITS):
                    if u != LOW_U:
                        low_part(b, u)
                    if u == 1 and not odd and not last:
                        root(n + 2)
                    if u == LAG + 1 and not first:
                        normalise(b - 1)

        body(0, False)
        with pool.Fori(1, LOOPS - 1) as g:
            body(g, False)
        body(LOOPS - 1, True)
        normalise(NB - 1)

    @block.scalar
    def _(act):
        act.wait_ge(c_in, 16 * CONSTS)
        act.activation(tmpc[:, 0:H], gh[:], ACT.Exp, scale=-1.0).then_inc(cstep_a, 1)
        act.activation(tmpc[:, H:H + 1], ghc[:], ACT.Exp, scale=-1.0).then_inc(cstep_a, 1)
        act.activation(tg_x[:], tg_x[:], ACT.Tanh).then_inc(tanh_ok, 1)
        act.activation(tg_f[:], tg_f[:], ACT.Tanh).then_inc(tanh_ok, 1)

        by_width = lambda w: w.rearrange("p (h d) -> p d h", h=H)
        out_by_width = lambda w: w.rearrange("p (d h) -> p d h", h=H)
        act.activation(out_by_width(wqk[:, 0, :]), by_width(wqkv[:, 0, :]), ACT.Copy).then_inc(wqk_ok, 1)
        act.activation(out_by_width(wqk[:, 1, :]), by_width(wqkv[:, 1, :]), ACT.Copy).then_inc(wqk_ok, 1)
        act.activation(out_by_width(wqk[:, 2, :]), by_width(wqkva[:, 1, :]), ACT.Copy).then_inc(wqk_ok, 1)

        def evac_t(n, i):
            wait(act, t_mm, n + 1)
            act.activation(xcT[i][:].rearrange("p a t -> p (a t)"), misc[0][:], ACT.Copy).then_inc(t_ev, 1)

        def hi_qk(n, n2, i):
            wait(act, qk_mm, n + 1)
            wait(act, scr[i], 16 * n2)
            for o in range(2):
                ins = act.activation(parts[i][:, o, 0, :], misc[0][:, o * TC:(o + 1) * TC], ACT.Identity,
                                     bias=bcol[:, o:o + 1])
            ins.then_inc(qk_hi, 1)

        def hi_ka(n, i):
            wait(act, ka_mm, n + 1)
            act.activation(parts[i][:, 2, 0, :], misc[0][:, 0:TC], ACT.Identity, bias=bcol[:, 3:4]).then_inc(ka_hi, 1)

        def mid(n, i):
            wait(act, ka_rest, n + 1)
            act.activation(parts[i][:, :, 1, :], rest[:], ACT.Copy).then_inc(mid_ok, 1)

        def hi_v(n, i):
            wait(act, v_mm, n + 1)
            act.activation(V[i][:, :, :, 0:DH], misc[0][:].rearrange("p (a h d) -> p a h d", h=H, d=DH),
                           ACT.Copy).then_inc(v_hi, 1)

        def mid_v(n, i):
            wait(act, v_rest, n + 1)
            act.activation(V[i][:, :, :, DH:2 * DH], vrest[:].rearrange("p a (h d) -> p a h d", d=DH),
                           ACT.Copy).then_inc(v_mid, 1)

        def exps(b, u):
            wait(act, st_mm, UNITS * b + u + 1)
            wait(act, pv_ok, UNITS * b + u + 1 - RP)
            act.activation(p_hi[u % RP][:], st_bank[u % 2][:], ACT.Exp, scale=scale).then_inc(ph_ok, 1)
            act.activation(p_all[u % RP][:], st_bank[u % 2][:], ACT.Exp, scale=scale).then_inc(pa_ok, 1)

        def evac_att(b):
            wait(act, at_mm, b + 1)
            wait(act, wo_mm, b)
            act.activation(attT[:], misc[1][:, 0:P], ACT.Identity, bias=bvcol[:, 0:1]).then_inc(at_ev, 1)

        act.wait_ge(kones_ok, 6)
        for n in range(2):
            evac_t(n, n)
            hi_qk(n, 0, n)
            hi_ka(n, n)
            mid(n, n)
            if n == 0:
                hi_v(0, 0)
                mid_v(0, 0)
        act.wait_ge(const_ok, 1)

        def body(g, last):
            for k in range(BODY):
                b, n, i, odd = BODY * g + k, 2 * g + k // CH, k // CH, k % CH
                first = isinstance(b, int) and b == 0
                more = not (last and i == 1)
                for u in range(UNITS):
                    exps(b, u)
                    if not last:
                        if u == 3 and not odd:
                            evac_t(n + 2, i)
                        if u == 6 and not odd:
                            hi_qk(n + 2, g + 1, i)
                        if u == 0 and odd:
                            hi_ka(n + 2, i)
                        if u == 2 and odd:
                            mid(n + 2, i)
                    if u == 4 and odd and more:
                        hi_v(n + 1, (i + 1) % 2)
                    if u == 6 and odd and more:
                        mid_v(n + 1, (i + 1) % 2)
                    if u == 7 and not first:
                        evac_att(b - 1)

        body(0, False)
        with act.Fori(1, LOOPS - 1) as g:
            body(g, False)
        body(LOOPS - 1, True)
        evac_att(NB - 1)

    @block.vector
    def _(dve):
        for o in range(3):
            for i in range(2):
                nc.vector.memset(stack[i][o][:], 0.0)
        dve.wait_ge(kones_ok, 4)
        nc.vector.memset(nmax[:], 0.0)
        nc.vector.memset(tick[:], 0.0)
        ins = nc.vector.memset(mx[0][:], 0.0)
        ins.then_inc(cstep_v, 1)
        dve.wait_ge(cstep_v, 1)
        for i in range(2):
            for o in (1, 2):
                ins = nc.vector.tensor_copy(stack[i][o][SHIFT:SHIFT + 4, :, :].rearrange("p h t -> p (h t)"),
                                            kones[SHIFT:SHIFT + 4, o - 1:o].to_broadcast([4, H * TC]))
        ins.then_inc(stack_zero, 1)

        dve.wait_ge(cstep_a, 2)
        nc.vector.tensor_scalar(tmpc[:, 0:H + 1], tmpc[:, 0:H + 1], 1.0, None, ALU.add).then_inc(cstep_v, 1)
        dve.wait_ge(cstep_v, 2)
        nc.vector.reciprocal(gcoef[:, 1, :], tmpc[:, 0:H]).then_inc(cstep_v, 1)
        nc.vector.reciprocal(gcol[:, 0:1], tmpc[:, H:H + 1]).then_inc(cstep_v, 1)
        dve.wait_ge(cstep_v, 4)
        nc.vector.tensor_scalar(gcoef[:, 0, :], gcoef[:, 1, :], -1.0, 1.0, ALU.mult, ALU.add).then_inc(cstep_v, 1)
        nc.vector.tensor_scalar(gcol[:, 1:2], gcol[:, 0:1], -1.0, 1.0, ALU.mult, ALU.add).then_inc(cstep_v, 1)
        dve.wait_ge(cstep_v, 6)
        nc.vector.tensor_scalar(bvcol[:], bcol[:, 4:5], gcol[:, 0:1], None, ALU.mult).then_inc(cstep_v, 1)
        dve.wait_ge(cstep_v, 7)
        nc.vector.scalar_tensor_tensor(out=bvcol[:], in0=bcol[:, 2:3], scalar=gcol[:, 1:2], in1=bvcol[:],
                                       op0=ALU.mult, op1=ALU.add).then_inc(const_ok, 1)

        def norm_stats(n, n2, i):
            wait(dve, x_in[i], 32 * (n2 + 1))
            for c in range(CH):
                ins = nc.vector.bn_stats(stats[:, c, :], xin[i][:, c, :])
            ins.then_inc(stats_ok, 1)
            wait_tick(nc, stats_ok, n + 1, tick)
            for c in range(CH):
                ins = nc.vector.bn_aggr(mv[:, c, :], stats[:, c, :])
            ins.then_inc(mv_ok, 1)
            wait(dve, mv_ok, n + 1)
            nc.vector.tensor_scalar(var[:], mv[:, :, 1], EPS, None, ALU.add).then_inc(var_ok, 1)

        def norm(n, i):
            wait(dve, rstd_ok, n + 1)
            wait(dve, t_mm, n)
            for c in range(CH):
                ins = nc.vector.tensor_scalar(xn[:, c, :], xin[i][:, c, :], mv[:, c, 0:1], rstd[:, c:c + 1],
                                              ALU.subtract, ALU.mult)
            ins.then_inc(xn_ok, 1)

        def rest_qk(n, i):
            wait(dve, qk_hi, n + 1)
            wait(dve, lo_ok, n)
            wait(dve, mid_ok, n)
            for o in range(2):
                ins = nc.vector.scalar_tensor_tensor(
                    out=rest[:, o, :], in0=misc[0][:, o * TC:(o + 1) * TC], scalar=bcol[:, o:o + 1],
                    in1=parts[i][:, o, 0, :], op0=ALU.add, op1=ALU.subtract)
            ins.then_inc(qk_rest, 1)

        def rest_ka(n, i):
            wait(dve, ka_hi, n + 1)
            nc.vector.scalar_tensor_tensor(
                out=rest[:, 2, :], in0=misc[0][:, 0:TC], scalar=bcol[:, 3:4],
                in1=parts[i][:, 2, 0, :], op0=ALU.add, op1=ALU.subtract).then_inc(ka_rest, 1)

        def low(n, i):
            wait(dve, mid_ok, n + 1)
            wait(dve, ka_rest, n + 1)
            nc.vector.tensor_tensor(parts[i][:, :, 2, :], rest[:], parts[i][:, :, 1, :],
                                    ALU.subtract).then_inc(lo_ok, 1)

        def rest_v(n, i):
            wait(dve, v_hi, n + 1)
            nc.vector.tensor_tensor(vrest[:].rearrange("p a (h d) -> p (a h) d", d=DH),
                                    misc[0][:].rearrange("p (a h d) -> p (a h) d", h=H, d=DH),
                                    V[i][:, :, :, 0:DH].rearrange("p a h d -> p (a h) d"),
                                    ALU.subtract).then_inc(v_rest, 1)

        def low_v(n, i):
            wait(dve, v_mid, n + 1)
            wait(dve, v_rest, n + 1)
            nc.vector.tensor_tensor(V[i][:, :, :, 2 * DH:3 * DH].rearrange("p a h d -> p (a h) d"),
                                    vrest[:].rearrange("p a (h d) -> p (a h) d", d=DH),
                                    V[i][:, :, :, DH:2 * DH].rearrange("p a h d -> p (a h) d"),
                                    ALU.subtract).then_inc(v_ok, 1)

        def maxima(b, par, u):
            wait(dve, s_mm, UNITS * b + u + 1)
            if u == 0:
                wait(dve, nm_ok, b - 1)
            a, h0 = u // (UNITS // 2), (u % (UNITS // 2)) * HPU
            nc.vector.tensor_reduce(mx[par][:, a, h0:h0 + HPU], s_bank[u % 2][:].rearrange("p (h k) -> p h k", h=HPU),
                                    AXX, ALU.max).then_inc(mx_ok, 1)

        def minus_max(b, par):
            wait(dve, mx_ok, UNITS * (b + 1))
            wait(dve, nm_mm, b)
            nc.vector.tensor_scalar(nmax[:, 0:2, 0, :], mx[par][:], -1.0, None, ALU.mult).then_inc(nm_hi, 1)
            wait(dve, nm_hi, b + 1)
            nc.vector.scalar_tensor_tensor(out=nmax[:, 0:2, 1, :], in0=mx[par][:], scalar=-1.0,
                                           in1=nmax[:, 0:2, 0, :], op0=ALU.mult, op1=ALU.subtract).then_inc(nm_ok, 1)

        def evac_nmax(b):
            wait(dve, nm_mm, b + 1)
            wait(dve, shift, 16 * b)
            nc.vector.tensor_copy(nmaxT[:], misc[1][0:4 * H, 0:P // 2].bitcast(BF16)).then_inc(nm_ev, 1)

        def sums(b, a):
            wait(dve, pv_ok, UNITS * b + (UNITS // 2) * (a + 1))
            wait(dve, on_ok, b)
            o = o_bank[a][:, 0:H * VC].rearrange("p (h c) -> p h c", h=H)
            nc.vector.tensor_reduce(osum[:, a], o[:, :, 0:PART * DH].rearrange("p h (s d) -> p h d s", s=PART),
                                    AXX, ALU.add)
            nc.vector.reciprocal(rden[:, a, :], o[:, :, VC - 1]).then_inc(o_red, 1)
            if a == 1:
                wait(dve, o_red, 2 * b + 2)
                nc.vector.tensor_tensor(rgate[:], rden[:], gcoef[:], ALU.mult).then_inc(rg_ok, 1)

        def low_unit(b):
            wait(dve, pa_ok, UNITS * b + LOW_U + 1)
            wait(dve, pv_ok, UNITS * b + LOW_U + 1 - RP)
            nc.vector.tensor_tensor(p_lo[LOW_U % RP][:], p_all[LOW_U % RP][:], p_hi[LOW_U % RP][:],
                                    ALU.subtract).then_inc(pd_ok, 1)

        def residual(b, n, n2, i, odd):
            wait(dve, wo_mm, b + 1)
            wait(dve, xr_in[i], 16 * (n2 + 1))
            if not odd:
                wait(dve, x2_st[i], 16 * ((n - i) // 2 if isinstance(n, int) else 0) if isinstance(n, int)
                     else n * 8 - 8 * i)
            nc.vector.scalar_tensor_tensor(out=x2[i][:, odd, :], in0=misc[1][:, 0:P], scalar=tg_x[:, 0:1],
                                           in1=xres[i][:, odd, :], op0=ALU.mult, op1=ALU.add).then_inc(x2_ok, 1)

        dve.wait_ge(tanh_ok, 2)
        dve.wait_ge(const_ok, 1)
        for n in range(2):
            norm_stats(n, 0, n)
            norm(n, n)
            rest_qk(n, n)
            rest_ka(n, n)
            low(n, n)
            if n == 0:
                rest_v(0, 0)
                low_v(0, 0)
        for u in range(UNITS):
            maxima(0, 0, u)
        minus_max(0, 0)
        evac_nmax(0)
        for u in range(FIRST_ODD):
            maxima(1, 1, u)

        def body(g, last):
            for k in range(BODY):
                b, n, i, odd = BODY * g + k, 2 * g + k // CH, k // CH, k % CH
                first = isinstance(b, int) and b == 0
                more = not (last and i == 1)
                ahead = not (last and k == BODY - 1)
                for u in range(UNITS):
                    for db, nu in S_PLAN[UNITS * odd + u]:
                        if db == 0 or more:
                            maxima(b - odd + 1 + db, (1 + db) % 2, nu)
                    if u == 2 and not (isinstance(b, int) and b < 2):
                        residual(b - 2, n - 1, g - 1 + i, 1 - i, odd)
                    if u == 0 and not first:
                        sums(b - 1, 0)
                    if u == LAG and not first:
                        sums(b - 1, 1)
                    if u == LOW_U + 1:
                        low_unit(b)
                    if u == 2 and ahead:
                        minus_max(b + 1, 1 - odd)
                    if u == 4 and ahead:
                        evac_nmax(b + 1)
                    if not last:
                        if u == 0 and not odd:
                            norm_stats(n + 2, g + 1, i)
                        if u == 1 and not odd:
                            norm(n + 2, i)
                        if u == 6 and not odd:
                            rest_qk(n + 2, i)
                        if u == 1 and odd:
                            rest_ka(n + 2, i)
                        if u == 3 and odd:
                            low(n + 2, i)
                    if u == 5 and odd and more:
                        rest_v(n + 1, (i + 1) % 2)
                    if u == 7 and odd and more:
                        low_v(n + 1, (i + 1) % 2)

        body(0, False)
        with dve.Fori(1, LOOPS - 1) as g:
            body(g, False)
        body(LOOPS - 1, True)
        sums(NB - 1, 0)
        sums(NB - 1, 1)
        residual(NB - 2, NC - 1, NC // 2 - 1, 1, 0)
        residual(NB - 1, NC - 1, NC // 2 - 1, 1, 1)

    @block.tensor
    def _(pe):
        def transposes(n, n2, i):
            wait(pe, xn_ok, n + 1)
            wait(pe, x_in[i], 32 * (n2 + 1))
            for c in range(CH):
                nc.tensor.transpose(misc[0][:, c * P:(c + 1) * P], xn[:, c, :], ident[:])
            for c in range(CH):
                ins = nc.tensor.transpose(misc[0][:, TC + c * P:TC + (c + 1) * P], cin[i][:, c, :], ident[:])
            ins.then_inc(t_mm, 1)

        def project_qk(n, i, o):
            wait(pe, t_ev, n + 1)
            ins = nc.tensor.matmul(misc[0][:, o * TC:(o + 1) * TC], wqk[:, o, :], xcT[i][:, 0, :],
                                   start=True, stop=True)
            if o == 1:
                ins.then_inc(qk_mm, 1)

        def project_ka(n, i):
            nc.tensor.matmul(misc[0][:, 0:TC], wqk[:, 2, :], xcT[i][:, 1, :],
                             start=True, stop=True).then_inc(ka_mm, 1)

        def project_v(n, i, a):
            for c in range(CH):
                o = (a * CH + c) * P
                ins = nc.tensor.matmul(misc[0][:, o:o + P], xcT[i][:, a, c * P:(c + 1) * P],
                                       (wqkv, wqkva)[a][:, 2, :], start=True, stop=True)
            if a == 1:
                ins.then_inc(v_mm, 1)

        def scores(b, k, u, n2):
            i, c = k // CH, k % CH
            if u == 0:
                wait(pe, stk[i], 16 * 3 * len(q_runs) * (n2 + 1))
            wait(pe, mx_ok, UNITS * b + u - 1)
            q, kk = stack[i][0], stack[i][1 + u // (UNITS // 2)]
            for j in range(HPU):
                h = (u % (UNITS // 2)) * HPU + j
                ins = nc.tensor.matmul(s_bank[u % 2][:, j * P:(j + 1) * P], q[0:ROWS_S, h, c * P:(c + 1) * P],
                                       kk[0:ROWS_S, h, c * P:(c + 1) * P], start=True, stop=True)
            ins.then_inc(s_mm, 1)

        def shifted(b, k, u):
            i, c = k // CH, k % CH
            if u == 0:
                wait(pe, shift, 16 * (b + 1))
            wait(pe, pa_ok, UNITS * b + u - 1)
            q, kk = stack[i][0], stack[i][1 + u // (UNITS // 2)]
            for j in range(HPU):
                h = (u % (UNITS // 2)) * HPU + j
                ins = nc.tensor.matmul(st_bank[u % 2][:, j * P:(j + 1) * P], kk[0:ROWS_ST, h, c * P:(c + 1) * P],
                                       q[0:ROWS_ST, h, c * P:(c + 1) * P], start=True, stop=True)
            ins.then_inc(st_mm, 1)

        def weighted(b, k, u):
            i, c = k // CH, k % CH
            a = u // (UNITS // 2)
            if u == LOW_U:
                wait(pe, pd_ok, b + 1)
            else:
                wait(pe, pl_ok, (UNITS - 1) * b + u + (u < LOW_U))
            if u == 0:
                wait(pe, v_ok, b // CH + 1 if isinstance(b, int) else v_ready_of(b))
                wait(pe, o_red, 2 * b - 1)
            if u == UNITS // 2:
                wait(pe, o_red, 2 * b)
            for j in range(HPU):
                h = (u % (UNITS // 2)) * HPU + j
                o = o_bank[a][:, h * VC:(h + 1) * VC]
                nc.tensor.matmul(o, p_hi[u % RP][:, j * P:(j + 1) * P], V[i][:, a * CH + c, h, :],
                                 start=True, stop=False)
                ins = nc.tensor.matmul(o, p_lo[u % RP][:, j * P:(j + 1) * P], V[i][:, a * CH + c, h, :],
                                       start=False, stop=True)
            ins.then_inc(pv_ok, 1)

        chunk_now = [None]

        def v_ready_of(b):
            return chunk_now[0] + 1

        def turn_att(b):
            wait(pe, at_ok, b + 1)
            nc.tensor.transpose(misc[1][:, 0:P], att[:], ident[:]).then_inc(at_mm, 1)

        def out_proj(b):
            wait(pe, at_ev, b + 1)
            nc.tensor.matmul(misc[1][:, 0:P], attT[:], wo[:], start=True, stop=False)
            nc.tensor.matmul(misc[1][:, 0:P], ones[0:1, :], bo_row[:], start=False, stop=True).then_inc(wo_mm, 1)

        def turn_max(b):
            wait(pe, nm_ok, b + 1)
            nc.tensor.transpose(misc[1][:, 0:P // 2].bitcast(BF16),
                                nmax[:].rearrange("p a s h -> p (a s h)"), ident_bf[:]).then_inc(nm_mm, 1)

        pe.wait_ge(ident_ok, 1)
        pe.wait_ge(c_in, 16 * CONSTS)
        pe.wait_ge(wqk_ok, 3)
        pe.wait_ge(kones_ok, 7)
        for n in range(2):
            if n == 1:
                pe.wait_ge(v_rest, 1)
            transposes(n, 0, n)
            project_qk(n, n, 0)
            project_qk(n, n, 1)
            pe.wait_ge(qk_rest, n + 1)
            project_ka(n, n)
            if n == 0:
                pe.wait_ge(ka_rest, 1)
                project_v(0, 0, 0)
                project_v(0, 0, 1)
        pe.wait_ge(stack_zero, 1)
        for u in range(UNITS):
            scores(0, 0, u, 0)
        turn_max(0)
        for u in range(FIRST_ODD):
            scores(1, 1, u, 0)

        def body(g, last):
            for k in range(BODY):
                b, n, i, odd = BODY * g + k, 2 * g + k // CH, k // CH, k % CH
                first, second = isinstance(b, int) and b == 0, isinstance(b, int) and b < 2
                more = not (last and i == 1)
                ahead = not (last and k == BODY - 1)
                for u in range(UNITS):
                    shifted(b, k, u)
                    if u >= LAG:
                        chunk_now[0] = n
                        weighted(b, k, u - LAG)
                    elif not first:
                        chunk_now[0] = n if odd else n - 1
                        weighted(b - 1, (k - 1) % BODY, u + UNITS - LAG)
                    for db, nu in S_PLAN[UNITS * odd + u]:
                        if db == 0 or more:
                            kk = k - odd + 1 + db
                            scores(b - odd + 1 + db, kk % BODY, nu, g + kk // BODY)
                    if u == 1 and not second:
                        out_proj(b - 2)
                    if u == 4 and ahead:
                        if second:
                            wait(pe, nm_ev, b + 1)
                        else:
                            wait(pe, x2_ok, b - 1)
                        turn_max(b + 1)
                    if u == 7 and not first:
                        if ahead:
                            wait(pe, nm_ev, b + 2)
                        else:
                            wait(pe, x2_ok, b - 1)
                        turn_att(b - 1)
                    if not odd and not last:
                        if u == 3:
                            wait(pe, v_rest, n + 1)
                            transposes(n + 2, g + 1, i)
                        if u in (5, 6):
                            project_qk(n + 2, i, u - 5)
                    if u == 0 and odd and not last:
                        wait(pe, qk_rest, n + 3)
                        project_ka(n + 2, i)
                    if u in (3, 4) and odd and more:
                        if u == 3 and not last:
                            wait(pe, ka_rest, n + 3)
                        project_v(n + 1, (i + 1) % 2, u - 3)

        body(0, False)
        with pe.Fori(1, LOOPS - 1) as g:
            body(g, False)
        body(LOOPS - 1, True)
        for u in range(LAG):
            chunk_now[0] = NC - 1
            weighted(NB - 1, BODY - 1, u + UNITS - LAG)
        out_proj(NB - 2)
        pe.wait_ge(x2_ok, NB - 1)
        turn_att(NB - 1)
        out_proj(NB - 1)


S_PLAN = (((0, 5),), ((0, 6),), ((0, 7),), (), (), (), ((1, 0), (1, 1)), ((1, 2), (1, 3)),
          ((1, 4),), ((1, 5), (1, 6)), ((1, 7),), ((2, 0),), ((2, 1),), ((2, 2),), ((2, 3),), ((2, 4),))
FIRST_ODD = 5


def experts(nc, ctx_, sem, m, r, psum, v):
    tick = v["tick"]
    x2d, out, ident, tg_f = v["x2d"], v["out"], v["ident"], v["tg_f"]
    wg_raw, wu_raw, wd_raw, w_in, w_zero = v["wg_raw"], v["wu_raw"], v["wd_raw"], v["w_in"], v["w_zero"]
    NEX, NP, NB = v["NEX"], v["NP"], v["NB"]
    K = 4
    T = K * P
    NCH = NB // K
    LOOPS = NCH // 2
    LAG = 4
    GP = 3
    GROUPS = NP // GP
    EPG = E // NG
    RS, RH = 3, 6

    wg = [m(f"wg_{s}", [P, NEX, F], F32R) for s in ("hi", "lo")]
    wu = [m(f"wu_{s}", [P, NEX, F], F32R) for s in ("hi", "lo")]
    wd = [m(f"wd_{s}", [P, NP, P], F32R) for s in ("hi", "lo")]
    x2c = [m(f"x2c{i}", [P, K, P], F32) for i in range(2)]
    xhi = [m(f"xhi{i}", [P, T], F32R) for i in range(2)]
    xlo = [m(f"xlo{i}", [P, T], F32R) for i in range(2)]
    hhi = [m(f"hhi{i}", [P, T], F32R) for i in range(RH)]
    hlo = [m(f"hlo{i}", [P, T], F32R) for i in range(RH)]
    xn = m("xn2", [P, K, P], F32)
    xT = m("xT2", [P, T], F32)
    wT = m("wT", [NEX, T], F32)
    stats = m("stats2", [P, K, 6], F32)
    mv = m("mv2", [P, K, 2], F32)
    var = m("var2", [P, K], F32)
    rstd = m("rstd2", [P, K], F32)
    mhalf = m("mhalf2", [P, K], F32)
    gw_in = m("gw_in", [E, P], F32)
    gwT = m("gwT", [P, E], F32)
    gbias = m("gbias", [P, E], F32)
    tri = m("tri", [P, NG, NG], F32)
    s_buf = [r(f"silu{i}", [P, T], F32) for i in range(RS)]
    a_buf = [r(f"act{i}", [P, T], F32) for i in range(RS)]
    h_buf = [r(f"hid{i}", [P, T], F32) for i in range(RS)]
    cwb = [r(f"cwb{i}", [P, GP, T], F32) for i in range(2)]
    ysb = r("ysb", [P, T], F32)
    osb = [r(f"osb{i}", [P, K, P], F32) for i in range(2)]
    sig = m("sig", [P, K, E], F32)
    sc = m("sc", [P, K, E], F32)
    top_a, low_a = m("top_a", [P, K * NG, 4], F32), m("low_a", [P, K * NG, 4], F32)
    top_b, low_b, mid_b = (m(f"{n}_b", [P, K * NG, 2], F32) for n in ("top", "low", "mid"))
    top_c, low_c, mid_c = (m(f"{n}_c", [P, K * NG, 1], F32) for n in ("top", "low", "mid"))
    gs = m("gs", [P, K, NG], F32)
    gt = r("gt", [P, K, NG, NG], F32)
    eq = r("eq", [P, K, NG, NG], F32)
    rank = m("rank", [P, K, NG], F32)
    gm = m("gm", [P, K, NG], F32)
    pen = m("pen", [P, K, NG], F32)
    masked = r("masked", [P, K, E], F32)
    best = m("best", [P, K, TK], F32)
    rep = r("rep", [P, K, E], F32)
    wsel = r("wsel", [P, K, E], F32)
    wsum = m("wsum", [P, K], F32)
    wnorm = r("wnorm", [P, K, E], F32)

    g_bank, u_bank, y_bank, misc = psum[0:2], psum[2:5], psum[5:7], psum[7]
    wts_d = nc.dram_tensor("wts_scratch", (NCH, NEX, T), F32, kind="Internal").ap()
    wts_v = wts_d.rearrange("c (p two) t -> c two p t", two=2)
    x2_v = x2d.rearrange("(c k) t d -> c t k d", k=K)
    out_v = out.rearrange("(c k) t d -> c t k d", k=K)

    g_in = sem("gate_loaded")
    c_ok = sem("expert_consts")
    gw_mm, gw_ev = sem("gate_w_transposed"), sem("gate_wT_ready")
    cv_hi, cv_lo = sem("weights_hi"), sem("weights_lo")
    x2_in = [sem(f"x2_loaded{i}") for i in range(2)]
    st_ok, mv_ok, var_ok, rstd_ok, xn_ok = (sem(f"{n}_2") for n in ("ln_stats", "ln_mv", "ln_var", "ln_rstd", "xn"))
    xt_mm, xhi_ok, xT_ok, xlo_ok = sem("x2_transposed"), sem("xhi_ready"), sem("xT_ready"), sem("xlo_ready")
    lg_mm, sig_ok, rt, w_ok = sem("logits"), sem("sigmoids"), sem("route_step"), sem("route_weights")
    rd_ok = sem("route_denominators")
    wt_mm, wt_ev, wt_st = sem("weights_transposed"), sem("wT_ready"), sem("wT_stored")
    cw_in = [sem(f"cwb_loaded{i}") for i in range(2)]
    g_mm, u_mm, s_ok, a_ok, h_ok = (sem(n) for n in ("gate_mm", "up_mm", "silu_ready", "act_ready", "hid_ready"))
    hh_ok, hl_ok, dn_mm = sem("hid_hi"), sem("hid_lo"), sem("down_mm")
    y_ev, yt_mm, out_ok = sem("y_copied"), sem("y_transposed"), sem("out_ready")
    o_st = [sem(f"out_stored{i}") for i in range(2)]

    F_COPY, F_TURN, F_OUT, F_GROUP = LAG + 1, LAG + 2, LAG + 3, 4
    P_STAT, P_ROOT, P_NORM, P_TURN, P_OPER, P_LOGIT, P_SIG, P_ROUTE, P_WT, P_WEV = 10, 10, 11, 12, 13, 14, 15, 16, 26, 27
    CONV = 3
    R_STEPS = 26

    block = ctx_.enter_context(nc.Block())

    def conv_slices():
        for s in range(CONV):
            e0, e1 = s * NEX // CONV, (s + 1) * NEX // CONV
            q0, q1 = s * NP // CONV, (s + 1) * NP // CONV
            yield wg_raw[:, e0:e1, :], [w[:, e0:e1, :] for w in wg]
            yield wu_raw[:, e0:e1, :], [w[:, e0:e1, :] for w in wu]
            yield wd_raw[:, q0:q1, :], [w[:, q0:q1, :] for w in wd]

    @block.sync
    def _(sp):
        def load_x2(c, c2, i):
            wait(sp, out_ok, c - 1)
            sp.dma_start(x2c[i][:], x2_v[c]).then_inc(x2_in[i], 16)

        def store_w(c):
            wait(sp, wt_ev, c + 1)
            sp.dma_start(wts_d[c], wT[:]).then_inc(wt_st, 16)
            wait(sp, wt_st, 16 * c + 16)

        def load_cwb(c, gr, slot):
            wait(sp, h_ok, NP * c + GP * (gr - 1))
            for half in range(2):
                sp.dma_start(cwb[slot][half * F:(half + 1) * F, :, :],
                             wts_v[c][half][GP * gr:GP * (gr + 1)].unsqueeze(0).to_broadcast([F, GP, T])
                             ).then_inc(cw_in[slot], 16)

        def store_out(c, i):
            wait(sp, out_ok, c + 1)
            sp.dma_start(out_v[c], osb[i][:]).then_inc(o_st[i], 16)

        sp.dma_start(gw_in[:], v["gate_w"]).then_inc(g_in, 16)
        sp.dma_start(gbias[:], v["gate_bias"].rearrange("(a n) -> a n", a=1).to_broadcast([P, E])).then_inc(g_in, 16)
        load_x2(0, 0, 0)
        store_w(0)
        sp.wait_ge(cv_lo, 3 * CONV)
        load_cwb(0, 0, 0)
        load_cwb(0, 1, 1)

        def body(g, last):
            for j in range(2):
                c = 2 * g + j
                first = isinstance(c, int) and c == 0
                more = not (last and j == 1)
                for gr in range(2, GROUPS):
                    load_cwb(c, gr, (GROUPS * j + gr) % 2)
                    if gr == F_GROUP:
                        if not first:
                            store_out(c - 1, 1 - j)
                        if more:
                            load_x2(c + 1, g + (j + 1) // 2, 1 - j)
                if more:
                    store_w(c + 1)
                    for gr in range(2):
                        load_cwb(c + 1, gr, (GROUPS * (j + 1) + gr) % 2)

        body(0, False)
        with sp.Fori(1, LOOPS - 1) as g:
            body(g, False)
        body(LOOPS - 1, True)
        store_out(NCH - 1, 1)
        for i in range(2):
            sp.wait_ge(o_st[i], 16 * (NCH // 2))

    @block.gpsimd
    def _(pool):
        pool.memset(mhalf[:], -0.5).then_inc(c_ok, 1)
        pool.wait_ge(c_ok, 1)
        pool.memset(wT[E:NEX, :], 1.0).then_inc(c_ok, 1)
        pool.wait_ge(c_ok, 2)
        pool.memset(tri[:], 1.0).then_inc(c_ok, 1)
        pool.wait_ge(c_ok, 3)
        pool.affine_select(out=tri[:], in_=tri[:], compare_op=ALU.is_gt, fill=0.0, base=0,
                           pattern=[[1, NG], [-1, NG]], channel_multiplier=0).then_inc(c_ok, 1)

        def root(c):
            wait(pool, var_ok, c + 1)
            pool.tensor_tensor(rstd[:], var[:], mhalf[:], ALU.pow).then_inc(rstd_ok, 1)

        def hidden(n, q, j, g):
            slot = (GROUPS * j + q // GP) % 2
            wait(pool, a_ok, n + 1)
            if q % GP == 0:
                wait(pool, cw_in[slot], 32 * (GROUPS * g + (GROUPS * j + q // GP) // 2 + 1))
            wait(pool, hl_ok, n + 1 - RS)
            k = (NP * j + q) % RS
            pool.tensor_tensor(h_buf[k][:], a_buf[k][:], cwb[slot][:, q % GP, :], ALU.mult).then_inc(h_ok, 1)

        root(0)
        pool.wait_ge(cv_lo, 3 * CONV)

        def body(g, last):
            for j in range(2):
                c = 2 * g + j
                for q in range(NP):
                    hidden(NP * c + q, q, j, g)
                    if q == P_ROOT and not (last and j == 1):
                        root(c + 1)

        body(0, False)
        with pool.Fori(1, LOOPS - 1) as g:
            body(g, False)
        body(LOOPS - 1, True)

    @block.scalar
    def _(act):
        def operands(c, i):
            wait(act, xt_mm, c + 1)
            wait(act, u_mm, NP * (c - 1))
            act.activation(xhi[i][:], misc[:], ACT.Copy).then_inc(xhi_ok, 1)
            wait(act, lg_mm, c)
            act.activation(xT[:], misc[:], ACT.Copy).then_inc(xT_ok, 1)

        def sigmoids(c):
            wait(act, lg_mm, c + 1)
            wait(act, w_ok, c)
            act.activation(sig[:].rearrange("p k e -> p (k e)"), misc[:, 0:K * E], ACT.Sigmoid).then_inc(sig_ok, 1)

        def evac_w(c):
            wait(act, wt_mm, c + 1)
            wait(act, wt_st, 16 * c)
            act.activation(wT[0:E, :], misc[0:E, :], ACT.Copy).then_inc(wt_ev, 1)

        def silu(n, k):
            wait(act, g_mm, n + 1)
            wait(act, a_ok, n + 1 - RS)
            act.activation(s_buf[k % RS][:], g_bank[k % 2][:], ACT.Silu).then_inc(s_ok, 1)

        def hid_hi(n, k):
            wait(act, h_ok, n + 1)
            wait(act, dn_mm, n + 1 - RH)
            act.activation(hhi[k % RH][:], h_buf[k % RS][:], ACT.Copy).then_inc(hh_ok, 1)

        def copy_y(c, i):
            wait(act, dn_mm, NP * (c + 1))
            wait(act, yt_mm, c)
            act.activation(ysb[:], y_bank[i][:], ACT.Copy).then_inc(y_ev, 1)

        act.wait_ge(gw_mm, 1)
        act.activation(gwT[:], misc[:, 0:E], ACT.Copy).then_inc(gw_ev, 1)
        act.wait_ge(w_zero, 3)
        for i, n in enumerate((2 * E // 16, 2, 3)):
            act.wait_ge(w_in[i], 16 * n)
        for s, (src, dst) in enumerate(conv_slices()):
            act.activation(dst[0], src, ACT.Copy).then_inc(cv_hi, 1)
            if s == 2:
                operands(0, 0)
            if s == 4:
                sigmoids(0)
        evac_w(0)
        act.wait_ge(cv_lo, 3 * CONV)

        def body(g, last):
            for j in range(2):
                c = 2 * g + j
                first = isinstance(c, int) and c == 0
                more = not (last and j == 1)
                for q in range(NP):
                    n, k = NP * c + q, NP * j + q
                    silu(n, k)
                    if not (first and q < 2):
                        hid_hi(n - 2, k - 2)
                    if q == F_COPY and not first:
                        copy_y(c - 1, 1 - j)
                    if more:
                        if q == P_OPER:
                            operands(c + 1, 1 - j)
                        if q == P_SIG:
                            sigmoids(c + 1)
                        if q == P_WEV:
                            evac_w(c + 1)

        body(0, False)
        with act.Fori(1, LOOPS - 1) as g:
            body(g, False)
        body(LOOPS - 1, True)
        for q in range(2):
            hid_hi(NP * NCH - 2 + q, 2 * NP - 2 + q)
        copy_y(NCH - 1, 1)

    @block.vector
    def _(dve):
        def norm_stats(c, c2, i):
            wait(dve, x2_in[i], 16 * (c2 + 1))
            for k in range(K):
                ins = nc.vector.bn_stats(stats[:, k, :], x2c[i][:, k, :])
            ins.then_inc(st_ok, 1)
            wait_tick(nc, st_ok, c + 1, tick)
            for k in range(K):
                ins = nc.vector.bn_aggr(mv[:, k, :], stats[:, k, :])
            ins.then_inc(mv_ok, 1)
            wait(dve, mv_ok, c + 1)
            nc.vector.tensor_scalar(var[:], mv[:, :, 1], EPS, None, ALU.add).then_inc(var_ok, 1)

        def norm(c, i):
            wait(dve, rstd_ok, c + 1)
            wait(dve, xt_mm, c)
            for k in range(K):
                ins = nc.vector.tensor_scalar(xn[:, k, :], x2c[i][:, k, :], mv[:, k, 0:1], rstd[:, k:k + 1],
                                              ALU.subtract, ALU.mult)
            ins.then_inc(xn_ok, 1)

        def oper_lo(c, i):
            wait(dve, xT_ok, c + 1)
            wait(dve, xhi_ok, c + 1)
            wait(dve, u_mm, NP * (c - 1))
            nc.vector.tensor_tensor(xlo[i][:], misc[:], xhi[i][:].bitcast(F32), ALU.subtract).then_inc(xlo_ok, 1)

        def route_groups(c, part):
            done = lambda k: wait(dve, rt, R_STEPS * c + k)
            tt = nc.vector.tensor_tensor
            if part == 0:
                wait(dve, sig_ok, c + 1)
                tt(sc[:], sig[:], gbias[:].unsqueeze(1).to_broadcast([P, K, E]), ALU.add).then_inc(rt, 1)
                s8 = sc[:].rearrange("p k (g e) -> p (k g) e", g=NG)
                done(1)
                tt(top_a[:], s8[:, :, 0:4], s8[:, :, 4:8], ALU.max).then_inc(rt, 1)
                tt(low_a[:], s8[:, :, 0:4], s8[:, :, 4:8], ALU.min).then_inc(rt, 1)
                done(3)
                tt(mid_b[:], top_a[:, :, 0:2], top_a[:, :, 2:4], ALU.min).then_inc(rt, 1)
                tt(top_b[:], top_a[:, :, 0:2], top_a[:, :, 2:4], ALU.max).then_inc(rt, 1)
                tt(low_b[:], low_a[:, :, 0:2], low_a[:, :, 2:4], ALU.max).then_inc(rt, 1)
                done(6)
                tt(low_b[:], low_b[:], mid_b[:], ALU.max).then_inc(rt, 1)
            if part == 1:
                tt(mid_c[:], top_b[:, :, 0:1], top_b[:, :, 1:2], ALU.min).then_inc(rt, 1)
                tt(top_c[:], top_b[:, :, 0:1], top_b[:, :, 1:2], ALU.max).then_inc(rt, 1)
                done(9)
                tt(low_c[:], low_b[:, :, 0:1], low_b[:, :, 1:2], ALU.max).then_inc(rt, 1)
                done(10)
                tt(low_c[:], low_c[:], mid_c[:], ALU.max).then_inc(rt, 1)
                done(11)
                tt(gs[:].rearrange("p k g -> p (k g)"), top_c[:, :, 0], low_c[:, :, 0], ALU.add).then_inc(rt, 1)
            if part == 2:
                done(12)
                other = gs[:].unsqueeze(2).to_broadcast([P, K, NG, NG])
                own = gs[:].unsqueeze(3).to_broadcast([P, K, NG, NG])
                tt(eq[:], other, own, ALU.is_equal).then_inc(rt, 1)
                tt(gt[:], other, own, ALU.is_gt).then_inc(rt, 1)
                done(14)
                tt(eq[:], eq[:], tri[:].unsqueeze(1).to_broadcast([P, K, NG, NG]), ALU.mult).then_inc(rt, 1)
            if part == 3:
                done(15)
                tt(gt[:], gt[:], eq[:], ALU.add).then_inc(rt, 1)
                done(16)
                nc.vector.tensor_reduce(rank[:], gt[:], AXX, ALU.add).then_inc(rt, 1)
                done(17)
                nc.vector.tensor_scalar(gm[:], rank[:], float(TG), None, ALU.is_lt).then_inc(rt, 1)
            if part == 4:
                done(18)
                nc.vector.tensor_scalar(pen[:], gm[:], -LOW, LOW, ALU.mult, ALU.add).then_inc(rt, 1)
                s8 = sc[:].rearrange("p k (g e) -> p (k g) e", g=NG)
                m8 = masked[:].rearrange("p k (g e) -> p (k g) e", g=NG)
                by_group = lambda t: t[:].rearrange("p k g -> p (k g)").unsqueeze(2).to_broadcast([P, K * NG, EPG])
                tt(m8, s8, by_group(gm), ALU.mult).then_inc(rt, 1)
                done(20)
                tt(m8, m8, by_group(pen), ALU.add).then_inc(rt, 1)

        def route_experts(c, part):
            done = lambda k: wait(dve, rt, R_STEPS * c + k)
            tt = nc.vector.tensor_tensor
            if part == 0:
                wait_tick(nc, rt, R_STEPS * c + 21, tick)
                for k in range(K):
                    ins = nc.vector.max(best[:, k, :], masked[:, k, :])
                ins.then_inc(rt, 1)
                wait_tick(nc, rt, R_STEPS * c + 22, tick)
                for k in range(K):
                    ins = nc.vector.match_replace(out=rep[:, k, :], in_to_replace=best[:, k, :],
                                                  in_values=masked[:, k, :], imm_value=LOWER)
                ins.then_inc(rt, 1)
            if part == 1:
                done(23)
                tt(wsel[:], rep[:], masked[:], ALU.not_equal).then_inc(rt, 1)
                done(24)
                tt(wsel[:], wsel[:], sig[:], ALU.mult).then_inc(rt, 1)
                done(25)
                nc.vector.tensor_reduce(wsum[:], wsel[:], AXX, ALU.add).then_inc(rt, 1)
            if part == 2:
                done(26)
                nc.vector.tensor_scalar(wsum[:], wsum[:], 1e-20, 1.0 / ROUTE_SCALE, ALU.add, ALU.mult).then_inc(rd_ok, 1)
                wait(dve, rd_ok, 2 * c + 1)
                nc.vector.reciprocal(wsum[:], wsum[:]).then_inc(rd_ok, 1)
                wait(dve, rd_ok, 2 * c + 2)
                wait(dve, wt_mm, c)
                tt(wnorm[:], wsel[:], wsum[:].unsqueeze(2).to_broadcast([P, K, E]), ALU.mult).then_inc(w_ok, 1)

        def act_up(n, k):
            wait(dve, s_ok, n + 1)
            wait(dve, u_mm, n + 1)
            wait(dve, h_ok, n + 1 - RS)
            nc.vector.tensor_tensor(a_buf[k % RS][:], s_buf[k % RS][:], u_bank[k % 3][:], ALU.mult).then_inc(a_ok, 1)

        def hid_lo(n, k):
            wait(dve, hh_ok, n + 1)
            nc.vector.tensor_tensor(hlo[k % RH][:], h_buf[k % RS][:], hhi[k % RH][:].bitcast(F32),
                                    ALU.subtract).then_inc(hl_ok, 1)

        def finish(c, c2, i):
            wait(dve, yt_mm, c + 1)
            wait(dve, o_st[i], 16 * c2)
            nc.vector.scalar_tensor_tensor(out=osb[i][:].rearrange("p k d -> p (k d)"), in0=misc[:],
                                           scalar=tg_f[:, 0:1], in1=x2c[i][:].rearrange("p k d -> p (k d)"),
                                           op0=ALU.mult, op1=ALU.add).then_inc(out_ok, 1)

        dve.wait_ge(c_ok, 4)
        dve.wait_ge(g_in, 32)
        norm_stats(0, 0, 0)
        norm(0, 0)
        for s, (src, dst) in enumerate(conv_slices()):
            wait(dve, cv_hi, s + 1)
            nc.vector.tensor_tensor(dst[1], src, dst[0].bitcast(F32), ALU.subtract).then_inc(cv_lo, 1)
            if s == 2:
                oper_lo(0, 0)
        for part in range(5):
            route_groups(0, part)
        for part in range(3):
            route_experts(0, part)

        def body(g, last):
            for j in range(2):
                c = 2 * g + j
                first = isinstance(c, int) and c == 0
                more = not (last and j == 1)
                for q in range(NP):
                    n, k = NP * c + q, NP * j + q
                    act_up(n, k)
                    if not (first and q < 2):
                        hid_lo(n - 2, k - 2)
                    if q == F_OUT and not first:
                        finish(c - 1, g - 1 + j, 1 - j)
                    if more:
                        if q == P_STAT:
                            norm_stats(c + 1, g + (j + 1) // 2, 1 - j)
                        if q == P_NORM:
                            norm(c + 1, 1 - j)
                        if q == P_OPER:
                            oper_lo(c + 1, 1 - j)
                        if P_ROUTE <= q < P_ROUTE + 5:
                            route_groups(c + 1, q - P_ROUTE)
                        if P_ROUTE + 5 <= q < P_ROUTE + 8:
                            route_experts(c + 1, q - P_ROUTE - 5)

        body(0, False)
        with dve.Fori(1, LOOPS - 1) as g:
            body(g, False)
        body(LOOPS - 1, True)
        for q in range(2):
            hid_lo(NP * NCH - 2 + q, 2 * NP - 2 + q)
        finish(NCH - 1, LOOPS - 1, 1)

    @block.tensor
    def _(pe):
        def turn_x(c):
            wait(pe, xn_ok, c + 1)
            for k in range(K):
                ins = nc.tensor.transpose(misc[:, k * P:(k + 1) * P], xn[:, k, :], ident[:])
            ins.then_inc(xt_mm, 1)

        def logits(c):
            wait(pe, xT_ok, c + 1)
            wait(pe, xlo_ok, c + 1)
            for k in range(K):
                ins = nc.tensor.matmul(misc[:, k * E:(k + 1) * E], xT[:, k * P:(k + 1) * P], gwT[:],
                                       start=True, stop=True)
            ins.then_inc(lg_mm, 1)

        def before_turn_w(c):
            wait(pe, sig_ok, c + 1)
            wait(pe, w_ok, c + 1)

        def turn_w(c):
            for k in range(K):
                ins = nc.tensor.transpose(misc[0:E, k * P:(k + 1) * P], wnorm[:, k, :], ident[:])
            ins.then_inc(wt_mm, 1)

        def turn_y(c):
            wait(pe, y_ev, c + 1)
            for k in range(K):
                ins = nc.tensor.transpose(misc[:, k * P:(k + 1) * P], ysb[:, k * P:(k + 1) * P], ident[:])
            ins.then_inc(yt_mm, 1)

        def three(bank, w, mh, ml, first, last):
            nc.tensor.matmul(bank, w[0], mh, start=first, stop=False)
            nc.tensor.matmul(bank, w[1], mh, start=False, stop=False)
            return nc.tensor.matmul(bank, w[0], ml, start=False, stop=last)

        def gate_up(n, k, q, i):
            pick = lambda w: [t[:, 2 * q:2 * q + 2, :].rearrange("p e f -> p (e f)") for t in w]
            wait(pe, s_ok, n - 1)
            three(g_bank[k % 2][:], pick(wg), xhi[i][:], xlo[i][:], True, True).then_inc(g_mm, 1)
            wait(pe, a_ok, n - 2)
            three(u_bank[k % 3][:], pick(wu), xhi[i][:], xlo[i][:], True, True).then_inc(u_mm, 1)

        def down(n, k, q, i):
            wait(pe, hl_ok, n + 1)
            three(y_bank[i][:], [w[:, q, :] for w in wd], hhi[k % RH][:], hlo[k % RH][:],
                  q == 0, q == NP - 1).then_inc(dn_mm, 1)

        pe.wait_ge(g_in, 32)
        nc.tensor.transpose(misc[:, 0:E], gw_in[:], ident[0:E, 0:E]).then_inc(gw_mm, 1)
        pe.wait_ge(gw_ev, 1)
        turn_x(0)
        logits(0)
        before_turn_w(0)
        turn_w(0)
        pe.wait_ge(cv_lo, 3 * CONV)

        def body(g, last):
            for j in range(2):
                c = 2 * g + j
                first = isinstance(c, int) and c == 0
                more = not (last and j == 1)
                for q in range(NP):
                    n, k = NP * c + q, NP * j + q
                    if q == P_WT and more:
                        before_turn_w(c + 1)
                    gate_up(n, k, q, j)
                    if q >= LAG:
                        if q == LAG:
                            wait(pe, y_ev, c - 1)
                        down(n - LAG, k - LAG, q - LAG, j)
                    elif not first:
                        down(n - LAG, k - LAG, q - LAG + NP, 1 - j)
                    if q == F_TURN and not first:
                        turn_y(c - 1)
                    if more:
                        if q == P_TURN:
                            wait(pe, out_ok, c)
                            turn_x(c + 1)
                        if q == P_LOGIT:
                            logits(c + 1)
                        if q == P_WT:
                            turn_w(c + 1)

        body(0, False)
        with pe.Fori(1, LOOPS - 1) as g:
            body(g, False)
        body(LOOPS - 1, True)
        for q in range(LAG):
            down(NP * NCH - LAG + q, 2 * NP - LAG + q, NP - LAG + q, 1)
        turn_y(NCH - 1)


_INS = ['x', 'ctx_1024', 'g_xattn', 'g_ffn', 'L0_xattn_Wqkv', 'L0_xattn_bqkv', 'L0_xattn_Wqkv_aux',
        'L0_xattn_bqkv_aux', 'L0_xattn_Wo', 'L0_xattn_bo', 'L0_xattn_g', 'L0_ffn_gate_w', 'L0_ffn_gate_bias',
        'L0_ffn_We_gate', 'L0_ffn_We_up', 'L0_ffn_We_down', 'L0_ffn_Ws_gate', 'L0_ffn_Ws_up', 'L0_ffn_Ws_down']
_OUTS = [((32, 128, 128), 'float32')]


def kernel(**inputs):
    import numpy as _np
    import concourse.bacc as _bacc
    from concourse import mybir as _mybir
    from concourse.bass_utils import run_bass_kernel_spmd as _run

    nc = _bacc.Bacc("TRN2", target_bir_lowering=False, num_devices=1)
    arrays, args = {}, []
    for name in _INS:
        a = _np.ascontiguousarray(inputs[name])
        arrays[f"in_{name}_dram"] = a
        args.append(nc.dram_tensor(f"in_{name}_dram", a.shape, _mybir.dt.from_np(a.dtype), kind="ExternalInput").ap())
    for i, (shape, dtype) in enumerate(_OUTS):
        dt = _mybir.dt.from_np(_np.dtype(dtype))
        args.append(nc.dram_tensor(f"out_{i}_dram", shape, dt, kind="ExternalOutput").ap())
    build(nc, *args)
    r = _run(nc, [arrays], core_ids=[0])
    got = tuple(r.results[0][f"out_{i}_dram"] for i in range(len(_OUTS)))
    return got[0]
```

```python
from contextlib import ExitStack

import concourse.bass as bass
from concourse import mybir

F32 = mybir.dt.float32
F32R = mybir.dt.float32r
BF16 = mybir.dt.bfloat16
FP16 = mybir.dt.float16
ALU = mybir.AluOpType
ACT = mybir.ActivationFunctionType
AXX = mybir.AxisListType.X

P = 128
H, DH = 16, 8
PART = 3
Q_SLOTS = (0, 0, 0, 1, 1, 2)
K_SLOTS = (0, 1, 2, 0, 1, 0)
ROWS = len(Q_SLOTS) * DH
SHIFT = 96
ROWS_S, ROWS_ST = SHIFT, P
VC = PART * DH + 1
EPS = 1e-5
HPU = 4
UNITS = 2 * H // HPU
E, F = 64, 64
NG, TG, TK = 8, 4, 8
ROUTE_SCALE = 2.5
LOW, LOWER = -3.0e38, -3.4e38


class Map:

    def __init__(self, nc, base, end):
        self.nc, self.at, self.end = nc, base, end

    def __call__(self, name, shape, dt):
        size = {F32: 4, F32R: 4, BF16: 2, FP16: 2}[dt]
        for n in shape[1:]:
            size *= n
        t = self.nc.alloc_sbuf_tensor_at(name, shape, dt, offset=self.at)
        self.at += (size + 31) // 32 * 32
        assert self.at <= self.end, (name, self.at, self.end)
        return t


def wait(eng, sem, value):
    if isinstance(value, int) and value <= 0:
        return
    eng.wait_ge(sem, value)


def wait_tick(nc, sem, value, tick):
    wait(nc.vector, sem, value)
    if not isinstance(value, int):
        nc.vector.tensor_copy(tick[0:1, 1:2], tick[0:1, 0:1])


def build(nc, x, ctx, g_xattn, g_ffn, Wqkv, bqkv, Wqkv_aux, bqkv_aux, Wo, bo, g_head,
          gate_w, gate_bias, We_gate, We_up, We_down, Ws_gate, Ws_up, Ws_down, out):
    NB = x.shape[0]
    CH = 2
    TC = CH * P
    base = (nc.sbuf_base + 63) // 64 * 64
    end = nc.sbuf_usable_end
    BODIES = NB // (2 * CH)

    x2d = nc.dram_tensor("x2_scratch", (NB, P, P), F32, kind="Internal").ap()
    parts_d = nc.dram_tensor("parts_scratch", (NB // CH, 3 * PART, P, TC), BF16, kind="Internal").ap()

    with ExitStack() as ctx_:
        psum = [ctx_.enter_context(nc.psum_tensor(f"bank{i}", [P, 512], F32)) for i in range(8)]
        names = {}

        def sem(name):
            names[name] = ctx_.enter_context(nc.semaphore(name))
            return names[name]

        keep = Map(nc, base, end)
        ident = keep("ident", [P, P], F32)
        tick = keep("tick", [P, 2], F32)
        ident_bf = keep("ident_bf", [P, P], BF16)
        tg_x = keep("tg_x", [P, 1], F32)
        tg_f = keep("tg_f", [P, 1], F32)
        gw_in = keep("gw_in", [E, P], F32)
        gbias = keep("gbias", [P, E], F32)
        xld = keep("xld", [P, 4, P], F32)
        g_in, xl_in = sem("gate_loaded"), sem("x2_loaded_for_norm")
        NEX = E + 2
        NP = NEX // 2
        raw_base = (end - (2 * NEX * F + NP * P) * 4) // 32 * 32
        raw = Map(nc, raw_base, end)
        wg_raw = raw("wg_raw", [P, NEX, F], F32)
        wu_raw = raw("wu_raw", [P, NEX, F], F32)
        wd_raw = raw("wd_raw", [P, NP, P], F32)
        w_in = [sem("expert_weights_loaded"), sem("shared_weights_loaded")]
        w_zero = sem("w_zero")

        v = dict(locals())
        with ExitStack() as stage:
            attention(nc, stage, sem, Map(nc, keep.at, raw_base), psum, v)
        with ExitStack() as stage:
            experts(nc, stage, sem, Map(nc, keep.at, raw_base), Map(nc, raw_base, end), psum, v)


def attention(nc, ctx_, sem, m, psum, v):
    x, ctx, x2d, parts_d = v["x"], v["ctx"], v["x2d"], v["parts_d"]
    tick = v["tick"]
    ident, ident_bf, tg_x, tg_f = v["ident"], v["ident_bf"], v["tg_x"], v["tg_f"]
    wg_raw, wu_raw, wd_raw, w_in, w_zero = v["wg_raw"], v["wu_raw"], v["wd_raw"], v["w_in"], v["w_zero"]
    NB, CH, TC = v["NB"], v["CH"], v["TC"]
    gw_in, gbias, xld, g_in, xl_in = v["gw_in"], v["gbias"], v["xld"], v["g_in"], v["xl_in"]
    NC = NB // CH
    BODY = 2 * CH
    LOOPS = NB // BODY

    stack = [[m(f"stack_{o}{i}", [P, H, TC], BF16) for o in ("q", "k", "ka")] for i in range(2)]
    kones = m("kones", [P, 6], BF16)
    xin = [m(f"xin{i}", [P, CH, P], F32) for i in range(2)]
    cin = [m(f"cin{i}", [P, CH, P], F32) for i in range(2)]
    xres = [m(f"xres{i}", [P, CH, P], F32) for i in range(2)]
    x2 = [m(f"x2_{i}", [P, CH, P], F32) for i in range(2)]
    stats = m("stats", [P, CH, 6], F32)
    mv = m("mv", [P, CH, 2], F32)
    var = m("var", [P, CH], F32)
    rstd = m("rstd", [P, CH], F32)
    mhalf = m("mhalf", [P, CH], F32)
    xn = m("xn", [P, CH, P], F32)
    xcT = [m(f"xcT{i}", [P, 2, TC], F32) for i in range(2)]
    parts = [m(f"parts{i}", [P, 3, PART, TC], BF16) for i in range(2)]
    rest = m("rest", [P, 3, TC], F32)
    vrest = m("vrest", [P, 2 * CH, P], F32)
    V = [m(f"V{i}", [P, 2 * CH, H, VC], BF16) for i in range(2)]
    RP = 8
    LOW_U = 3
    LAG = 4
    p_hi = [m(f"p_hi{i}", [P, HPU * P], FP16) for i in range(RP)]
    p_all = [m(f"p_all{i}", [P, HPU * P], F32) for i in range(RP)]
    p_lo = [m(f"p_lo{i}", [P, HPU * P], FP16) for i in range(RP)]
    mx = [m(f"mx{i}", [P, 2, H], F32) for i in range(2)]
    nmax = m("nmax", [P, 4, 2, H], BF16)
    nmaxT = m("nmaxT", [4 * H, P], BF16)
    osum = m("osum", [P, 2, H, DH], F32)
    rden = m("rden", [P, 2, H], F32)
    rgate = m("rgate", [P, 2, H], F32)
    onorm = m("onorm", [P, 2, H, DH], F32)
    att = m("att", [P, P], F32)
    attT = m("attT", [P, P], F32)
    wqkv = m("wqkv", [P, 3, P], F32)
    wqkva = m("wqkva", [P, 3, P], F32)
    wqk = m("wqk", [P, 3, P], F32)
    wo = m("wo", [P, P], F32)
    bcol = m("bcol", [P, 5], F32)
    bo_row = m("bo_row", [P, P], F32)
    gh = m("gh", [P, H], F32)
    ghc = m("ghc", [P, 1], F32)
    gcoef = m("gcoef", [P, 2, H], F32)
    gcol = m("gcol", [P, 2], F32)
    bvcol = m("bvcol", [P, 1], F32)
    tmpc = m("tmpc", [P, 4 + H], F32)
    scale = float(DH) ** -0.5

    s_bank, st_bank, o_bank, misc = psum[0:2], psum[2:4], psum[4:6], psum[6:8]

    c_in, w_qkv_in, gate_in, wo_in = (sem(n) for n in ("biases_loaded", "wqkv_loaded", "gates_loaded", "wo_loaded"))
    ident_ok = sem("ident_ready")
    ident_step = sem("ident_step")
    kones_ok = sem("kones_ready")
    const_ok, tanh_ok = sem("consts_ready"), sem("tanh_ready")
    cstep_a, cstep_v = sem("const_step_act"), sem("const_step_dve")
    wqk_ok = sem("wqk_reordered")
    stack_zero = sem("stacks_ready")
    x_in = [sem(f"x_in{i}") for i in range(2)]
    xr_in = [sem(f"xres_in{i}") for i in range(2)]
    stats_ok, mv_ok, var_ok, rstd_ok, xn_ok = (sem(n) for n in ("ln_stats", "ln_mv", "ln_var", "ln_rstd", "xn_ready"))
    t_mm, t_ev = sem("transposes_done"), sem("xcT_ready")
    qk_mm, ka_mm, v_mm = sem("qk_projected"), sem("ka_projected"), sem("v_projected")
    qk_hi, ka_hi, v_hi = sem("qk_hi"), sem("ka_hi"), sem("v_hi")
    qk_rest, ka_rest, v_rest = sem("qk_rest"), sem("ka_rest"), sem("v_rest")
    mid_ok, lo_ok, v_mid, v_ok = sem("mid_ready"), sem("lo_ready"), sem("v_mid"), sem("v_ready")
    scr = [sem(f"parts_stored{i}") for i in range(2)]
    stk = [sem(f"stack_loaded{i}") for i in range(2)]
    s_mm, mx_ok = sem("scores_for_max"), sem("max_taken")
    nm_hi, nm_ok, nm_mm, nm_ev = sem("nmax_hi"), sem("nmax_ready"), sem("nmax_transposed"), sem("nmaxT_ready")
    shift = sem("shift_rows_loaded")
    st_mm, ph_ok, pa_ok, pl_ok = sem("shifted_scores"), sem("p_hi_ready"), sem("p_ready"), sem("p_lo_ready")
    pv_ok, pd_ok = sem("pv_done"), sem("p_lo_by_dve")
    o_sum, o_red = sem("o_summed"), sem("o_reduced")
    rg_ok, on_ok, at_ok = sem("rgate_ready"), sem("onorm_ready"), sem("att_ready")
    at_mm, at_ev, wo_mm = sem("att_transposed"), sem("attT_ready"), sem("wo_done")
    xb_ok, bo_ok, x2_ok = sem("xres_biased"), sem("bo_row_scaled"), sem("x2_ready")
    x2_st = [sem(f"x2_stored{i}") for i in range(2)]

    x_v = x.rearrange("(n k) t d -> n t k d", k=CH)
    c_v = ctx.rearrange("(n k) t d -> n t k d", k=CH)
    x2_v = x2d.rearrange("(n k) t d -> n t k d", k=CH)
    parts_v = parts_d.rearrange("n a (d h) t -> n a d (h t)", d=DH)
    q_runs = ((0, (0, 0, 0)), (3, (1, 1)), (5, (2,)))
    k_runs = ((0, (0, 1, 2)), (3, (0, 1)), (5, (0,)))

    block = ctx_.enter_context(nc.Block())

    one = lambda a: a.rearrange("(a n) -> a n", a=1)

    def const_loads(sp):
        col = lambda a: a.rearrange("(n a) -> n a", a=1)
        turned = lambda a: a.rearrange("(h d a) -> d h a", d=DH, a=1)
        sp.dma_start(wqkv[:], v["Wqkv"].rearrange("d (o n) -> d o n", o=3)).then_inc(w_qkv_in, 16)
        sp.dma_start(wqkva[:], v["Wqkv_aux"].rearrange("d (o n) -> d o n", o=3)).then_inc(w_qkv_in, 16)
        for i, b in enumerate((turned(v["bqkv"][0:P]), turned(v["bqkv"][P:2 * P]), col(v["bqkv"][2 * P:3 * P]),
                               turned(v["bqkv_aux"][P:2 * P]), col(v["bqkv_aux"][2 * P:3 * P]))):
            sp.dma_start(bcol[:, i:i + 1], b, allow_slow_non_contiguous=True).then_inc(c_in, 16)

    def gate_loads(act):
        act.dma_start(gh[:], one(v["g_head"]).to_broadcast([P, H])).then_inc(gate_in, 16)
        act.dma_start(ghc[:].rearrange("p a -> p a"),
                      v["g_head"].rearrange("(h a b) -> h a b", a=1, b=1).to_broadcast([H, DH, 1])).then_inc(gate_in, 16)
        act.dma_start(tg_x[:], one(v["g_xattn"]).to_broadcast([P, 1])).then_inc(gate_in, 16)
        act.dma_start(tg_f[:], one(v["g_ffn"]).to_broadcast([P, 1])).then_inc(gate_in, 16)
        act.dma_start(wo[:], v["Wo"]).then_inc(wo_in, 16)
        act.dma_start(bo_row[:], one(v["bo"]).to_broadcast([P, P])).then_inc(wo_in, 16)

    @block.sync
    def _(sp):
        def load_x(n, i):
            wait(sp, t_ev, n - 1)
            sp.dma_start(xin[i][:], x_v[n]).then_inc(x_in[i], 16)
            sp.dma_start(cin[i][:], c_v[n]).then_inc(x_in[i], 16)

        def load_res(n, i):
            wait(sp, x2_ok, CH * (n - 1))
            sp.dma_start(xres[i][:], x_v[n]).then_inc(xr_in[i], 16)

        def store_parts(n, n2, i):
            wait(sp, lo_ok, n + 1)
            sp.dma_start(parts_d[n].rearrange("a p t -> p a t"),
                         parts[i][:].rearrange("p o a t -> p (o a) t")).then_inc(scr[i], 16)

        def load_stack(n, n2, i):
            wait(sp, st_mm, UNITS * CH * (n - 1))
            wait(sp, scr[i], 16 * (n2 + 1))
            for o in range(3):
                for slot, run in (k_runs if o else q_runs):
                    src = parts_v[n][o * PART + run[0]]
                    if o == 0:
                        src = src.unsqueeze(0).to_broadcast([len(run), DH, H * TC])
                    else:
                        src = parts_v[n][o * PART + run[0]:o * PART + run[0] + len(run)]
                    sp.dma_start(stack[i][o][slot * DH:(slot + len(run)) * DH, :, :].rearrange("p h t -> p (h t)"),
                                 src).then_inc(stk[i], 16)

        def shift_rows(b, k):
            wait(sp, nm_ev, b + 1)
            sp.dma_start(stack[k // CH][0][SHIFT:SHIFT + 4, :, (k % CH) * P:(k % CH + 1) * P],
                         nmaxT[:]).then_inc(shift, 16)

        def expert_weights(g, j):
            eg, pg = E // LOOPS, E // 2 // LOOPS
            if j == 0:
                for w, d in ((wg_raw, v["We_gate"]), (wu_raw, v["We_up"])):
                    sp.dma_start(w[:, bass.ds(eg * g, eg), :],
                                 d[bass.ds(eg * g, eg)].rearrange("e d f -> d e f")).then_inc(w_in[0], 16)
            else:
                wd_v = v["We_down"].rearrange("(p two) f d -> two f p d", two=2)
                for half in range(2):
                    sp.dma_start(wd_raw[half * F:(half + 1) * F, bass.ds(pg * g, pg), :],
                                 wd_v[half][:, bass.ds(pg * g, pg), :]).then_inc(w_in[0], 16)

        def small_weights(j):
            if j == 0:
                sp.dma_start(gw_in[:], v["gate_w"]).then_inc(g_in, 16)
                sp.dma_start(gbias[:], one(v["gate_bias"]).to_broadcast([P, E])).then_inc(g_in, 16)
            else:
                sp.dma_start(wg_raw[:, E, :], v["Ws_gate"]).then_inc(w_in[1], 16)
                sp.dma_start(wu_raw[:, E, :], v["Ws_up"]).then_inc(w_in[1], 16)
                sp.dma_start(wd_raw[0:F, E // 2, :], v["Ws_down"]).then_inc(w_in[1], 16)

        def store_x2(n, i):
            wait(sp, x2_ok, CH * (n + 1))
            sp.dma_start(x2_v[n], x2[i][:]).then_inc(x2_st[i], 16)

        load_x(0, 0)
        const_loads(sp)
        load_x(1, 1)
        load_res(0, 0)
        load_res(1, 1)
        store_parts(0, 0, 0)
        sp.wait_ge(stack_zero, 1)
        load_stack(0, 0, 0)
        load_x(2, 0)
        store_parts(1, 0, 1)
        shift_rows(0, 0)
        sp.wait_ge(stack_zero, 2)

        def body(g, last):
            for j in range(2):
                n, i = 2 * g + j, j
                first = isinstance(n, int) and n == 0
                more, more2 = not (last and j == 1), not last
                if more:
                    load_stack(n + 1, g + (j + 1) // 2, 1 - j)
                shift_rows(2 * n + 1, 2 * i + 1)
                if first:
                    sp.wait_ge(w_zero, 3)
                if not first:
                    store_x2(n - 1, 1 - j)
                    if more:
                        load_res(n + 1, 1 - j)
                if not isinstance(n, int) or n + 3 < NC:
                    load_x(n + 3, 1 - j)
                if more:
                    shift_rows(2 * n + 2, (2 * i + 2) % BODY)
                if more2:
                    store_parts(n + 2, g + 1, i)
                expert_weights(g, j)
                if isinstance(g, int) and g == 0:
                    small_weights(j)
                if last and j == 0:
                    for t in range(2):
                        sp.wait_ge(x2_st[t], 16)
                    sp.dma_start(xld[:], x2d.rearrange("(c k) t d -> c t k d", k=4)[0]).then_inc(xl_in, 16)

        body(0, False)
        with sp.Fori(1, LOOPS - 2) as g:
            body(g, False)
        body(LOOPS - 2, False)
        body(LOOPS - 1, True)
        store_x2(NC - 1, 1)
        for i in range(2):
            sp.wait_ge(x2_st[i], 16 * (NC // 2))

    @block.gpsimd
    def _(pool):
        pool.memset(ident[:], 0.0).then_inc(ident_step, 1)
        pool.wait_ge(ident_step, 1)
        pool.affine_select(out=ident[:], in_=ident[:], compare_op=ALU.not_equal, fill=1.0, base=0,
                           pattern=[[-1, P]], channel_multiplier=1).then_inc(ident_step, 1)
        pool.wait_ge(ident_step, 2)
        pool.tensor_copy(ident_bf[:], ident[:]).then_inc(ident_ok, 1)
        pool.memset(kones[:], 1.0).then_inc(kones_ok, 1)
        pool.memset(mhalf[:], -0.5).then_inc(kones_ok, 1)
        pool.wait_ge(kones_ok, 2)
        pool.affine_select(out=kones[:, 0:2], in_=kones[:, 0:2], compare_op=ALU.is_ge, fill=0.0,
                           base=SHIFT + 1, pattern=[[0, 2]], channel_multiplier=-1).then_inc(kones_ok, 1)
        pool.affine_select(out=kones[:, 2:4], in_=kones[:, 2:4], compare_op=ALU.is_ge, fill=0.0,
                           base=-SHIFT - 2, pattern=[[0, 2]], channel_multiplier=1).then_inc(kones_ok, 1)
        pool.memset(kones[:, 4:6], 0.0).then_inc(kones_ok, 1)
        pool.wait_ge(kones_ok, 5)
        pool.affine_select(out=kones[:, 0:2], in_=kones[:, 0:2], compare_op=ALU.is_ge, fill=0.0,
                           base=-SHIFT, pattern=[[0, 2]], channel_multiplier=1).then_inc(kones_ok, 1)
        for t in (V[0], V[1]):
            pool.memset(t[:], 1.0).then_inc(kones_ok, 1)
        pool.memset(wg_raw[:, E + 1, :], 0.0).then_inc(w_zero, 1)
        pool.memset(wu_raw[:, E + 1, :], 0.0).then_inc(w_zero, 1)
        pool.wait_ge(kones_ok, 8)
        pool.wait_ge(w_zero, 2)
        pool.memset(wd_raw[F:P, (E + 1) // 2, :], 0.0).then_inc(w_zero, 1)
        pool.wait_ge(w_zero, 3)

        def root(n):
            wait(pool, var_ok, n + 1)
            pool.tensor_tensor(rstd[:], var[:], mhalf[:], ALU.pow).then_inc(rstd_ok, 1)

        def bias_res(n, g, i):
            wait(pool, xr_in[i], 16 * (g + 1))
            pool.tensor_tensor(xres[i][:], xres[i][:], bo_row[:].unsqueeze(1).to_broadcast([P, CH, P]),
                               ALU.add).then_inc(xb_ok, 1)

        def low_part(b, u):
            wait(pool, pa_ok, UNITS * b + u + 1)
            wait(pool, pv_ok, UNITS * b + u + 1 - RP)
            pool.tensor_tensor(p_lo[u % RP][:], p_all[u % RP][:], p_hi[u % RP][:], ALU.subtract).then_inc(pl_ok, 1)

        def normalise(b):
            wait(pool, rg_ok, b + 1)
            pool.tensor_tensor(onorm[:], osum[:], rgate[:].unsqueeze(3).to_broadcast([P, 2, H, DH]),
                               ALU.mult).then_inc(on_ok, 1)
            wait(pool, on_ok, b + 1)
            wait(pool, at_mm, b)
            pool.tensor_tensor(att[:].rearrange("p (h d) -> p h d", h=H), onorm[:, 0], onorm[:, 1],
                               ALU.add).then_inc(at_ok, 1)

        root(0)
        root(1)
        pool.wait_ge(tanh_ok, 2)
        pool.wait_ge(wo_in, 32)
        pool.tensor_scalar(bo_row[:], bo_row[:], tg_x[:, 0:1], 1.0, ALU.mult, ALU.mult).then_inc(bo_ok, 1)
        pool.wait_ge(bo_ok, 1)

        def body(g, last):
            for k in range(BODY):
                b, n, i = BODY * g + k, 2 * g + k // CH, k // CH
                first = isinstance(b, int) and b == 0
                odd = k % CH
                for u in range(UNITS):
                    if u == 0 and not odd and not last:
                        root(n + 2)
                    if u == LOW_U and odd:
                        bias_res(n, g, i)
                    if u != LOW_U:
                        low_part(b, u)
                    if u == LAG and not first:
                        normalise(b - 1)

        body(0, False)
        with pool.Fori(1, LOOPS - 1) as g:
            body(g, False)
        body(LOOPS - 1, True)
        normalise(NB - 1)

    @block.scalar
    def _(act):
        gate_loads(act)
        by_width = lambda w: w.rearrange("p (h d) -> p d h", h=H)
        out_by_width = lambda w: w.rearrange("p (d h) -> p d h", h=H)
        act.wait_ge(w_qkv_in, 32)
        act.activation(out_by_width(wqk[:, 0, :]), by_width(wqkv[:, 0, :]), ACT.Copy).then_inc(wqk_ok, 1)
        act.activation(out_by_width(wqk[:, 1, :]), by_width(wqkv[:, 1, :]), ACT.Copy).then_inc(wqk_ok, 1)
        act.activation(out_by_width(wqk[:, 2, :]), by_width(wqkva[:, 1, :]), ACT.Copy).then_inc(wqk_ok, 1)
        act.wait_ge(gate_in, 64)
        act.activation(tmpc[:, 0:H], gh[:], ACT.Exp, scale=-1.0).then_inc(cstep_a, 1)
        act.activation(tmpc[:, H:H + 1], ghc[:], ACT.Exp, scale=-1.0).then_inc(cstep_a, 1)
        act.activation(tg_x[:], tg_x[:], ACT.Tanh).then_inc(tanh_ok, 1)
        act.activation(tg_f[:], tg_f[:], ACT.Tanh).then_inc(tanh_ok, 1)

        def evac_t(n, i):
            wait(act, t_mm, n + 1)
            act.activation(xcT[i][:].rearrange("p a t -> p (a t)"), misc[0][:], ACT.Copy).then_inc(t_ev, 1)

        def hi_qk(n, n2, i):
            wait(act, qk_mm, n + 1)
            wait(act, scr[i], 16 * n2)
            for o in range(2):
                ins = act.activation(parts[i][:, o, 0, :], misc[0][:, o * TC:(o + 1) * TC], ACT.Identity,
                                     bias=bcol[:, o:o + 1])
            ins.then_inc(qk_hi, 1)

        def hi_ka(n, i):
            wait(act, ka_mm, n + 1)
            act.activation(parts[i][:, 2, 0, :], misc[0][:, 0:TC], ACT.Identity, bias=bcol[:, 3:4]).then_inc(ka_hi, 1)

        def mid(n, i):
            wait(act, ka_rest, n + 1)
            act.activation(parts[i][:, :, 1, :], rest[:], ACT.Copy).then_inc(mid_ok, 1)

        def hi_v(n, i):
            wait(act, v_mm, n + 1)
            act.activation(V[i][:, :, :, 0:DH], misc[0][:].rearrange("p (a h d) -> p a h d", h=H, d=DH),
                           ACT.Copy).then_inc(v_hi, 1)

        def mid_v(n, i):
            wait(act, v_rest, n + 1)
            act.activation(V[i][:, :, :, DH:2 * DH], vrest[:].rearrange("p a (h d) -> p a h d", d=DH),
                           ACT.Copy).then_inc(v_mid, 1)

        def exps(b, u):
            wait(act, st_mm, UNITS * b + u + 1)
            wait(act, pv_ok, UNITS * b + u + 1 - RP)
            act.activation(p_hi[u % RP][:], st_bank[u % 2][:], ACT.Exp, scale=scale).then_inc(ph_ok, 1)
            act.activation(p_all[u % RP][:], st_bank[u % 2][:], ACT.Exp, scale=scale).then_inc(pa_ok, 1)

        def evac_att(b):
            wait(act, at_mm, b + 1)
            wait(act, wo_mm, b)
            act.activation(attT[:], misc[1][:, 0:P], ACT.Identity, bias=bvcol[:, 0:1]).then_inc(at_ev, 1)

        act.wait_ge(kones_ok, 6)
        for n in range(2):
            evac_t(n, n)
            if n == 0:
                act.wait_ge(c_in, 16 * 5)
            hi_qk(n, 0, n)
            hi_ka(n, n)
            mid(n, n)
            if n == 0:
                hi_v(0, 0)
                mid_v(0, 0)
        act.wait_ge(const_ok, 1)

        def body(g, last):
            for k in range(BODY):
                b, n, i, odd = BODY * g + k, 2 * g + k // CH, k // CH, k % CH
                first = isinstance(b, int) and b == 0
                more = not (last and i == 1)
                for u in range(UNITS):
                    exps(b, u)
                    if not last:
                        if u == 3 and not odd:
                            evac_t(n + 2, i)
                        if u == 6 and not odd:
                            hi_qk(n + 2, g + 1, i)
                        if u == 0 and odd:
                            hi_ka(n + 2, i)
                        if u == 2 and odd:
                            mid(n + 2, i)
                    if u == 4 and odd and more:
                        hi_v(n + 1, (i + 1) % 2)
                    if u == 7 and odd and more:
                        mid_v(n + 1, (i + 1) % 2)
                    if u == 7 and not first:
                        evac_att(b - 1)

        body(0, False)
        with act.Fori(1, LOOPS - 1) as g:
            body(g, False)
        body(LOOPS - 1, True)
        evac_att(NB - 1)

    @block.vector
    def _(dve):
        nc.vector.memset(nmax[:], 0.0)
        nc.vector.memset(tick[:], 0.0)
        nc.vector.memset(mx[0][:], 0.0).then_inc(cstep_v, 1)

        def clear_stack(i):
            dve.wait_ge(kones_ok, 6)
            for o in range(3):
                col = 2 * ((o - 1) % 3)
                ins = nc.vector.tensor_copy(stack[i][o][:].rearrange("p h t -> p (h t)").bitcast(F32),
                                            kones[:, col:col + 2].bitcast(F32).to_broadcast([P, H * TC // 2]))
            ins.then_inc(stack_zero, 1)

        def gate_consts():
            dve.wait_ge(cstep_a, 2)
            nc.vector.tensor_scalar(tmpc[:, 0:H + 1], tmpc[:, 0:H + 1], 1.0, None, ALU.add).then_inc(cstep_v, 1)
            dve.wait_ge(cstep_v, 2)
            nc.vector.reciprocal(gcoef[:, 1, :], tmpc[:, 0:H]).then_inc(cstep_v, 1)
            nc.vector.reciprocal(gcol[:, 0:1], tmpc[:, H:H + 1]).then_inc(cstep_v, 1)
            dve.wait_ge(cstep_v, 4)
            nc.vector.tensor_scalar(gcoef[:, 0, :], gcoef[:, 1, :], -1.0, 1.0, ALU.mult, ALU.add).then_inc(cstep_v, 1)
            nc.vector.tensor_scalar(gcol[:, 1:2], gcol[:, 0:1], -1.0, 1.0, ALU.mult, ALU.add).then_inc(cstep_v, 1)
            dve.wait_ge(cstep_v, 6)
            nc.vector.tensor_scalar(bvcol[:], bcol[:, 4:5], gcol[:, 0:1], None, ALU.mult).then_inc(cstep_v, 1)
            dve.wait_ge(cstep_v, 7)
            nc.vector.scalar_tensor_tensor(out=bvcol[:], in0=bcol[:, 2:3], scalar=gcol[:, 1:2], in1=bvcol[:],
                                           op0=ALU.mult, op1=ALU.add).then_inc(const_ok, 1)

        def norm_stats(n, n2, i):
            wait(dve, x_in[i], 32 * (n2 + 1))
            for c in range(CH):
                ins = nc.vector.bn_stats(stats[:, c, :], xin[i][:, c, :])
            ins.then_inc(stats_ok, 1)
            wait_tick(nc, stats_ok, n + 1, tick)
            for c in range(CH):
                ins = nc.vector.bn_aggr(mv[:, c, :], stats[:, c, :])
            ins.then_inc(mv_ok, 1)
            wait(dve, mv_ok, n + 1)
            nc.vector.tensor_scalar(var[:], mv[:, :, 1], EPS, None, ALU.add).then_inc(var_ok, 1)

        def norm(n, i):
            wait(dve, rstd_ok, n + 1)
            wait(dve, t_mm, n)
            for c in range(CH):
                ins = nc.vector.tensor_scalar(xn[:, c, :], xin[i][:, c, :], mv[:, c, 0:1], rstd[:, c:c + 1],
                                              ALU.subtract, ALU.mult)
            ins.then_inc(xn_ok, 1)

        def rest_qk(n, i):
            wait(dve, qk_hi, n + 1)
            wait(dve, lo_ok, n)
            wait(dve, mid_ok, n)
            for o in range(2):
                ins = nc.vector.scalar_tensor_tensor(
                    out=rest[:, o, :], in0=misc[0][:, o * TC:(o + 1) * TC], scalar=bcol[:, o:o + 1],
                    in1=parts[i][:, o, 0, :], op0=ALU.add, op1=ALU.subtract)
            ins.then_inc(qk_rest, 1)

        def rest_ka(n, i):
            wait(dve, ka_hi, n + 1)
            nc.vector.scalar_tensor_tensor(
                out=rest[:, 2, :], in0=misc[0][:, 0:TC], scalar=bcol[:, 3:4],
                in1=parts[i][:, 2, 0, :], op0=ALU.add, op1=ALU.subtract).then_inc(ka_rest, 1)

        def low(n, i):
            wait(dve, mid_ok, n + 1)
            wait(dve, ka_rest, n + 1)
            nc.vector.tensor_tensor(parts[i][:, :, 2, :], rest[:], parts[i][:, :, 1, :],
                                    ALU.subtract).then_inc(lo_ok, 1)

        def rest_v(n, i):
            wait(dve, v_hi, n + 1)
            nc.vector.tensor_tensor(vrest[:].rearrange("p a (h d) -> p (a h) d", d=DH),
                                    misc[0][:].rearrange("p (a h d) -> p (a h) d", h=H, d=DH),
                                    V[i][:, :, :, 0:DH].rearrange("p a h d -> p (a h) d"),
                                    ALU.subtract).then_inc(v_rest, 1)

        def low_v(n, i):
            wait(dve, v_mid, n + 1)
            wait(dve, v_rest, n + 1)
            nc.vector.tensor_tensor(V[i][:, :, :, 2 * DH:3 * DH].rearrange("p a h d -> p (a h) d"),
                                    vrest[:].rearrange("p a (h d) -> p (a h) d", d=DH),
                                    V[i][:, :, :, DH:2 * DH].rearrange("p a h d -> p (a h) d"),
                                    ALU.subtract).then_inc(v_ok, 1)

        def maxima(b, par, u):
            wait(dve, s_mm, UNITS * b + u + 1)
            if u == 0:
                wait(dve, nm_ok, b - 1)
            a, h0 = u // (UNITS // 2), (u % (UNITS // 2)) * HPU
            nc.vector.tensor_reduce(mx[par][:, a, h0:h0 + HPU], s_bank[u % 2][:].rearrange("p (h k) -> p h k", h=HPU),
                                    AXX, ALU.max).then_inc(mx_ok, 1)

        def minus_max(b, par):
            wait(dve, mx_ok, UNITS * (b + 1))
            wait(dve, nm_mm, b)
            nc.vector.tensor_scalar(nmax[:, 0:2, 0, :], mx[par][:], -1.0, None, ALU.mult).then_inc(nm_hi, 1)
            wait(dve, nm_hi, b + 1)
            nc.vector.scalar_tensor_tensor(out=nmax[:, 0:2, 1, :], in0=mx[par][:], scalar=-1.0,
                                           in1=nmax[:, 0:2, 0, :], op0=ALU.mult, op1=ALU.subtract).then_inc(nm_ok, 1)

        def evac_nmax(b):
            wait(dve, nm_mm, b + 1)
            wait(dve, shift, 16 * b)
            nc.vector.tensor_copy(nmaxT[:], misc[1][0:4 * H, 0:P // 2].bitcast(BF16)).then_inc(nm_ev, 1)

        def sums(b, a):
            wait(dve, pv_ok, UNITS * b + (UNITS // 2) * (a + 1))
            wait(dve, on_ok, b)
            o = o_bank[a][:, 0:H * VC].rearrange("p (h c) -> p h c", h=H)
            nc.vector.tensor_reduce(osum[:, a], o[:, :, 0:PART * DH].rearrange("p h (s d) -> p h d s", s=PART),
                                    AXX, ALU.add)
            nc.vector.reciprocal(rden[:, a, :], o[:, :, VC - 1]).then_inc(o_red, 1)
            if a == 1:
                wait(dve, o_red, 2 * b + 2)
                nc.vector.tensor_tensor(rgate[:], rden[:], gcoef[:], ALU.mult).then_inc(rg_ok, 1)

        def low_unit(b):
            wait(dve, pa_ok, UNITS * b + LOW_U + 1)
            wait(dve, pv_ok, UNITS * b + LOW_U + 1 - RP)
            nc.vector.tensor_tensor(p_lo[LOW_U % RP][:], p_all[LOW_U % RP][:], p_hi[LOW_U % RP][:],
                                    ALU.subtract).then_inc(pd_ok, 1)

        def residual(b, n, i, odd):
            wait(dve, wo_mm, b + 1)
            wait(dve, xb_ok, n + 1)
            if not odd:
                wait(dve, x2_st[i], 8 * (n - i))
            nc.vector.scalar_tensor_tensor(out=x2[i][:, odd, :], in0=misc[1][:, 0:P], scalar=tg_x[:, 0:1],
                                           in1=xres[i][:, odd, :], op0=ALU.mult, op1=ALU.add).then_inc(x2_ok, 1)

        for n in range(2):
            norm_stats(n, 0, n)
            norm(n, n)
            clear_stack(n)
            if n == 0:
                dve.wait_ge(c_in, 16 * 5)
                gate_consts()
                dve.wait_ge(tanh_ok, 2)
            rest_qk(n, n)
            rest_ka(n, n)
            low(n, n)
            if n == 0:
                rest_v(0, 0)
                low_v(0, 0)
        for u in range(UNITS):
            maxima(0, 0, u)
        minus_max(0, 0)
        evac_nmax(0)
        for u in range(FIRST_ODD):
            maxima(1, 1, u)

        def body(g, last):
            for k in range(BODY):
                b, n, i, odd = BODY * g + k, 2 * g + k // CH, k // CH, k % CH
                first = isinstance(b, int) and b == 0
                more = not (last and i == 1)
                ahead = not (last and k == BODY - 1)
                for u in range(UNITS):
                    if u == 0 and not odd and not last:
                        norm_stats(n + 2, g + 1, i)
                    if u == 1 and not odd and not last:
                        norm(n + 2, i)
                    if u == 4 and ahead:
                        evac_nmax(b + 1)
                    for db, nu in S_PLAN[UNITS * odd + u]:
                        if db == 0 or more:
                            maxima(b - odd + 1 + db, (1 + db) % 2, nu)
                    if u == 1 and not (isinstance(b, int) and b < 2):
                        residual(b - 2, n - 1, 1 - i, odd)
                    if u == 0 and not first:
                        sums(b - 1, 0)
                    if u == LAG and not first:
                        sums(b - 1, 1)
                    if u == LOW_U + 1:
                        low_unit(b)
                    if u == 2 and ahead:
                        minus_max(b + 1, 1 - odd)
                    if not last:
                        if u == 7 and not odd:
                            rest_qk(n + 2, i)
                        if u == 1 and odd:
                            rest_ka(n + 2, i)
                        if u == 3 and odd:
                            low(n + 2, i)
                    if u == 5 and odd and more:
                        rest_v(n + 1, (i + 1) % 2)
                    if u == 0 and not odd and not first:
                        low_v(n, i)

        body(0, False)
        with dve.Fori(1, LOOPS - 1) as g:
            body(g, False)
        body(LOOPS - 1, True)
        sums(NB - 1, 0)
        sums(NB - 1, 1)
        residual(NB - 2, NC - 1, 1, 0)
        residual(NB - 1, NC - 1, 1, 1)

    @block.tensor
    def _(pe):
        def transposes(n, n2, i):
            wait(pe, xn_ok, n + 1)
            wait(pe, x_in[i], 32 * (n2 + 1))
            for c in range(CH):
                nc.tensor.transpose(misc[0][:, c * P:(c + 1) * P], xn[:, c, :], ident[:])
            for c in range(CH):
                ins = nc.tensor.transpose(misc[0][:, TC + c * P:TC + (c + 1) * P], cin[i][:, c, :], ident[:])
            ins.then_inc(t_mm, 1)

        def project_qk(n, i, o):
            wait(pe, t_ev, n + 1)
            ins = nc.tensor.matmul(misc[0][:, o * TC:(o + 1) * TC], wqk[:, o, :], xcT[i][:, 0, :],
                                   start=True, stop=True)
            if o == 1:
                ins.then_inc(qk_mm, 1)

        def project_ka(n, i):
            nc.tensor.matmul(misc[0][:, 0:TC], wqk[:, 2, :], xcT[i][:, 1, :],
                             start=True, stop=True).then_inc(ka_mm, 1)

        def project_v(n, i, a):
            for c in range(CH):
                o = (a * CH + c) * P
                ins = nc.tensor.matmul(misc[0][:, o:o + P], xcT[i][:, a, c * P:(c + 1) * P],
                                       (wqkv, wqkva)[a][:, 2, :], start=True, stop=True)
            if a == 1:
                ins.then_inc(v_mm, 1)

        def scores(b, k, u, n2):
            i, c = k // CH, k % CH
            if u == 0:
                wait(pe, stk[i], 16 * 3 * len(q_runs) * (n2 + 1))
            wait(pe, mx_ok, UNITS * b + u - 1)
            q, kk = stack[i][0], stack[i][1 + u // (UNITS // 2)]
            for j in range(HPU):
                h = (u % (UNITS // 2)) * HPU + j
                ins = nc.tensor.matmul(s_bank[u % 2][:, j * P:(j + 1) * P], q[0:ROWS_S, h, c * P:(c + 1) * P],
                                       kk[0:ROWS_S, h, c * P:(c + 1) * P], start=True, stop=True)
            ins.then_inc(s_mm, 1)

        def shifted(b, k, u):
            i, c = k // CH, k % CH
            if u == 0:
                wait(pe, shift, 16 * (b + 1))
            wait(pe, pa_ok, UNITS * b + u - 1)
            q, kk = stack[i][0], stack[i][1 + u // (UNITS // 2)]
            for j in range(HPU):
                h = (u % (UNITS // 2)) * HPU + j
                ins = nc.tensor.matmul(st_bank[u % 2][:, j * P:(j + 1) * P], kk[0:ROWS_ST, h, c * P:(c + 1) * P],
                                       q[0:ROWS_ST, h, c * P:(c + 1) * P], start=True, stop=True)
            ins.then_inc(st_mm, 1)

        def weighted(b, k, u, n):
            i, c = k // CH, k % CH
            a = u // (UNITS // 2)
            if u == LOW_U:
                wait(pe, pd_ok, b + 1)
            else:
                wait(pe, pl_ok, (UNITS - 1) * b + u + (u < LOW_U))
            if u == 0:
                wait(pe, v_ok, n + 1)
                wait(pe, o_red, 2 * b - 1)
            if u == UNITS // 2:
                wait(pe, o_red, 2 * b)
            for j in range(HPU):
                h = (u % (UNITS // 2)) * HPU + j
                o = o_bank[a][:, h * VC:(h + 1) * VC]
                nc.tensor.matmul(o, p_hi[u % RP][:, j * P:(j + 1) * P], V[i][:, a * CH + c, h, :],
                                 start=True, stop=False)
                ins = nc.tensor.matmul(o, p_lo[u % RP][:, j * P:(j + 1) * P], V[i][:, a * CH + c, h, :],
                                       start=False, stop=True)
            ins.then_inc(pv_ok, 1)

        def turn_att(b):
            wait(pe, at_ok, b + 1)
            nc.tensor.transpose(misc[1][:, 0:P], att[:], ident[:]).then_inc(at_mm, 1)

        def out_proj(b):
            wait(pe, at_ev, b + 1)
            nc.tensor.matmul(misc[1][:, 0:P], attT[:], wo[:], start=True, stop=True).then_inc(wo_mm, 1)

        def turn_max(b):
            wait(pe, nm_ok, b + 1)
            nc.tensor.transpose(misc[1][:, 0:P // 2].bitcast(BF16),
                                nmax[:].rearrange("p a s h -> p (a s h)"), ident_bf[:]).then_inc(nm_mm, 1)

        pe.wait_ge(ident_ok, 1)
        for n in range(2):
            if n == 1:
                pe.wait_ge(v_rest, 1)
            transposes(n, 0, n)
            pe.wait_ge(wqk_ok, 3)
            project_qk(n, n, 0)
            project_qk(n, n, 1)
            pe.wait_ge(qk_rest, n + 1)
            project_ka(n, n)
            if n == 0:
                pe.wait_ge(ka_rest, 1)
                project_v(0, 0, 0)
                project_v(0, 0, 1)
        pe.wait_ge(stack_zero, 2)
        for u in range(UNITS):
            scores(0, 0, u, 0)
        turn_max(0)
        pe.wait_ge(wo_in, 32)
        for u in range(FIRST_ODD):
            scores(1, 1, u, 0)

        def body(g, last):
            for k in range(BODY):
                b, n, i, odd = BODY * g + k, 2 * g + k // CH, k // CH, k % CH
                first, second = isinstance(b, int) and b == 0, isinstance(b, int) and b < 2
                more = not (last and i == 1)
                ahead = not (last and k == BODY - 1)
                for u in range(UNITS):
                    shifted(b, k, u)
                    for db, nu in S_PLAN[UNITS * odd + u]:
                        if db == 0 or more:
                            kk = k - odd + 1 + db
                            scores(b - odd + 1 + db, kk % BODY, nu, g + kk // BODY)
                    if u >= LAG:
                        weighted(b, k, u - LAG, n)
                    elif not first:
                        weighted(b - 1, (k - 1) % BODY, u + UNITS - LAG, n if odd else n - 1)
                    if u == 1 and not second:
                        out_proj(b - 2)
                    if u == 4 and ahead:
                        if second:
                            wait(pe, nm_ev, b + 1)
                        else:
                            wait(pe, x2_ok, b - 1)
                        turn_max(b + 1)
                    if u == 7 and not first:
                        if ahead:
                            wait(pe, nm_ev, b + 2)
                        else:
                            wait(pe, x2_ok, b - 1)
                        turn_att(b - 1)
                    if not odd and not last:
                        if u == 3:
                            wait(pe, v_rest, n + 1)
                            transposes(n + 2, g + 1, i)
                        if u in (5, 6):
                            project_qk(n + 2, i, u - 5)
                    if u == 0 and odd and not last:
                        wait(pe, qk_rest, n + 3)
                        project_ka(n + 2, i)
                    if u in (3, 4) and odd and more:
                        if u == 3 and not last:
                            wait(pe, ka_rest, n + 3)
                        project_v(n + 1, (i + 1) % 2, u - 3)

        body(0, False)
        with pe.Fori(1, LOOPS - 1) as g:
            body(g, False)
        body(LOOPS - 1, True)
        for u in range(LAG):
            weighted(NB - 1, BODY - 1, u + UNITS - LAG, NC - 1)
        out_proj(NB - 2)
        pe.wait_ge(x2_ok, NB - 1)
        turn_att(NB - 1)
        out_proj(NB - 1)


S_PLAN = (((0, 5),), ((0, 6),), ((0, 7),), (), (), (), ((1, 0), (1, 1)), ((1, 2), (1, 3)),
          ((1, 4),), ((1, 5), (1, 6)), ((1, 7),), ((2, 0),), ((2, 1),), ((2, 2),), ((2, 3),), ((2, 4),))
FIRST_ODD = 5


def experts(nc, ctx_, sem, m, r, psum, v):
    tick = v["tick"]
    x2d, out, ident, tg_f = v["x2d"], v["out"], v["ident"], v["tg_f"]
    wg_raw, wu_raw, wd_raw, w_in, w_zero = v["wg_raw"], v["wu_raw"], v["wd_raw"], v["w_in"], v["w_zero"]
    NEX, NP, NB = v["NEX"], v["NP"], v["NB"]
    gw_in, gbias, g_in, xl_in = v["gw_in"], v["gbias"], v["g_in"], v["xl_in"]
    K = 4
    T = K * P
    NCH = NB // K
    LOOPS = NCH // 2
    LAG = 4
    GP = 3
    GROUPS = NP // GP
    EPG = E // NG
    RS, RH = 3, 6

    wg = [m(f"wg_{s}", [P, NEX, F], F32R) for s in ("hi", "lo")]
    wu = [m(f"wu_{s}", [P, NEX, F], F32R) for s in ("hi", "lo")]
    wd = [m(f"wd_{s}", [P, NP, P], F32R) for s in ("hi", "lo")]
    xld = v["xld"]
    x2c = m("x2c", [P, K, P], F32)
    xhi = [m(f"xhi{i}", [P, T], F32R) for i in range(2)]
    xlo = [m(f"xlo{i}", [P, T], F32R) for i in range(2)]
    hhi = [m(f"hhi{i}", [P, T], F32R) for i in range(RH)]
    hlo = [m(f"hlo{i}", [P, T], F32R) for i in range(RH)]
    xn = m("xn2", [P, K, P], F32)
    xT = m("xT2", [P, T], F32)
    wT = m("wT", [NEX, T], F32)
    stats = m("stats2", [P, K, 6], F32)
    mv = m("mv2", [P, K, 2], F32)
    var = m("var2", [P, K], F32)
    rstd = m("rstd2", [P, K], F32)
    mhalf = m("mhalf2", [P, K], F32)
    gwT = m("gwT", [P, E], F32)
    tri = m("tri", [P, NG, NG], F32)
    s_buf = [r(f"silu{i}", [P, T], F32) for i in range(RS)]
    a_buf = [r(f"act{i}", [P, T], F32) for i in range(RS)]
    h_buf = [r(f"hid{i}", [P, T], F32) for i in range(RS)]
    cwb = [r(f"cwb{i}", [P, GP, T], F32) for i in range(2)]
    ysb = r("ysb", [P, T], F32)
    osb = [r(f"osb{i}", [P, K, P], F32) for i in range(2)]
    sig = m("sig", [P, K, E], F32)
    sc = m("sc", [P, K, E], F32)
    top_a, low_a = m("top_a", [P, K * NG, 4], F32), m("low_a", [P, K * NG, 4], F32)
    top_b, low_b, mid_b = (m(f"{n}_b", [P, K * NG, 2], F32) for n in ("top", "low", "mid"))
    top_c, low_c, mid_c = (m(f"{n}_c", [P, K * NG, 1], F32) for n in ("top", "low", "mid"))
    gs = m("gs", [P, K, NG], F32)
    gt = m("gt", [P, K, NG, NG], F32)
    eq = m("eq", [P, K, NG, NG], F32)
    rank = m("rank", [P, K, NG], F32)
    gm = m("gm", [P, K, NG], F32)
    pen = m("pen", [P, K, NG], F32)
    masked = m("masked", [P, K, E], F32)
    best = m("best", [P, K, TK], F32)
    rep = m("rep", [P, K, E], F32)
    wsel = m("wsel", [P, K, E], F32)
    wsum = m("wsum", [P, K], F32)
    wnorm = m("wnorm", [P, K, E], F32)

    g_bank, u_bank, y_bank, misc = psum[0:2], psum[2:5], psum[5:7], psum[7]
    wts_d = nc.dram_tensor("wts_scratch", (NCH, NEX, T), F32, kind="Internal").ap()
    wts_v = wts_d.rearrange("c (p two) t -> c two p t", two=2)
    x2_v = x2d.rearrange("(c k) t d -> c t k d", k=K)
    out_v = out.rearrange("(c k) t d -> c t k d", k=K)

    c_ok = sem("expert_consts")
    gw_mm, gw_ev = sem("gate_w_transposed"), sem("gate_wT_ready")
    cv_hi, dl_ok = sem("weights_hi"), sem("down_lo")
    gl_dve, gl_pool = sem("gate_up_lo_by_dve"), sem("gate_up_lo_by_pool")
    x2_in = sem("x2_loaded_for_residual")
    st_ok, mv_ok, var_ok, rstd_ok, xn_ok = (sem(f"{n}_2") for n in ("ln_stats", "ln_mv", "ln_var", "ln_rstd", "xn"))
    xt_mm, xhi_ok, xT_ok, xlo_ok = sem("x2_transposed"), sem("xhi_ready"), sem("xT_ready"), sem("xlo_ready")
    lg_mm, sig_ok, rt, w_ok = sem("logits"), sem("sigmoids"), sem("route_step"), sem("route_weights")
    rd_ok = sem("route_denominators")
    wt_mm, wt_ev, wt_st = sem("weights_transposed"), sem("wT_ready"), sem("wT_stored")
    cw_in = [sem(f"cwb_loaded{i}") for i in range(2)]
    g_mm, u_mm, s_ok, a_ok, h_ok = (sem(n) for n in ("gate_mm", "up_mm", "silu_ready", "act_ready", "hid_ready"))
    hh_ok, hl_ok, dn_mm = sem("hid_hi"), sem("hid_lo"), sem("down_mm")
    y_ev, yt_mm, out_ok = sem("y_copied"), sem("y_transposed"), sem("out_ready")
    o_st = [sem(f"out_stored{i}") for i in range(2)]

    P_STAT, P_NORM, P_TURN, P_OPER, P_LOGIT, P_SIG, P_ROUTE, P_WT, P_WEV = 2, 3, 5, 6, 7, 8, 9, 27, 28
    F_COPY, F_TURN, F_OUT, F_GROUP = LAG + 1, LAG + 5, LAG + 6, 5
    ROUTE_PARTS = 17
    EARLY = 1
    CONV = 3
    GU_DVE, GU_POOL = (2, 3), (0, 1, 4, 5)
    R_STEPS = 26

    block = ctx_.enter_context(nc.Block())

    def gu_slice(k):
        e0, e1 = (k // 2) * NEX // CONV, (k // 2 + 1) * NEX // CONV
        raw, parts = ((wg_raw, wg), (wu_raw, wu))[k % 2]
        return raw[:, e0:e1, :], parts[0][:, e0:e1, :], parts[1][:, e0:e1, :]

    def down_slice(k):
        q0, q1 = k * NP // CONV, (k + 1) * NP // CONV
        return wd_raw[:, q0:q1, :], wd[0][:, q0:q1, :], wd[1][:, q0:q1, :]

    def gate_up_free(eng):
        eng.wait_ge(gl_dve, len(GU_DVE))
        eng.wait_ge(gl_pool, len(GU_POOL))

    @block.sync
    def _(sp):
        def load_norm(c):
            wait(sp, xn_ok, c)
            sp.dma_start(xld[:], x2_v[c]).then_inc(xl_in, 16)

        def load_res(c):
            wait(sp, out_ok, c)
            sp.dma_start(x2c[:], x2_v[c]).then_inc(x2_in, 16)

        def store_w(c):
            wait(sp, wt_ev, c + 1)
            sp.dma_start(wts_d[c], wT[:]).then_inc(wt_st, 16)
            wait(sp, wt_st, 16 * c + 16)

        def load_cwb(c, gr, slot):
            wait(sp, h_ok, NP * c + GP * (gr - 1))
            for half in range(2):
                sp.dma_start(cwb[slot][half * F:(half + 1) * F, :, :],
                             wts_v[c][half][GP * gr:GP * (gr + 1)].unsqueeze(0).to_broadcast([F, GP, T])
                             ).then_inc(cw_in[slot], 16)

        def store_out(c, i):
            wait(sp, out_ok, c + 1)
            sp.dma_start(out_v[c], osb[i][:]).then_inc(o_st[i], 16)

        load_res(0)
        load_norm(1)
        store_w(0)
        gate_up_free(sp)
        load_cwb(0, 0, 0)
        load_cwb(0, 1, 1)

        def body(g, last):
            for j in range(2):
                c = 2 * g + j
                first = isinstance(c, int) and c == 0
                more = not (last and j == 1)
                for gr in range(2, GROUPS):
                    load_cwb(c, gr, (GROUPS * j + gr) % 2)
                    if gr == F_GROUP:
                        if not first:
                            store_out(c - 1, 1 - j)
                            load_res(c)
                        if not last:
                            load_norm(c + 2)
                if more:
                    store_w(c + 1)
                    for gr in range(2):
                        load_cwb(c + 1, gr, (GROUPS * (j + 1) + gr) % 2)

        body(0, False)
        with sp.Fori(1, LOOPS - 1) as g:
            body(g, False)
        body(LOOPS - 1, True)
        store_out(NCH - 1, 1)
        for i in range(2):
            sp.wait_ge(o_st[i], 16 * (NCH // 2))

    @block.gpsimd
    def _(pool):
        pool.memset(mhalf[:], -0.5).then_inc(c_ok, 1)
        pool.wait_ge(c_ok, 1)
        pool.memset(wT[E:NEX, :], 1.0).then_inc(c_ok, 1)
        pool.wait_ge(c_ok, 2)
        pool.memset(tri[:], 1.0).then_inc(c_ok, 1)
        pool.wait_ge(c_ok, 3)
        pool.affine_select(out=tri[:], in_=tri[:], compare_op=ALU.is_gt, fill=0.0, base=0,
                           pattern=[[1, NG], [-1, NG]], channel_multiplier=0).then_inc(c_ok, 1)

        def root(c):
            wait(pool, var_ok, c + 1)
            pool.tensor_tensor(rstd[:], var[:], mhalf[:], ALU.pow).then_inc(rstd_ok, 1)

        def hidden(n, q, j, g):
            slot = (GROUPS * j + q // GP) % 2
            wait(pool, a_ok, n + 1)
            if q % GP == 0:
                wait(pool, cw_in[slot], 32 * (GROUPS * g + (GROUPS * j + q // GP) // 2 + 1))
            wait(pool, hl_ok, n + 1 - RS)
            k = (NP * j + q) % RS
            pool.tensor_tensor(h_buf[k][:], a_buf[k][:], cwb[slot][:, q % GP, :], ALU.mult).then_inc(h_ok, 1)

        root(0)
        for k in GU_POOL:
            wait(pool, cv_hi, k + 1)
            src, hi, lo = gu_slice(k)
            pool.tensor_tensor(lo, src, hi.bitcast(F32), ALU.subtract).then_inc(gl_pool, 1)
        gate_up_free(pool)

        def body(g, last):
            for j in range(2):
                c = 2 * g + j
                for q in range(NP):
                    hidden(NP * c + q, q, j, g)
                    if q == P_STAT and not (last and j == 1):
                        root(c + 1)

        body(0, False)
        with pool.Fori(1, LOOPS - 1) as g:
            body(g, False)
        body(LOOPS - 1, True)

    @block.scalar
    def _(act):
        def operands(c, i):
            wait(act, xt_mm, c + 1)
            wait(act, u_mm, NP * (c - 1))
            act.activation(xhi[i][:], misc[:], ACT.Copy).then_inc(xhi_ok, 1)
            wait(act, lg_mm, c)
            act.activation(xT[:], misc[:], ACT.Copy).then_inc(xT_ok, 1)

        def sigmoids(c):
            wait(act, lg_mm, c + 1)
            wait(act, w_ok, c)
            act.activation(sig[:].rearrange("p k e -> p (k e)"), misc[:, 0:K * E], ACT.Sigmoid).then_inc(sig_ok, 1)

        def evac_w(c):
            wait(act, wt_mm, c + 1)
            wait(act, wt_st, 16 * c)
            act.activation(wT[0:E, :], misc[0:E, :], ACT.Copy).then_inc(wt_ev, 1)

        def silu(n, k):
            wait(act, g_mm, n + 1)
            wait(act, a_ok, n + 1 - RS)
            act.activation(s_buf[k % RS][:], g_bank[k % 2][:], ACT.Silu).then_inc(s_ok, 1)

        def hid_hi(n, k):
            wait(act, h_ok, n + 1)
            wait(act, dn_mm, n + 1 - RH)
            act.activation(hhi[k % RH][:], h_buf[k % RS][:], ACT.Copy).then_inc(hh_ok, 1)

        def copy_y(c, i):
            wait(act, dn_mm, NP * (c + 1))
            wait(act, yt_mm, c)
            act.activation(ysb[:], y_bank[i][:], ACT.Copy).then_inc(y_ev, 1)

        act.wait_ge(gw_mm, 1)
        act.activation(gwT[:], misc[:, 0:E], ACT.Copy).then_inc(gw_ev, 1)
        act.wait_ge(w_zero, 3)
        act.wait_ge(w_in[0], 16 * 4 * v["BODIES"])
        act.wait_ge(w_in[1], 16 * 3)
        for k in range(3 * CONV):
            src, hi, _ = gu_slice(k) if k < 2 * CONV else down_slice(k - 2 * CONV)
            act.activation(hi, src, ACT.Copy).then_inc(cv_hi, 1)
            if k == 3:
                operands(0, 0)
            if k == 4:
                sigmoids(0)
        gate_up_free(act)

        def body(g, last):
            for j in range(2):
                c = 2 * g + j
                first = isinstance(c, int) and c == 0
                more = not (last and j == 1)
                for q in range(NP):
                    n, k = NP * c + q, NP * j + q
                    if first and q == EARLY:
                        evac_w(0)
                    silu(n, k)
                    if not (first and q < 2):
                        hid_hi(n - 2, k - 2)
                    if q == F_COPY and not first:
                        copy_y(c - 1, 1 - j)
                    if more:
                        if q == P_OPER:
                            operands(c + 1, 1 - j)
                        if q == P_SIG:
                            sigmoids(c + 1)
                        if q == P_WEV:
                            evac_w(c + 1)

        body(0, False)
        with act.Fori(1, LOOPS - 1) as g:
            body(g, False)
        body(LOOPS - 1, True)
        for q in range(2):
            hid_hi(NP * NCH - 2 + q, 2 * NP - 2 + q)
        copy_y(NCH - 1, 1)

    @block.vector
    def _(dve):
        def norm_stats(c):
            wait(dve, xl_in, 16 * (c + 1))
            for k in range(K):
                ins = nc.vector.bn_stats(stats[:, k, :], xld[:, k, :])
            ins.then_inc(st_ok, 1)
            wait_tick(nc, st_ok, c + 1, tick)
            for k in range(K):
                ins = nc.vector.bn_aggr(mv[:, k, :], stats[:, k, :])
            ins.then_inc(mv_ok, 1)
            wait(dve, mv_ok, c + 1)
            nc.vector.tensor_scalar(var[:], mv[:, :, 1], EPS, None, ALU.add).then_inc(var_ok, 1)

        def norm(c):
            wait(dve, rstd_ok, c + 1)
            wait(dve, xt_mm, c)
            for k in range(K):
                ins = nc.vector.tensor_scalar(xn[:, k, :], xld[:, k, :], mv[:, k, 0:1], rstd[:, k:k + 1],
                                              ALU.subtract, ALU.mult)
            ins.then_inc(xn_ok, 1)

        def oper_lo(c, i):
            wait(dve, xT_ok, c + 1)
            wait(dve, xhi_ok, c + 1)
            wait(dve, u_mm, NP * (c - 1))
            nc.vector.tensor_tensor(xlo[i][:], misc[:], xhi[i][:].bitcast(F32), ALU.subtract).then_inc(xlo_ok, 1)

        def route(c, part):
            done = lambda k: wait(dve, rt, R_STEPS * c + k)
            tt = nc.vector.tensor_tensor
            s8 = sc[:].rearrange("p k (g e) -> p (k g) e", g=NG)
            m8 = masked[:].rearrange("p k (g e) -> p (k g) e", g=NG)
            by_group = lambda t: t[:].rearrange("p k g -> p (k g)").unsqueeze(2).to_broadcast([P, K * NG, EPG])
            if part == 0:
                wait(dve, sig_ok, c + 1)
                tt(sc[:], sig[:], gbias[:].unsqueeze(1).to_broadcast([P, K, E]), ALU.add).then_inc(rt, 1)
            if part == 1:
                done(1)
                tt(top_a[:], s8[:, :, 0:4], s8[:, :, 4:8], ALU.max).then_inc(rt, 1)
                tt(low_a[:], s8[:, :, 0:4], s8[:, :, 4:8], ALU.min).then_inc(rt, 1)
            if part == 2:
                done(3)
                tt(mid_b[:], top_a[:, :, 0:2], top_a[:, :, 2:4], ALU.min).then_inc(rt, 1)
                tt(top_b[:], top_a[:, :, 0:2], top_a[:, :, 2:4], ALU.max).then_inc(rt, 1)
                tt(low_b[:], low_a[:, :, 0:2], low_a[:, :, 2:4], ALU.max).then_inc(rt, 1)
            if part == 3:
                done(6)
                tt(low_b[:], low_b[:], mid_b[:], ALU.max).then_inc(rt, 1)
                tt(mid_c[:], top_b[:, :, 0:1], top_b[:, :, 1:2], ALU.min).then_inc(rt, 1)
                tt(top_c[:], top_b[:, :, 0:1], top_b[:, :, 1:2], ALU.max).then_inc(rt, 1)
            if part == 4:
                done(9)
                tt(low_c[:], low_b[:, :, 0:1], low_b[:, :, 1:2], ALU.max).then_inc(rt, 1)
                done(10)
                tt(low_c[:], low_c[:], mid_c[:], ALU.max).then_inc(rt, 1)
                done(11)
                tt(gs[:].rearrange("p k g -> p (k g)"), top_c[:, :, 0], low_c[:, :, 0], ALU.add).then_inc(rt, 1)
            if part == 5:
                done(12)
                other = gs[:].unsqueeze(2).to_broadcast([P, K, NG, NG])
                own = gs[:].unsqueeze(3).to_broadcast([P, K, NG, NG])
                tt(eq[:], other, own, ALU.is_equal).then_inc(rt, 1)
                tt(gt[:], other, own, ALU.is_gt).then_inc(rt, 1)
            if part == 6:
                done(14)
                tt(eq[:], eq[:], tri[:].unsqueeze(1).to_broadcast([P, K, NG, NG]), ALU.mult).then_inc(rt, 1)
            if part == 7:
                done(15)
                tt(gt[:], gt[:], eq[:], ALU.add).then_inc(rt, 1)
            if part == 8:
                done(16)
                nc.vector.tensor_reduce(rank[:], gt[:], AXX, ALU.add).then_inc(rt, 1)
                done(17)
                nc.vector.tensor_scalar(gm[:], rank[:], float(TG), None, ALU.is_lt).then_inc(rt, 1)
            if part == 9:
                done(18)
                nc.vector.tensor_scalar(pen[:], gm[:], -LOW, LOW, ALU.mult, ALU.add).then_inc(rt, 1)
                tt(m8, s8, by_group(gm), ALU.mult).then_inc(rt, 1)
            if part == 10:
                done(20)
                tt(m8, m8, by_group(pen), ALU.add).then_inc(rt, 1)
            if part == 11:
                wait_tick(nc, rt, R_STEPS * c + 21, tick)
                for k in range(K):
                    ins = nc.vector.max(best[:, k, :], masked[:, k, :])
                ins.then_inc(rt, 1)
            if part == 12:
                wait_tick(nc, rt, R_STEPS * c + 22, tick)
                for k in range(K):
                    ins = nc.vector.match_replace(out=rep[:, k, :], in_to_replace=best[:, k, :],
                                                  in_values=masked[:, k, :], imm_value=LOWER)
                ins.then_inc(rt, 1)
            if part == 13:
                done(23)
                tt(wsel[:], rep[:], masked[:], ALU.not_equal).then_inc(rt, 1)
            if part == 14:
                done(24)
                tt(wsel[:], wsel[:], sig[:], ALU.mult).then_inc(rt, 1)
            if part == 15:
                done(25)
                nc.vector.tensor_reduce(wsum[:], wsel[:], AXX, ALU.add).then_inc(rt, 1)
                done(26)
                nc.vector.tensor_scalar(wsum[:], wsum[:], 1e-20, 1.0 / ROUTE_SCALE, ALU.add, ALU.mult).then_inc(rd_ok, 1)
            if part == 16:
                wait(dve, rd_ok, 2 * c + 1)
                nc.vector.reciprocal(wsum[:], wsum[:]).then_inc(rd_ok, 1)
                wait(dve, rd_ok, 2 * c + 2)
                wait(dve, wt_mm, c)
                tt(wnorm[:], wsel[:], wsum[:].unsqueeze(2).to_broadcast([P, K, E]), ALU.mult).then_inc(w_ok, 1)

        def act_up(n, k):
            wait(dve, s_ok, n + 1)
            wait(dve, u_mm, n + 1)
            wait(dve, h_ok, n + 1 - RS)
            nc.vector.tensor_tensor(a_buf[k % RS][:], s_buf[k % RS][:], u_bank[k % 3][:], ALU.mult).then_inc(a_ok, 1)

        def hid_lo(n, k):
            wait(dve, hh_ok, n + 1)
            nc.vector.tensor_tensor(hlo[k % RH][:], h_buf[k % RS][:], hhi[k % RH][:].bitcast(F32),
                                    ALU.subtract).then_inc(hl_ok, 1)

        def finish(c, c2, i):
            wait(dve, yt_mm, c + 1)
            wait(dve, x2_in, 16 * (c + 1))
            wait(dve, o_st[i], 16 * c2)
            nc.vector.scalar_tensor_tensor(out=osb[i][:].rearrange("p k d -> p (k d)"), in0=misc[:],
                                           scalar=tg_f[:, 0:1], in1=x2c[:].rearrange("p k d -> p (k d)"),
                                           op0=ALU.mult, op1=ALU.add).then_inc(out_ok, 1)

        dve.wait_ge(g_in, 32)
        norm_stats(0)
        norm(0)
        def split_down(k):
            wait(dve, cv_hi, 2 * CONV + k + 1)
            src, hi, lo = down_slice(k)
            nc.vector.tensor_tensor(lo, src, hi.bitcast(F32), ALU.subtract).then_inc(dl_ok, 1)

        for k in GU_DVE:
            wait(dve, cv_hi, k + 1)
            src, hi, lo = gu_slice(k)
            nc.vector.tensor_tensor(lo, src, hi.bitcast(F32), ALU.subtract).then_inc(gl_dve, 1)
            if k == GU_DVE[0]:
                oper_lo(0, 0)
        dve.wait_ge(c_ok, 4)
        for part in range(ROUTE_PARTS):
            route(0, part)
        gate_up_free(dve)

        def body(g, last):
            for j in range(2):
                c = 2 * g + j
                first = isinstance(c, int) and c == 0
                more = not (last and j == 1)
                for q in range(NP):
                    n, k = NP * c + q, NP * j + q
                    act_up(n, k)
                    if not (first and q < 2):
                        hid_lo(n - 2, k - 2)
                    if first and q in (1, 5, 7):
                        split_down((1, 5, 7).index(q))
                    if q == F_OUT and not first:
                        finish(c - 1, g - 1 + j, 1 - j)
                    if more:
                        if q == P_STAT:
                            norm_stats(c + 1)
                        if q == P_NORM:
                            norm(c + 1)
                        if q == P_OPER:
                            oper_lo(c + 1, 1 - j)
                        if P_ROUTE <= q < P_ROUTE + ROUTE_PARTS:
                            route(c + 1, q - P_ROUTE)

        body(0, False)
        with dve.Fori(1, LOOPS - 1) as g:
            body(g, False)
        body(LOOPS - 1, True)
        for q in range(2):
            hid_lo(NP * NCH - 2 + q, 2 * NP - 2 + q)
        finish(NCH - 1, LOOPS - 1, 1)

    @block.tensor
    def _(pe):
        def turn_x(c):
            wait(pe, xn_ok, c + 1)
            for k in range(K):
                ins = nc.tensor.transpose(misc[:, k * P:(k + 1) * P], xn[:, k, :], ident[:])
            ins.then_inc(xt_mm, 1)

        def logits(c):
            wait(pe, xT_ok, c + 1)
            wait(pe, xlo_ok, c + 1)
            for k in range(K):
                ins = nc.tensor.matmul(misc[:, k * E:(k + 1) * E], xT[:, k * P:(k + 1) * P], gwT[:],
                                       start=True, stop=True)
            ins.then_inc(lg_mm, 1)

        def before_turn_w(c):
            wait(pe, out_ok, c - 1)
            wait(pe, sig_ok, c + 1)
            wait(pe, w_ok, c + 1)

        def turn_w(c):
            for k in range(K):
                ins = nc.tensor.transpose(misc[0:E, k * P:(k + 1) * P], wnorm[:, k, :], ident[:])
            ins.then_inc(wt_mm, 1)

        def turn_y(c):
            wait(pe, y_ev, c + 1)
            for k in range(K):
                ins = nc.tensor.transpose(misc[:, k * P:(k + 1) * P], ysb[:, k * P:(k + 1) * P], ident[:])
            ins.then_inc(yt_mm, 1)

        def three(bank, w, mh, ml, first, last):
            nc.tensor.matmul(bank, w[0], mh, start=first, stop=False)
            nc.tensor.matmul(bank, w[1], mh, start=False, stop=False)
            return nc.tensor.matmul(bank, w[0], ml, start=False, stop=last)

        def gate_up(n, k, q, i):
            pick = lambda w: [t[:, 2 * q:2 * q + 2, :].rearrange("p e f -> p (e f)") for t in w]
            wait(pe, s_ok, n - 1)
            three(g_bank[k % 2][:], pick(wg), xhi[i][:], xlo[i][:], True, True).then_inc(g_mm, 1)
            wait(pe, a_ok, n - 2)
            three(u_bank[k % 3][:], pick(wu), xhi[i][:], xlo[i][:], True, True).then_inc(u_mm, 1)

        def down(n, k, q, i):
            wait(pe, hl_ok, n + 1)
            three(y_bank[i][:], [w[:, q, :] for w in wd], hhi[k % RH][:], hlo[k % RH][:],
                  q == 0, q == NP - 1).then_inc(dn_mm, 1)

        pe.wait_ge(g_in, 32)
        nc.tensor.transpose(misc[:, 0:E], gw_in[:], ident[0:E, 0:E]).then_inc(gw_mm, 1)
        pe.wait_ge(gw_ev, 1)
        turn_x(0)
        logits(0)
        gate_up_free(pe)

        def body(g, last):
            for j in range(2):
                c = 2 * g + j
                first = isinstance(c, int) and c == 0
                more = not (last and j == 1)
                for q in range(NP):
                    n, k = NP * c + q, NP * j + q
                    if first and q == EARLY:
                        before_turn_w(0)
                        turn_w(0)
                    if q == P_WT and more:
                        before_turn_w(c + 1)
                    gate_up(n, k, q, j)
                    if q >= LAG:
                        if q == LAG:
                            wait(pe, y_ev, c - 1)
                        if first and (q - LAG) % (NP // CONV) == 0:
                            pe.wait_ge(dl_ok, (q - LAG) // (NP // CONV) + 1)
                        down(n - LAG, k - LAG, q - LAG, j)
                    elif not first:
                        down(n - LAG, k - LAG, q - LAG + NP, 1 - j)
                    if q == F_TURN and not first:
                        if more:
                            wait(pe, sig_ok, c + 2)
                        turn_y(c - 1)
                    if more:
                        if q == P_TURN:
                            wait(pe, wt_ev, c + 1)
                            turn_x(c + 1)
                        if q == P_LOGIT:
                            logits(c + 1)
                        if q == P_WT:
                            turn_w(c + 1)

        body(0, False)
        with pe.Fori(1, LOOPS - 1) as g:
            body(g, False)
        body(LOOPS - 1, True)
        for q in range(LAG):
            down(NP * NCH - LAG + q, 2 * NP - LAG + q, NP - LAG + q, 1)
        turn_y(NCH - 1)


_INS = ['x', 'ctx_1024', 'g_xattn', 'g_ffn', 'L0_xattn_Wqkv', 'L0_xattn_bqkv', 'L0_xattn_Wqkv_aux',
        'L0_xattn_bqkv_aux', 'L0_xattn_Wo', 'L0_xattn_bo', 'L0_xattn_g', 'L0_ffn_gate_w', 'L0_ffn_gate_bias',
        'L0_ffn_We_gate', 'L0_ffn_We_up', 'L0_ffn_We_down', 'L0_ffn_Ws_gate', 'L0_ffn_Ws_up', 'L0_ffn_Ws_down']
_OUTS = [((32, 128, 128), 'float32')]


def kernel(**inputs):
    import numpy as _np
    import concourse.bacc as _bacc
    from concourse import mybir as _mybir
    from concourse.bass_utils import run_bass_kernel_spmd as _run

    nc = _bacc.Bacc("TRN2", target_bir_lowering=False, num_devices=1)
    arrays, args = {}, []
    for name in _INS:
        a = _np.ascontiguousarray(inputs[name])
        arrays[f"in_{name}_dram"] = a
        args.append(nc.dram_tensor(f"in_{name}_dram", a.shape, _mybir.dt.from_np(a.dtype), kind="ExternalInput").ap())
    for i, (shape, dtype) in enumerate(_OUTS):
        dt = _mybir.dt.from_np(_np.dtype(dtype))
        args.append(nc.dram_tensor(f"out_{i}_dram", shape, dt, kind="ExternalOutput").ap())
    build(nc, *args)
    r = _run(nc, [arrays], core_ids=[0])
    got = tuple(r.results[0][f"out_{i}_dram"] for i in range(len(_OUTS)))
    return got[0]
```
